# Optimizing a Trainium2 kernel written in Bass

```python
import numpy as np
import jax
import jax.numpy as jnp

def _softmax(x, axis=-1):
    return jax.nn.softmax(x, axis=axis)

def _gelu(x):
    return jax.nn.gelu(x, approximate=True)

def _silu(x):
    return jax.nn.silu(x)

def _sigmoid(x):
    return jax.nn.sigmoid(x)

def _layernorm(x, axis=-1, eps=1e-05):
    m = jnp.mean(x, axis=axis, keepdims=True)
    v = jnp.var(x, axis=axis, keepdims=True)
    return (x - m) / jnp.sqrt(v + eps)

def _scatter_add(tgt, idx, src, axis=0):
    return tgt.at[idx].add(src)

def _segment_sum(src, seg, n):
    return jax.ops.segment_sum(src, seg, n)
kernel_name = 'mk_flamingo_gated_d4_seqx_r8_62987a'

def setup_inputs(seed: int=0):
    np.random.seed(seed)
    _w = jnp.asarray

    def _rec_inputs():
        import jax
        import jax.numpy as jnp
        _rk = jax.random.key(seed)
        x = -0.000125 + 0.9999 * jax.random.normal(jax.random.fold_in(_rk, 1), (32, 64, 256), jnp.float32)
        _lenS = 64 - jax.random.randint(jax.random.fold_in(_rk, 7), (32,), 0, max(1, 64 // 4) + 1, jnp.int32)
        _lenS2 = 64 - jax.random.randint(jax.random.fold_in(_rk, 8), (32,), 0, max(1, 64 // 4) + 1, jnp.int32)
        _ctx_2048P = jax.random.normal(jax.random.fold_in(_rk, 11), (32, 16, 256), jnp.float32)
        _ctx_2048c = jax.random.dirichlet(jax.random.fold_in(_rk, 511), 0.3 * jnp.ones((16,), jnp.float32), (32, 64))
        _ctx_2048t = jnp.einsum('bsk,bkd->bsd', _ctx_2048c, _ctx_2048P)
        _ctx_2048t = _ctx_2048t * jax.lax.rsqrt(jnp.mean(jnp.square(_ctx_2048t)) + 1e-12) * 0.953939
        ctx_2048 = -1.52775e-05 + 0.999936 * (_ctx_2048t + 0.3 * jax.random.normal(jax.random.fold_in(_rk, 611), (32, 64, 256), jnp.float32))
        _g = jax.random.normal(jax.random.fold_in(_rk, 9001), (2, 4), jnp.float32)
        _g = jnp.sign(_g) * jnp.maximum(jnp.abs(_g), 1.0) + (_g == 0) * 1.0
        g_xattn = _g[0]
        g_ffn = _g[1]
        return (x, ctx_2048, g_xattn, g_ffn)
    x, ctx_2048, g_xattn, g_ffn = _rec_inputs()

    def _L0_xattn_setup():
        import jax, jax.numpy as jnp
        import numpy as np
        EPS = 1e-06
        NUM_HEADS = 16

        def _feature_map(x):
            return jnp.where(x > 0, x + 1.0, jnp.exp(x))
        key = jax.random.key(seed)
        ks = jax.random.split(key, 7)
        B, L, S, D = (4, 512, 512, 256)
        sc = 1.0 / np.sqrt(D)
        return {'query': jax.random.normal(ks[0], (B, L, D), jnp.float32), 'kv': jax.random.normal(ks[1], (B, S, D), jnp.float32), 'Wq': jax.random.normal(ks[2], (D, D), jnp.float32) * sc, 'Wg': jax.random.normal(ks[3], (D, D), jnp.float32) * sc, 'bg': jnp.ones((D,), jnp.float32), 'Wkv': jax.random.normal(ks[4], (2 * D, D), jnp.float32) * sc, 'Wo': jax.random.normal(ks[5], (D, D), jnp.float32) * sc}
    _L0_xattn_all = _L0_xattn_setup()
    _L0_xattn_in = {k: v for k, v in _L0_xattn_all.items() if k in ('Wq', 'Wg', 'bg', 'Wkv', 'Wo')}
    del _L0_xattn_all

    def _L0_ffn_setup():
        import jax, jax.numpy as jnp
        import numpy as np
        B, S, D = (4, 256, 256)
        E, K, M = (8, 2, 128)
        key = jax.random.key(seed)
        k0, k1, k2, k3, k4 = jax.random.split(key, 5)
        d_scale = D ** (-0.5)
        m_scale = M ** (-0.5)
        return {'x': jax.random.normal(k0, (B, S, D), jnp.float32), 'w_gate': jax.random.normal(k1, (D, E), jnp.float32) * d_scale, 'wi_0': jax.random.normal(k2, (E, D, M), jnp.float32) * d_scale, 'wi_1': jax.random.normal(k3, (E, D, M), jnp.float32) * d_scale, 'wo': jax.random.normal(k4, (E, M, D), jnp.float32) * m_scale}
    _L0_ffn_all = _L0_ffn_setup()
    _L0_ffn_in = {k: v for k, v in _L0_ffn_all.items() if k in ('w_gate', 'wi_0', 'wi_1', 'wo')}
    del _L0_ffn_all

    def _L1_xattn_setup():
        import math
        import jax, jax.numpy as jnp
        import numpy as np
        N_HEADS = 8
        CHANNELS = 64
        K_CH = CHANNELS // N_HEADS
        THETA = 10000.0

        def _rope_freqs(length, dim):
            inv_freq = 1.0 / THETA ** (jnp.arange(0, dim, 2, dtype=jnp.float32) / dim)
            f = jnp.arange(length, dtype=jnp.float32)[:, None] * inv_freq[None, :]
            return jnp.concatenate([f, f], axis=-1)

        def _apply_rotary(pos, t):
            half = t.shape[-1] // 2
            rot = jnp.concatenate([-t[..., half:], t[..., :half]], axis=-1)
            return t * jnp.cos(pos) + rot * jnp.sin(pos)

        def _proj(inp, W, b):
            return jnp.einsum('oc,bct->bot', W, inp) + b[None, :, None]
        key = jax.random.key(seed)
        ks = jax.random.split(key, 10)
        B, C, T = (4, CHANNELS, 256)
        bound = math.sqrt(6.0 / (C + C))

        def w(k):
            return jax.random.uniform(k, (C, C), jnp.float32, -bound, bound)
        return {'x': jax.random.normal(ks[0], (B, C, T), jnp.float32), 'c': jax.random.normal(ks[1], (B, C, T), jnp.float32), 'Wq': w(ks[2]), 'bq': jnp.zeros((C,), jnp.float32), 'Wk': w(ks[3]), 'bk': jnp.zeros((C,), jnp.float32), 'Wv': w(ks[4]), 'bv': jnp.zeros((C,), jnp.float32), 'Wo': w(ks[5]), 'bo': jnp.zeros((C,), jnp.float32)}
    _L1_xattn_all = _L1_xattn_setup()
    _L1_xattn_in = {k: v for k, v in _L1_xattn_all.items() if k in ('Wq', 'bq', 'Wk', 'bk', 'Wv', 'bv', 'Wo', 'bo')}
    del _L1_xattn_all

    def _L1_ffn_setup():
        import jax, jax.numpy as jnp
        import numpy as np
        B, S, D, M, E, K = (4, 256, 256, 512, 8, 2)

        def _routed_moe(x, gate_w, w0, w1, wo):
            T = x.shape[0]
            logits = jnp.einsum('td,de->te', x, gate_w)
            top_logits, top_idx = jax.lax.top_k(logits, K)
            top_w = jax.nn.softmax(top_logits, axis=-1)
            cw = jnp.zeros((T, E), dtype=x.dtype).at[jnp.arange(T)[:, None], top_idx].add(top_w)
            out = jnp.zeros_like(x)
            for e in range(E):
                h = jax.nn.silu(x @ w0[e]) * (x @ w1[e])
                out = out + cw[:, e:e + 1] * (h @ wo[e])
            return out
        key = jax.random.key(seed)
        ks = jax.random.split(key, 5)
        inputs = jax.random.normal(ks[0], (B, S, D), dtype=jnp.float32)
        gate_w = jax.random.normal(ks[1], (D, E), dtype=jnp.float32) * D ** (-0.5)
        w0 = jax.random.normal(ks[2], (E, D, M), dtype=jnp.float32) * D ** (-0.5)
        w1 = jax.random.normal(ks[3], (E, D, M), dtype=jnp.float32) * D ** (-0.5)
        wo = jax.random.normal(ks[4], (E, M, D), dtype=jnp.float32) * M ** (-0.5)
        decoder_segment_ids = jax.random.randint(jax.random.fold_in(key, 1), (B, S), 0, 2).astype(jnp.int32)
        decoder_positions = jnp.tile(jnp.arange(S, dtype=jnp.int32)[None, :], (B, 1))
        return {'inputs': inputs, 'gate_w': gate_w, 'w0': w0, 'w1': w1, 'wo': wo, 'decoder_segment_ids': decoder_segment_ids, 'decoder_positions': decoder_positions}
    _L1_ffn_all = _L1_ffn_setup()
    _L1_ffn_in = {k: v for k, v in _L1_ffn_all.items() if k in ('gate_w', 'w0', 'w1', 'wo', 'decoder_segment_ids', 'decoder_positions')}
    del _L1_ffn_all

    def _L2_xattn_setup():
        import jax, jax.numpy as jnp
        import numpy as np
        from jax import lax
        LN_EPS = 1e-05
        key = jax.random.key(seed)
        ks = jax.random.split(key, 8)
        B, S, T, D = (4, 128, 256, 256)
        scale = 0.02
        return {'Z': jax.random.normal(ks[0], (B, S, D), dtype=jnp.float32), 'kv': jax.random.normal(ks[1], (B, T, D), dtype=jnp.float32), 'decay': jnp.float32(0.9), 'W_in': jax.random.normal(ks[2], (D, D), dtype=jnp.float32) * scale, 'b_in': jnp.zeros((D,), dtype=jnp.float32), 'W_out': jax.random.normal(ks[3], (D, D), dtype=jnp.float32) * scale, 'b_out': jnp.zeros((D,), dtype=jnp.float32), 'gamma': jnp.ones((D,), dtype=jnp.float32), 'beta': jnp.zeros((D,), dtype=jnp.float32)}
    _L2_xattn_all = _L2_xattn_setup()
    _L2_xattn_in = {k: v for k, v in _L2_xattn_all.items() if k in ('decay', 'W_in', 'b_in', 'W_out', 'b_out', 'gamma', 'beta')}
    del _L2_xattn_all

    def _L2_ffn_setup():
        import jax, jax.numpy as jnp
        import numpy as np
        TOP_K = 2
        key = jax.random.key(seed)
        ks = jax.random.split(key, 5)
        B, T, D, E, H = (4, 256, 256, 8, 176)
        s = 1.0 / np.sqrt(D)
        sh = 1.0 / np.sqrt(H)
        return {'x': jax.random.normal(ks[0], (B, T, D), dtype=jnp.float32), 'Wg': jax.random.normal(ks[1], (E, D), dtype=jnp.float32) * s, 'W1': jax.random.normal(ks[2], (E, H, D), dtype=jnp.float32) * s, 'W2': jax.random.normal(ks[3], (E, H, D), dtype=jnp.float32) * s, 'W3': jax.random.normal(ks[4], (E, D, H), dtype=jnp.float32) * sh}
    _L2_ffn_all = _L2_ffn_setup()
    _L2_ffn_in = {k: v for k, v in _L2_ffn_all.items() if k in ('Wg', 'W1', 'W2', 'W3')}
    del _L2_ffn_all

    def _L3_xattn_setup():
        import jax, jax.numpy as jnp
        import numpy as np
        import math
        EMBED = 256
        HEADS = 32
        GROUPS = 8
        GROUP_HEADS = HEADS // GROUPS
        HEAD_DIM = EMBED // HEADS
        B, S = (4, 128)
        key = jax.random.key(seed)
        ks = jax.random.split(key, 8)
        sc = 0.02
        return {'q': jax.random.normal(ks[0], (B, S, EMBED), jnp.float32), 'k': jax.random.normal(ks[1], (B, S, EMBED), jnp.float32), 'v': jax.random.normal(ks[2], (B, S, EMBED), jnp.float32), 'Wq': jax.random.normal(ks[3], (EMBED, EMBED), jnp.float32) * sc, 'Wk': jax.random.normal(ks[4], (GROUPS * HEAD_DIM, EMBED), jnp.float32) * sc, 'Wv': jax.random.normal(ks[5], (GROUPS * HEAD_DIM, EMBED), jnp.float32) * sc, 'Wfc': jax.random.normal(ks[6], (EMBED, EMBED), jnp.float32) * sc, 'bfc': jnp.zeros((EMBED,), jnp.float32)}
    _L3_xattn_all = _L3_xattn_setup()
    _L3_xattn_in = {k: v for k, v in _L3_xattn_all.items() if k in ('Wq', 'Wk', 'Wv', 'Wfc', 'bfc')}
    del _L3_xattn_all

    def _L3_ffn_setup():
        import jax, jax.numpy as jnp
        import numpy as np
        D_HIDDEN = 256
        D_EXPERT = 176
        N_EXPERTS = 8
        TOP_K = 2
        N_SHARED = 2
        D_SHARED = D_EXPERT * N_SHARED
        key = jax.random.key(seed)
        ks = jax.random.split(key, 8)
        s = 0.02
        return {'x': jax.random.normal(ks[0], (4, 256, D_HIDDEN), dtype=jnp.float32), 'W_g': jax.random.normal(ks[1], (D_HIDDEN, N_EXPERTS), dtype=jnp.float32) * s, 'Wg': jax.random.normal(ks[2], (N_EXPERTS, D_HIDDEN, D_EXPERT), dtype=jnp.float32) * s, 'Wu': jax.random.normal(ks[3], (N_EXPERTS, D_HIDDEN, D_EXPERT), dtype=jnp.float32) * s, 'Wd': jax.random.normal(ks[4], (N_EXPERTS, D_EXPERT, D_HIDDEN), dtype=jnp.float32) * s, 'Ws_gate': jax.random.normal(ks[5], (D_HIDDEN, D_SHARED), dtype=jnp.float32) * s, 'Ws_up': jax.random.normal(ks[6], (D_HIDDEN, D_SHARED), dtype=jnp.float32) * s, 'Ws_down': jax.random.normal(ks[7], (D_SHARED, D_HIDDEN), dtype=jnp.float32) * s}
    _L3_ffn_all = _L3_ffn_setup()
    _L3_ffn_in = {k: v for k, v in _L3_ffn_all.items() if k in ('W_g', 'Wg', 'Wu', 'Wd', 'Ws_gate', 'Ws_up', 'Ws_down')}
    del _L3_ffn_all
    return {'x': x, 'ctx_2048': ctx_2048, 'g_xattn': g_xattn, 'g_ffn': g_ffn, 'L0_xattn_Wq': _L0_xattn_in['Wq'], 'L0_xattn_Wg': _L0_xattn_in['Wg'], 'L0_xattn_bg': _L0_xattn_in['bg'], 'L0_xattn_Wkv': _L0_xattn_in['Wkv'], 'L0_xattn_Wo': _L0_xattn_in['Wo'], 'L0_ffn_w_gate': _L0_ffn_in['w_gate'], 'L0_ffn_wi_0': _L0_ffn_in['wi_0'], 'L0_ffn_wi_1': _L0_ffn_in['wi_1'], 'L0_ffn_wo': _L0_ffn_in['wo'], 'L1_xattn_Wq': _L1_xattn_in['Wq'], 'L1_xattn_bq': _L1_xattn_in['bq'], 'L1_xattn_Wk': _L1_xattn_in['Wk'], 'L1_xattn_bk': _L1_xattn_in['bk'], 'L1_xattn_Wv': _L1_xattn_in['Wv'], 'L1_xattn_bv': _L1_xattn_in['bv'], 'L1_xattn_Wo': _L1_xattn_in['Wo'], 'L1_xattn_bo': _L1_xattn_in['bo'], 'L1_ffn_gate_w': _L1_ffn_in['gate_w'], 'L1_ffn_w0': _L1_ffn_in['w0'], 'L1_ffn_w1': _L1_ffn_in['w1'], 'L1_ffn_wo': _L1_ffn_in['wo'], 'L1_ffn_decoder_segment_ids': _L1_ffn_in['decoder_segment_ids'], 'L1_ffn_decoder_positions': _L1_ffn_in['decoder_positions'], 'L2_xattn_decay': _L2_xattn_in['decay'], 'L2_xattn_W_in': _L2_xattn_in['W_in'], 'L2_xattn_b_in': _L2_xattn_in['b_in'], 'L2_xattn_W_out': _L2_xattn_in['W_out'], 'L2_xattn_b_out': _L2_xattn_in['b_out'], 'L2_xattn_gamma': _L2_xattn_in['gamma'], 'L2_xattn_beta': _L2_xattn_in['beta'], 'L2_ffn_Wg': _L2_ffn_in['Wg'], 'L2_ffn_W1': _L2_ffn_in['W1'], 'L2_ffn_W2': _L2_ffn_in['W2'], 'L2_ffn_W3': _L2_ffn_in['W3'], 'L3_xattn_Wq': _L3_xattn_in['Wq'], 'L3_xattn_Wk': _L3_xattn_in['Wk'], 'L3_xattn_Wv': _L3_xattn_in['Wv'], 'L3_xattn_Wfc': _L3_xattn_in['Wfc'], 'L3_xattn_bfc': _L3_xattn_in['bfc'], 'L3_ffn_W_g': _L3_ffn_in['W_g'], 'L3_ffn_Wg': _L3_ffn_in['Wg'], 'L3_ffn_Wu': _L3_ffn_in['Wu'], 'L3_ffn_Wd': _L3_ffn_in['Wd'], 'L3_ffn_Ws_gate': _L3_ffn_in['Ws_gate'], 'L3_ffn_Ws_up': _L3_ffn_in['Ws_up'], 'L3_ffn_Ws_down': _L3_ffn_in['Ws_down']}

def reference(x, ctx_2048, g_xattn, g_ffn, L0_xattn_Wq, L0_xattn_Wg, L0_xattn_bg, L0_xattn_Wkv, L0_xattn_Wo, L0_ffn_w_gate, L0_ffn_wi_0, L0_ffn_wi_1, L0_ffn_wo, L1_xattn_Wq, L1_xattn_bq, L1_xattn_Wk, L1_xattn_bk, L1_xattn_Wv, L1_xattn_bv, L1_xattn_Wo, L1_xattn_bo, L1_ffn_gate_w, L1_ffn_w0, L1_ffn_w1, L1_ffn_wo, L1_ffn_decoder_segment_ids, L1_ffn_decoder_positions, L2_xattn_decay, L2_xattn_W_in, L2_xattn_b_in, L2_xattn_W_out, L2_xattn_b_out, L2_xattn_gamma, L2_xattn_beta, L2_ffn_Wg, L2_ffn_W1, L2_ffn_W2, L2_ffn_W3, L3_xattn_Wq, L3_xattn_Wk, L3_xattn_Wv, L3_xattn_Wfc, L3_xattn_bfc, L3_ffn_W_g, L3_ffn_Wg, L3_ffn_Wu, L3_ffn_Wd, L3_ffn_Ws_gate, L3_ffn_Ws_up, L3_ffn_Ws_down):
    import jax
    import jax.numpy as jnp

    def _L0_xattn_ref(query, kv, Wq, Wg, bg, Wkv, Wo):
        import jax, jax.numpy as jnp
        import numpy as np
        EPS = 1e-06
        NUM_HEADS = 16

        def _feature_map(x):
            return jnp.where(x > 0, x + 1.0, jnp.exp(x))
        B, L, D = query.shape
        S = kv.shape[1]
        H = NUM_HEADS
        hd = D // H
        q = query @ Wq.T
        gate = jax.nn.sigmoid(query @ Wg.T + bg)
        kvp = kv @ Wkv.T
        k, v = jnp.split(kvp, 2, axis=-1)
        q = _feature_map(q.reshape(B, L, H, hd).transpose(0, 2, 1, 3))
        k = _feature_map(k.reshape(B, S, H, hd).transpose(0, 2, 1, 3))
        v = v.reshape(B, S, H, hd).transpose(0, 2, 1, 3)
        kv_summary = jnp.einsum('bhsd,bhse->bhde', k, v)
        k_sum = k.sum(axis=-2)
        z = 1.0 / (jnp.einsum('bhld,bhd->bhl', q, k_sum)[..., None] + EPS)
        attn = jnp.einsum('bhld,bhde->bhle', q, kv_summary) * z
        attn = attn.transpose(0, 2, 1, 3).reshape(B, L, D)
        out = attn * gate @ Wo.T
        return out

    def _L0_ffn_ref(x, w_gate, wi_0, wi_1, wo):
        import jax, jax.numpy as jnp
        import numpy as np
        B, S, D = (4, 256, 256)
        E, K, M = (8, 2, 128)
        b, s, d = x.shape
        e = w_gate.shape[1]
        xf = x.reshape(-1, d)
        logits = jnp.dot(xf, w_gate)
        top_logits, top_idx = jax.lax.top_k(logits, K)
        weights = jax.nn.softmax(top_logits, axis=-1)
        flat_idx = top_idx.reshape(-1)
        sort_order = jnp.argsort(flat_idx)
        token_ids = sort_order // K
        sorted_x = jnp.take(xf, token_ids, axis=0)
        group_sizes = jnp.bincount(flat_idx, length=E).astype(jnp.int32)
        h0 = jax.lax.ragged_dot(sorted_x, wi_0, group_sizes)
        h1 = jax.lax.ragged_dot(sorted_x, wi_1, group_sizes)
        inter = jax.nn.silu(h0) * h1
        out_sorted = jax.lax.ragged_dot(inter, wo, group_sizes)
        unsort = jnp.argsort(sort_order)
        out = jnp.take(out_sorted, unsort, axis=0).reshape(-1, K, d)
        out = jnp.einsum('tkd,tk->td', out, weights)
        return out.reshape(b, s, d)

    def _L1_xattn_ref(x, c, Wq, bq, Wk, bk, Wv, bv, Wo, bo):
        import math
        import jax, jax.numpy as jnp
        import numpy as np
        N_HEADS = 8
        CHANNELS = 64
        K_CH = CHANNELS // N_HEADS
        THETA = 10000.0

        def _rope_freqs(length, dim):
            inv_freq = 1.0 / THETA ** (jnp.arange(0, dim, 2, dtype=jnp.float32) / dim)
            f = jnp.arange(length, dtype=jnp.float32)[:, None] * inv_freq[None, :]
            return jnp.concatenate([f, f], axis=-1)

        def _apply_rotary(pos, t):
            half = t.shape[-1] // 2
            rot = jnp.concatenate([-t[..., half:], t[..., :half]], axis=-1)
            return t * jnp.cos(pos) + rot * jnp.sin(pos)

        def _proj(inp, W, b):
            return jnp.einsum('oc,bct->bot', W, inp) + b[None, :, None]
        b, _, t_t = x.shape
        t_s = c.shape[2]
        q_emb = _rope_freqs(t_t, K_CH)
        k_emb = _rope_freqs(t_s, K_CH)

        def split_heads(t):
            return t.reshape(b, N_HEADS, K_CH, t.shape[2]).transpose(0, 1, 3, 2)
        q = split_heads(_proj(x, Wq, bq))
        k = split_heads(_proj(c, Wk, bk))
        v = split_heads(_proj(c, Wv, bv))
        q = _apply_rotary(q_emb, q)
        k = _apply_rotary(k_emb, k)
        scores = jnp.einsum('bhtc,bhsc->bhts', q, k) / math.sqrt(K_CH)
        p_attn = jax.nn.softmax(scores, axis=-1)
        out = jnp.einsum('bhts,bhsc->bhtc', p_attn, v)
        out = out.transpose(0, 1, 3, 2).reshape(b, N_HEADS * K_CH, t_t)
        return _proj(out, Wo, bo)

    def _L1_ffn_ref(inputs, gate_w, w0, w1, wo, decoder_segment_ids, decoder_positions):
        import jax, jax.numpy as jnp
        import numpy as np
        B, S, D, M, E, K = (4, 256, 256, 512, 8, 2)

        def _routed_moe(x, gate_w, w0, w1, wo):
            T = x.shape[0]
            logits = jnp.einsum('td,de->te', x, gate_w)
            top_logits, top_idx = jax.lax.top_k(logits, K)
            top_w = jax.nn.softmax(top_logits, axis=-1)
            cw = jnp.zeros((T, E), dtype=x.dtype).at[jnp.arange(T)[:, None], top_idx].add(top_w)
            out = jnp.zeros_like(x)
            for e in range(E):
                h = jax.nn.silu(x @ w0[e]) * (x @ w1[e])
                out = out + cw[:, e:e + 1] * (h @ wo[e])
            return out
        b, s, d = inputs.shape
        x = inputs.reshape(b * s, d)
        out = _routed_moe(x, gate_w, w0, w1, wo)
        return out.reshape(b, s, d)

    def _L2_xattn_ref(Z, kv, decay, W_in, b_in, W_out, b_out, gamma, beta):
        import jax, jax.numpy as jnp
        import numpy as np
        from jax import lax
        LN_EPS = 1e-05
        B, T, D = kv.shape
        K = jax.nn.sigmoid(decay)
        x = jnp.einsum('btd,ed->bte', kv, W_in) + b_in

        def scan_fn(s, xt):
            s = K * s + xt
            return (s, s)
        s0 = jnp.zeros((B, D), dtype=kv.dtype)
        _, states = lax.scan(scan_fn, s0, jnp.swapaxes(x, 0, 1))
        states = jnp.swapaxes(states, 0, 1)
        proj = jnp.einsum('btd,ed->bte', states, W_out) + b_out
        summary = jnp.mean(proj, axis=1, keepdims=True)
        y = Z + summary
        mu = jnp.mean(y, axis=-1, keepdims=True)
        var = jnp.mean((y - mu) ** 2, axis=-1, keepdims=True)
        return (y - mu) / jnp.sqrt(var + LN_EPS) * gamma + beta

    def _L2_ffn_ref(x, Wg, W1, W2, W3):
        import jax, jax.numpy as jnp
        import numpy as np
        TOP_K = 2
        E = Wg.shape[0]
        scores = jnp.einsum('btd,ed->bte', x, Wg)
        topk_s, topk_i = jax.lax.top_k(scores, TOP_K)
        probs = jax.nn.softmax(topk_s, axis=-1)
        onehot = (topk_i[..., None] == jnp.arange(E)).astype(x.dtype)
        w = jnp.einsum('btk,btke->bte', probs, onehot)
        y = jnp.zeros_like(x)
        for e in range(E):
            h = jax.nn.silu(jnp.einsum('btd,hd->bth', x, W1[e])) * jnp.einsum('btd,hd->bth', x, W2[e])
            y = y + w[..., e:e + 1] * jnp.einsum('bth,dh->btd', h, W3[e])
        return y

    def _L3_xattn_ref(q, k, v, Wq, Wk, Wv, Wfc, bfc):
        import jax, jax.numpy as jnp
        import numpy as np
        import math
        EMBED = 256
        HEADS = 32
        GROUPS = 8
        GROUP_HEADS = HEADS // GROUPS
        HEAD_DIM = EMBED // HEADS
        B, S = (4, 128)
        N, S_, _ = q.shape
        qh = (q @ Wq.T).reshape(N, S_, HEADS, HEAD_DIM).transpose(0, 2, 1, 3)
        kh = (k @ Wk.T).reshape(N, S_, GROUPS, HEAD_DIM).transpose(0, 2, 1, 3)
        vh = (v @ Wv.T).reshape(N, S_, GROUPS, HEAD_DIM).transpose(0, 2, 1, 3)
        kh = jnp.repeat(kh, GROUP_HEADS, axis=1)
        vh = jnp.repeat(vh, GROUP_HEADS, axis=1)
        score = jnp.einsum('bhqd,bhkd->bhqk', qh, kh) / math.sqrt(HEAD_DIM)
        attn = jax.nn.softmax(score, axis=-1)
        out = jnp.einsum('bhqk,bhkd->bhqd', attn, vh)
        out = out.transpose(0, 2, 1, 3).reshape(N, S_, EMBED)
        return out @ Wfc.T + bfc

    def _L3_ffn_ref(x, W_g, Wg, Wu, Wd, Ws_gate, Ws_up, Ws_down):
        import jax, jax.numpy as jnp
        import numpy as np
        D_HIDDEN = 256
        D_EXPERT = 176
        N_EXPERTS = 8
        TOP_K = 2
        N_SHARED = 2
        D_SHARED = D_EXPERT * N_SHARED
        B, S, D = x.shape
        shared = jax.nn.silu(x @ Ws_gate) * (x @ Ws_up) @ Ws_down
        xf = x.reshape(-1, D)
        T = xf.shape[0]
        scores = jax.nn.softmax(xf @ W_g, axis=-1)
        topk_scores, topk_idx = jax.lax.top_k(scores, TOP_K)
        combine = jnp.zeros((T, N_EXPERTS), dtype=xf.dtype).at[jnp.arange(T)[:, None], topk_idx].add(topk_scores)
        gate = jax.nn.silu(jnp.einsum('td,edh->teh', xf, Wg))
        up = jnp.einsum('td,edh->teh', xf, Wu)
        out = jnp.einsum('teh,ehd->ted', gate * up, Wd)
        routed = jnp.einsum('ted,te->td', out, combine)
        return routed.reshape(B, S, D) + shared
    x = x + jnp.tanh(g_xattn[0]) * _L0_xattn_ref(_layernorm(x, axis=-1), ctx_2048, L0_xattn_Wq, L0_xattn_Wg, L0_xattn_bg, L0_xattn_Wkv, L0_xattn_Wo)
    x = x + jnp.tanh(g_ffn[0]) * _L0_ffn_ref(_layernorm(x, axis=-1), L0_ffn_w_gate, L0_ffn_wi_0, L0_ffn_wi_1, L0_ffn_wo)
    x = x + jnp.tanh(g_xattn[1]) * _L1_xattn_ref(_layernorm(x, axis=-1), ctx_2048, L1_xattn_Wq, L1_xattn_bq, L1_xattn_Wk, L1_xattn_bk, L1_xattn_Wv, L1_xattn_bv, L1_xattn_Wo, L1_xattn_bo)
    x = x + jnp.tanh(g_ffn[1]) * _L1_ffn_ref(_layernorm(x, axis=-1), L1_ffn_gate_w, L1_ffn_w0, L1_ffn_w1, L1_ffn_wo, L1_ffn_decoder_segment_ids, L1_ffn_decoder_positions)
    x = x + jnp.tanh(g_xattn[2]) * _L2_xattn_ref(_layernorm(x, axis=-1), ctx_2048, L2_xattn_decay, L2_xattn_W_in, L2_xattn_b_in, L2_xattn_W_out, L2_xattn_b_out, L2_xattn_gamma, L2_xattn_beta)
    x = x + jnp.tanh(g_ffn[2]) * _L2_ffn_ref(_layernorm(x, axis=-1), L2_ffn_Wg, L2_ffn_W1, L2_ffn_W2, L2_ffn_W3)
    x = x + jnp.tanh(g_xattn[3]) * _L3_xattn_ref(_layernorm(x, axis=-1), ctx_2048, ctx_2048, L3_xattn_Wq, L3_xattn_Wk, L3_xattn_Wv, L3_xattn_Wfc, L3_xattn_bfc)
    x = x + jnp.tanh(g_ffn[3]) * _L3_ffn_ref(_layernorm(x, axis=-1), L3_ffn_W_g, L3_ffn_Wg, L3_ffn_Wu, L3_ffn_Wd, L3_ffn_Ws_gate, L3_ffn_Ws_up, L3_ffn_Ws_down)
    return x

_drawn_inputs = setup_inputs


def setup_inputs(seed=0):
    import zlib

    import numpy as np

    out = dict(_drawn_inputs(seed))
    spreads = {'L0_xattn_bg': (1.0, 0.2),
     'L1_xattn_bq': (0.0, 0.1),
     'L1_xattn_bk': (0.0, 0.1),
     'L1_xattn_bv': (0.0, 0.503),
     'L1_xattn_bo': (0.0, 0.55),
     'L2_xattn_b_in': (0.0, 0.1),
     'L2_xattn_b_out': (0.0, 0.1),
     'L2_xattn_gamma': (1.0, 0.2),
     'L2_xattn_beta': (0.0, 0.1),
     'L3_xattn_bfc': (0.0, 0.1)}
    factors = {'L3_xattn_Wq': 8.0,
     'L3_xattn_Wk': 8.0,
     'L3_ffn_W_g': 8.0,
     'L3_ffn_Wg': 8.0,
     'L3_ffn_Wu': 8.0,
     'L3_ffn_Wd': 8.0,
     'L3_ffn_Ws_gate': 8.0,
     'L3_ffn_Ws_up': 8.0,
     'L3_ffn_Ws_down': 8.0}
    for name, (base, spread) in spreads.items():
        noise = np.random.default_rng([zlib.crc32(name.encode()), seed]).standard_normal(out[name].shape)
        drawn = base * np.exp(spread * noise) if base else spread * noise
        out[name] = jnp.asarray(drawn.astype(out[name].dtype))
    for name, factor in factors.items():
        out[name] = (out[name] * factor).astype(out[name].dtype)
    return out
```

```python
from contextlib import ExitStack

import numpy as np

import concourse.bass as bass
from concourse import mybir

F32 = mybir.dt.float32
I32 = mybir.dt.int32
U32 = mybir.dt.uint32
ALU = mybir.AluOpType
ACT = mybir.ActivationFunctionType
AX = mybir.AxisListType

P = 128
B, L, D = 32, 64, 256
T = B * L // P
KC = D // P
E = 8
TOP = 2
LAYERS = 4
START = 2
SLOT_TILES = TOP * B * L // P + E - 1
WORK = 14700
LN_EPS = 1e-5
LIN_EPS = 1e-6
HIDDEN = (128, 512, 176, 176)
SHARED = 352
HD0 = 16
H1, C1 = 8, 8
H3, G3, C3 = 32, 8, 8
TW = L

COLS = (("g", 8), ("bg", 2), ("bq", 2), ("bk", 2), ("bo", 1), ("mask1", 8), ("mask3", 16),
        ("decay", 1), ("b_in", 2), ("batch_of", 2))
ROWS = (("bv", 128), ("bfc", D), ("gamma", D), ("beta", D), ("b_out", D), ("iota8", E), ("iota_k", T),
        ("iota_j", SLOT_TILES), ("cos_q", D), ("sin_q", D), ("cos_k", D), ("sin_k", D))


class Signal:

    def __init__(self, sem, step, start):
        self.sem, self.step, self.start = sem, step, start
        self.base, self.raised = start * step, 0

    def up(self, times=1):
        self.raised += times
        return self.sem

    def at(self, n):
        return n * self.step + self.base

    def end_stage(self):
        self.base += self.raised * self.step
        self.raised = 0


def chunks(m):
    return [(c, min(P, m - c * P)) for c in range((m + P - 1) // P)]


def build(nc, d, out):
    ctx = ExitStack()
    with ctx:
        def sb(name, shape, dt=F32):
            return ctx.enter_context(nc.sbuf_tensor(name, shape, dt))

        signals = []

        def sig(name, step=1, start=START):
            signals.append(Signal(ctx.enter_context(nc.semaphore(name)), step, start))
            return signals[-1]

        def end_stage():
            for s in signals:
                s.end_stage()

        slot_x = nc.dram_tensor("slot_x", (SLOT_TILES * P, D), F32, kind="Internal").ap()
        slot_y = nc.dram_tensor("slot_y", (SLOT_TILES * P, D), F32, kind="Internal").ap()

        x = sb("x", [P, T, D])
        xn2 = sb("xn2", [P, T, D])
        ffn_w = sb("ffn_w", [P, E * (KC * 2 * 512 + 4 * D)])
        att_w = sb("att_w", [P, 2560])
        ident = sb("ident", [P, P])
        before = sb("before", [P, P])
        ones = sb("ones", [P, P])
        cols = sb("cols", [P, sum(n for _, n in COLS)])
        rows = sb("rows", [P, sum(n for _, n in ROWS)])
        router_w = sb("router_w", [P, 4, KC, E])
        gain = sb("gain", [P, 8])
        half = sb("half", [P, 1])
        table_call = sb("table_call", [P, 1])
        logits = sb("logits", [P, T, E])
        slots = sb("slots", [P, TOP, T], U32)
        weight = sb("weight", [P, TOP, T])
        tile_expert = sb("tile_expert", [1, SLOT_TILES], I32)
        work = sb("work", [P, WORK])
        ps = ctx.enter_context(nc.psum_tensor("ps", [P, 8, 512], F32))
        used = [0]

        def carve(*shape):
            n = int(np.prod(shape))
            v = work[:, used[0]:used[0] + n]
            used[0] += n
            assert used[0] <= WORK, used
            if len(shape) == 1:
                return v
            names = "abcdef"[:len(shape)]
            return v.rearrange(f"p ({' '.join(names)}) -> p {' '.join(names)}",
                               **dict(zip(names[1:], shape[1:])))

        def place(table):
            at, o = {}, 0
            for name, n in table:
                at[name] = (o, n)
                o += n
            return at

        col_at, row_at = place(COLS), place(ROWS)

        def col(name, j=0, n=1):
            return cols[:, col_at[name][0] + j:col_at[name][0] + j + n]

        def row(name):
            o, n = row_at[name]
            return rows[:, o:o + n]

        consts_in, ffn_w_in, att_w_in = sig("consts_in", 16), sig("ffn_w_in", 16), sig("att_w_in", 16)
        zeros_out, out_done, ctx_in = sig("zeros_out", 16), sig("out_done", 16), sig("ctx_in", 16)
        slot_in = [sig(f"slot_in{u}", 16) for u in range(2)]
        slot_out = [sig(f"slot_out{u}", 16) for u in range(2)]
        y_in, scattered = sig("y_in", 16, 0), sig("scattered", 16, 0)
        ready, index_ready, held_pool, held_dve = (sig(n) for n in ("ready", "index_ready", "held_pool", "held_dve"))
        half_added, added, tile_done = (sig(n) for n in ("half_added", "added", "tile_done"))
        saved = sig("saved")
        ln_stats, ln_mean, ln_var, ln_rstd, ln_done = (
            sig(n) for n in ("ln_stats", "ln_mean", "ln_var", "ln_rstd", "ln_done"))
        turned, turned_out = sig("turned"), sig("turned_out")
        projected, projected_kv, proj_min, proj_exp, proj_out = (
            sig(n) for n in ("projected", "projected_kv", "proj_min", "proj_exp", "proj_out"))
        gate_step, masked, scored, shifted, probs = (
            sig(n) for n in ("gate_step", "masked", "scored", "shifted", "probs"))
        probs_turned, probs_out, attended, norm_step, attn_ready, out_made = (
            sig(n) for n in ("probs_turned", "probs_out", "attended", "norm_step", "attn_ready", "out_made"))
        logits_made, step = sig("logits_made"), sig("step")
        xT_made, xT_ready, up_made, silu_ready = (sig(n) for n in ("xT_made", "xT_ready", "up_made", "silu_ready"))
        h_ready, hT_made, hT_ready, y_made, y_ready = (
            sig(n) for n in ("h_ready", "hT_made", "hT_ready", "y_made", "y_ready"))

        with nc.Block() as block:
            @block.sync
            def _(sp):
                for s in signals:
                    if s.start:
                        sp.sem_inc(s.sem, s.start * s.step)

        consts = ((ident, "ident"), (before, "before"), (cols, "cols"), (rows, "rows"),
                  (router_w, "router_w"), (x, "x"))
        zeros = work[:, 0:SLOT_TILES // 3 * D]
        with nc.Block() as block:
            @block.sync
            def _(sp):
                for buf, name in consts:
                    sp.dma_start(buf[:], d[name]).then_inc(consts_in.up(), 16)
                sp.wait_ge(ready.sem, ready.at(1))
                n = SLOT_TILES // 3
                for j in range(3):
                    sp.dma_start(slot_x[j * n * P:(j + 1) * n * P].rearrange("(t p) d -> p t d", p=P),
                                 zeros.rearrange("p (t d) -> p t d", d=D)).then_inc(zeros_out.up(), 16)
                sp.wait_ge(zeros_out.sem, zeros_out.at(3))

            @block.vector
            def _(dve):
                nc.vector.memset(zeros, 0.0).then_inc(ready.up(), 1)
                nc.vector.memset(ones[:], 1.0)
                nc.vector.memset(half[:], -0.5)

            @block.scalar
            def _(act):
                act.wait_ge(consts_in.sem, consts_in.at(len(consts)))
                nc.scalar.activation(gain[:], col("g", 0, 8), ACT.Tanh)
        end_stage()

        def gather_rows(pool, i, index, y_buf):
            pool.wait_ge(tile_done.sem, tile_done.at(i))
            nc.gpsimd.tensor_copy(index, slots[:, :, bass.ds(i, 1)].rearrange("p a b -> p (a b)")
                                  ).then_inc(index_ready.up(T), 1)
            pool.wait_ge(index_ready.sem, index_ready.at(i + 1))
            pool.sem_inc(held_pool.up(T), 1)
            for a in range(TOP):
                nc.gpsimd.indirect_dma_start(
                    y_buf[:, a, :], None, slot_y,
                    bass.IndirectOffsetOnAxis(ap=index[:, a:a + 1], axis=0)).then_inc(y_in.up(T), 16)

        def add_rows(dve, i, y_buf):
            dve.wait_ge(y_in.sem, y_in.at(TOP * i + TOP))
            nc.vector.scalar_tensor_tensor(
                out=x[:, i, :], in0=y_buf[:, 0, :], scalar=weight[:, 0, bass.ds(i, 1)], in1=x[:, i, :],
                op0=ALU.mult, op1=ALU.add).then_inc(half_added.up(T), 1)
            dve.wait_ge(half_added.sem, half_added.at(i + 1))
            nc.vector.scalar_tensor_tensor(
                out=x[:, i, :], in0=y_buf[:, 1, :], scalar=weight[:, 1, bass.ds(i, 1)], in1=x[:, i, :],
                op0=ALU.mult, op1=ALU.add).then_inc(added.up(T), 1)
            dve.wait_ge(added.sem, added.at(i + 1))

        def norm_dve(dve, n, src, dst, stats):
            dve.sem_inc(held_dve.up(T), 1)
            nc.vector.bn_stats(stats["bn"], src).then_inc(ln_stats.up(T), 1)
            dve.wait_ge(ln_stats.sem, ln_stats.at(n + 1))
            dve.sem_inc(held_dve.up(T), 1)
            nc.vector.bn_aggr(stats["mv"], stats["bn"]).then_inc(ln_mean.up(T), 1)
            dve.wait_ge(ln_mean.sem, ln_mean.at(n + 1))
            nc.vector.tensor_scalar(stats["var"], stats["mv"][:, 1:2], LN_EPS, None, ALU.add).then_inc(ln_var.up(T), 1)
            dve.wait_ge(ln_rstd.sem, ln_rstd.at(n + 1))
            nc.vector.tensor_scalar(dst, src, stats["mv"][:, 0:1], stats["rstd"], ALU.subtract, ALU.mult
                                    ).then_inc(ln_done.up(T), 1)

        def norm_pool(pool, n, stats):
            pool.wait_ge(ln_var.sem, ln_var.at(n + 1))
            nc.gpsimd.tensor_tensor(stats["rstd"], stats["var"], half[:], ALU.pow).then_inc(ln_rstd.up(T), 1)

        def carve_stats():
            return {"bn": carve(6), "mv": carve(2), "var": carve(1), "rstd": carve(1)}

        def turn(pe, src, bank, at=0):
            for k in range(KC):
                mm = nc.tensor.transpose(ps[:, bank, at + k * P:at + (k + 1) * P], src[:, k * P:(k + 1) * P], ident[:])
            return mm

        def save_norm(pool, i, n_norm, xn):
            pool.wait_ge(ln_done.sem, ln_done.at(n_norm + 1))
            nc.gpsimd.tensor_copy(xn2[:, i, :], xn).then_inc(saved.up(T), 1)

        def router_pe(pe, layer, n_norm, n_turn, xn, xT):
            pe.wait_ge(ln_done.sem, ln_done.at(n_norm + 1))
            turn(pe, xn, 0).then_inc(turned.up(T), 1)
            pe.wait_ge(turned_out.sem, turned_out.at(n_turn + 1))
            for k in range(KC):
                mm = nc.tensor.matmul(ps[:, 1, 0:E], xT[:, k, :], router_w[:, layer, k, :],
                                      start=(k == 0), stop=(k == KC - 1))
            mm.then_inc(logits_made.up(T), 1)

        def turned_act(act, n_turn, xT, n=2 * P, at=0):
            act.wait_ge(turned.sem, turned.at(n_turn + 1))
            nc.scalar.copy(xT.rearrange("p k t -> p (k t)"), ps[:, 0, at:at + n]).then_inc(turned_out.up(T), 1)

        def router_dve(dve, i):
            dve.wait_ge(logits_made.sem, logits_made.at(i + 1))
            nc.vector.tensor_copy(logits[:, i, :], ps[:, 1, 0:E]).then_inc(tile_done.up(T), 1)

        def load_ffn(sp, layer):
            m = HIDDEN[layer]
            sp.dma_start(up_view(layer), d[f"up{layer}"].rearrange("e (k p) m -> p e k m", p=P)
                         ).then_inc(ffn_w_in.up(), 16)
            for e in range(E):
                for c, n in chunks(m):
                    sp.dma_start(down_view(layer)[0:n, e, c, :], d[f"down{layer}"][e, c * P:c * P + n, :]
                                 ).then_inc(ffn_w_in.up(), 16)

        def up_view(layer):
            m = HIDDEN[layer]
            return ffn_w[:, 0:E * KC * 2 * m].rearrange("p (e k m) -> p e k m", e=E, k=KC)

        def down_view(layer):
            m = HIDDEN[layer]
            n, o = len(chunks(m)), E * KC * 2 * m
            return ffn_w[:, o:o + E * n * D].rearrange("p (e c n) -> p e c n", e=E, c=n)

        def n_ffn_dmas(layer):
            return 1 + E * len(chunks(HIDDEN[layer]))

        def attention0():
            used[0] = 0
            layer = 0
            wq = att_w[:, 0:2 * D].rearrange("p (k n) -> p k n", k=KC)
            wg = att_w[:, 2 * D:4 * D].rearrange("p (k n) -> p k n", k=KC)
            wkv = att_w[:, 4 * D:8 * D].rearrange("p (k n) -> p k n", k=KC)
            wo = att_w[:, 8 * D:10 * D].rearrange("p (k n) -> p k n", k=KC)
            stats = carve_stats()
            head_mask = carve(2 * P)
            neg_bg = carve(2)
            xn, xT = carve(D), carve(KC, P)
            cT = carve(KC, P)
            low_q, qT = carve(KC, P), carve(KC, P)
            low_k, k_map = carve(D), carve(D)
            v_ones = carve(KC, 2, P)
            e_gate = carve(KC, P)
            state = carve(2, KC, 2 * P)
            divisor, attn = carve(KC, P), carve(KC, P)
            bank_x, bank_q, bank_g, bank_k, bank_n, bank_d = 0, 2, 3, 4, 5, 3

            with nc.Block() as block:
                @block.sync
                def _(sp):
                    for buf, name in ((wq, "wq0"), (wg, "wg0"), (wkv, "wkv0"), (wo, "wo0")):
                        sp.dma_start(buf, d[name].rearrange("(k p) n -> p k n", p=P)).then_inc(att_w_in.up(), 16)
                    sp.dma_start(head_mask, d["mask0"]).then_inc(att_w_in.up(), 16)
                    load_ffn(sp, layer)
                    with sp.Fori(0, T) as i:
                        sp.wait_ge(projected.sem, projected.at(i))
                        sp.dma_start(cT, d["ctxT"][i]).then_inc(ctx_in.up(T), 16)

                @block.gpsimd
                def _(pool):
                    with pool.Fori(0, T) as i:
                        norm_pool(pool, 2 * i, stats)
                        norm_pool(pool, 2 * i + 1, stats)
                        save_norm(pool, i, 2 * i + 1, xn)

                @block.tensor
                def _(pe):
                    pe.wait_ge(att_w_in.sem, att_w_in.at(5))
                    pe.wait_ge(ready.sem, ready.at(2))
                    with pe.Fori(0, T) as i:
                        pe.wait_ge(ln_done.sem, ln_done.at(2 * i + 1))
                        turn(pe, xn, 0).then_inc(turned.up(T), 1)
                        pe.wait_ge(ctx_in.sem, ctx_in.at(i + 1))
                        pe.wait_ge(turned_out.sem, turned_out.at(2 * i + 1))
                        for w, bank in ((wq, bank_q), (wg, bank_g)):
                            for g in range(KC):
                                for k in range(KC):
                                    mm = nc.tensor.matmul(ps[:, bank, g * P:(g + 1) * P], w[:, k, g * P:(g + 1) * P],
                                                          xT[:, k, :], start=(k == 0), stop=(k == KC - 1))
                        for k in range(KC):
                            mm = nc.tensor.matmul(ps[:, bank_k, :], cT[:, k, :], wkv[:, k, :],
                                                  start=(k == 0), stop=(k == KC - 1))
                        mm.then_inc(projected.up(T), 1)
                        pe.wait_ge(proj_out.sem, proj_out.at(3 * i + 3))
                        for b in range(2):
                            for g in range(KC):
                                mm = nc.tensor.matmul(
                                    ps[:, 6 + b, g * 2 * P:(g + 1) * 2 * P], k_map[b * L:(b + 1) * L, g * P:(g + 1) * P],
                                    v_ones[b * L:(b + 1) * L, g, :, :].rearrange("p a n -> p (a n)"),
                                    start=True, stop=True)
                        mm.then_inc(scored.up(T), 1)
                        pe.wait_ge(masked.sem, masked.at(i + 1))
                        for b in range(2):
                            for g in range(KC):
                                for a, bank in ((0, bank_n), (1, bank_q)):
                                    mm = nc.tensor.matmul(
                                        ps[:, bank, g * P + b * L:g * P + (b + 1) * L],
                                        state[:, b, g, a * P:(a + 1) * P], qT[:, g, b * L:(b + 1) * L],
                                        start=True, stop=True)
                        mm.then_inc(attended.up(T), 1)
                        pe.wait_ge(attn_ready.sem, attn_ready.at(i + 1))
                        for g in range(KC):
                            mm = nc.tensor.matmul(ps[:, bank_k, 0:D], attn[:, g, :], wo[:, g, :],
                                                  start=(g == 0), stop=(g == KC - 1))
                        mm.then_inc(out_made.up(T), 1)
                        router_pe(pe, layer, 2 * i + 1, 2 * i + 1, xn, xT)

                @block.scalar
                def _(act):
                    nc.scalar.activation(table_call[:], half[:], ACT.Exp)
                    act.wait_ge(ready.sem, ready.at(2))
                    with act.Fori(0, T) as i:
                        act.wait_ge(turned.sem, turned.at(2 * i + 1))
                        nc.scalar.copy(xT.rearrange("p k t -> p (k t)"), ps[:, 0, 0:2 * P]).then_inc(turned_out.up(T), 1)
                        act.wait_ge(projected.sem, projected.at(i + 1))
                        for g in range(KC):
                            nc.scalar.activation(e_gate[:, g, :], ps[:, bank_g, g * P:(g + 1) * P], ACT.Exp,
                                                 bias=neg_bg[:, g:g + 1], scale=-1.0).then_inc(gate_step.up(T), 1)
                        act.wait_ge(proj_min.sem, proj_min.at(2 * i + 1))
                        nc.scalar.activation(low_q, low_q, ACT.Exp).then_inc(proj_exp.up(T), 1)
                        act.wait_ge(proj_min.sem, proj_min.at(2 * i + 2))
                        nc.scalar.activation(low_k, low_k, ACT.Exp).then_inc(proj_exp.up(T), 1)
                        turned_act(act, 2 * i + 1, xT)

                @block.vector
                def _(dve):
                    nc.vector.tensor_scalar(neg_bg, col("bg", 0, 2), -1.0, None, ALU.mult).then_inc(ready.up(), 1)
                    nc.vector.memset(v_ones[:, :, 1, :], 1.0).then_inc(ready.up(), 1)
                    dve.wait_ge(att_w_in.sem, att_w_in.at(5))
                    with dve.Fori(0, T) as i:
                        dve.wait_ge(saved.sem, saved.at(i))
                        norm_dve(dve, 2 * i, x[:, i, :], xn, stats)
                        dve.wait_ge(projected.sem, projected.at(i + 1))
                        dve.wait_ge(gate_step.sem, gate_step.at(2 * i + 2))
                        nc.vector.tensor_scalar(low_q.rearrange("p k t -> p (k t)"), ps[:, bank_q, 0:2 * P], 0.0, None,
                                                ALU.min).then_inc(proj_min.up(T), 1)
                        nc.vector.tensor_scalar(low_k, ps[:, bank_k, 0:D], 0.0, None, ALU.min).then_inc(proj_min.up(T), 1)
                        nc.vector.tensor_copy(v_ones[:, :, 0, :], ps[:, bank_k, D:2 * D].rearrange("p (g n) -> p g n", g=KC)
                                              ).then_inc(proj_out.up(T), 1)
                        dve.wait_ge(proj_exp.sem, proj_exp.at(2 * i + 1))
                        nc.vector.scalar_tensor_tensor(
                            out=qT.rearrange("p k t -> p (k t)"), in0=ps[:, bank_q, 0:2 * P], scalar=1.0,
                            in1=low_q.rearrange("p k t -> p (k t)"), op0=ALU.add, op1=ALU.max).then_inc(proj_out.up(T), 1)
                        dve.wait_ge(proj_exp.sem, proj_exp.at(2 * i + 2))
                        nc.vector.scalar_tensor_tensor(
                            out=k_map, in0=ps[:, bank_k, 0:D], scalar=1.0, in1=low_k,
                            op0=ALU.add, op1=ALU.max).then_inc(proj_out.up(T), 1)
                        dve.wait_ge(scored.sem, scored.at(i + 1))
                        nc.vector.tensor_tensor(
                            state.rearrange("p b g n -> p (b g) n"), ps[:, 6:8, :].rearrange("p b (g n) -> p (b g) n", g=KC),
                            head_mask.unsqueeze(1).to_broadcast([P, 2 * KC, 2 * P]), ALU.mult).then_inc(masked.up(T), 1)
                        dve.wait_ge(attended.sem, attended.at(i + 1))
                        nc.vector.tensor_scalar(e_gate, e_gate, 1.0, None, ALU.add).then_inc(norm_step.up(T), 1)
                        dve.wait_ge(norm_step.sem, norm_step.at(3 * i + 1))
                        nc.vector.scalar_tensor_tensor(
                            out=divisor.rearrange("p k t -> p (k t)"), in0=ps[:, bank_q, 0:2 * P], scalar=LIN_EPS,
                            in1=e_gate.rearrange("p k t -> p (k t)"), op0=ALU.add, op1=ALU.mult).then_inc(norm_step.up(T), 1)
                        dve.wait_ge(norm_step.sem, norm_step.at(3 * i + 2))
                        nc.vector.reciprocal(divisor, divisor).then_inc(norm_step.up(T), 1)
                        dve.wait_ge(norm_step.sem, norm_step.at(3 * i + 3))
                        nc.vector.tensor_tensor(attn.rearrange("p k t -> p (k t)"), ps[:, bank_n, 0:2 * P],
                                                divisor.rearrange("p k t -> p (k t)"), ALU.mult).then_inc(attn_ready.up(T), 1)
                        dve.wait_ge(out_made.sem, out_made.at(i + 1))
                        nc.vector.scalar_tensor_tensor(
                            out=x[:, i, :], in0=ps[:, bank_k, 0:D], scalar=gain[:, layer:layer + 1], in1=x[:, i, :],
                            op0=ALU.mult, op1=ALU.add).then_inc(added.up(T), 1)
                        dve.wait_ge(added.sem, added.at(i + 1))
                        norm_dve(dve, 2 * i + 1, x[:, i, :], xn, stats)
                        router_dve(dve, i)
            end_stage()

        def attention1():
            used[0] = 0
            layer = 1
            names = ("wq1", "wq1_turned", "wk1", "wk1_turned", "wv1")
            wq, wq_turned, wk, wk_turned, wv = (att_w[:, j * P:(j + 1) * P] for j in range(5))
            wo = att_w[0:C1 * H1, 5 * P:7 * P].rearrange("p (b n) -> p b n", b=2)
            stats = carve_stats()
            index, y_buf = carve(TOP).bitcast(U32), carve(TOP, D)
            xn, xT, ctx_t = carve(D), carve(KC, P), carve(D)
            rope_a, rope_b = carve(2, D), carve(2, D)
            qk = carve(2, D)
            k_head = carve(H1, D)
            v = carve(2, 2 * H1 * C1)
            v_flat = carve(2 * H1 * P + H1 * C1)
            v_ones = v_flat[:, 0:2 * H1 * P].rearrange("p (s h n) -> p s h n", s=2, h=H1)
            neg_max = carve(H1)
            p = carve(H1, 2, P)
            pT = carve(H1, 2, D)
            inv = carve(D)
            attn = carve(2, D)
            tmp = carve(D)

            with nc.Block() as block:
                @block.sync
                def _(sp):
                    for j, name in enumerate(names):
                        sp.dma_start(att_w[:, j * P:(j + 1) * P], d[name]).then_inc(att_w_in.up(), 16)
                    sp.dma_start(wo, d["wo1"]).then_inc(att_w_in.up(), 16)
                    load_ffn(sp, layer)
                    with sp.Fori(0, T) as i:
                        sp.wait_ge(projected.sem, projected.at(i))
                        sp.dma_start(ctx_t, d["ctx"][i]).then_inc(ctx_in.up(T), 16)

                @block.gpsimd
                def _(pool):
                    with pool.Fori(0, T) as i:
                        gather_rows(pool, i, index, y_buf)
                        norm_pool(pool, 2 * i, stats)
                        norm_pool(pool, 2 * i + 1, stats)
                        save_norm(pool, i, 2 * i + 1, xn)

                @block.tensor
                def _(pe):
                    pe.wait_ge(att_w_in.sem, att_w_in.at(6))
                    with pe.Fori(0, T) as i:
                        pe.wait_ge(ctx_in.sem, ctx_in.at(i + 1))
                        pe.wait_ge(ln_done.sem, ln_done.at(2 * i + 1))
                        for w, src, bank, o in ((wq, xn, 0, 0), (wq_turned, xn, 0, D), (wk, ctx_t, 1, 0), (wk_turned, ctx_t, 1, D)):
                            nc.tensor.matmul(ps[:, bank, o:o + D], w, src, start=True, stop=True)
                        for c in range(2):
                            mm = nc.tensor.matmul(ps[:, 2, c * P:(c + 1) * P], ctx_t[:, c * P:(c + 1) * P], wv,
                                                  start=True, stop=True)
                        mm.then_inc(projected.up(T), 1)
                        for b in range(2):
                            rows_b = slice(b * 64, (b + 1) * 64)
                            for c in range(2):
                                n = 4 * i + 2 * b + c
                                pe.wait_ge(masked.sem, masked.at(i + 1))
                                pe.wait_ge(attn_ready.sem, attn_ready.at(2 * i + b))
                                for q4 in range(4):
                                    mm = nc.tensor.matmul(
                                        ps[:, 4 + q4, :], qk[rows_b, 0, c * P:(c + 1) * P],
                                        k_head[rows_b, 2 * q4:2 * q4 + 2, :].rearrange("p h s -> p (h s)"),
                                        start=True, stop=True)
                                mm.then_inc(scored.up(T), 1)
                                pe.wait_ge(probs.sem, probs.at(n + 1))
                                pe.wait_ge(probs_out.sem, probs_out.at(2 * n))
                                for h in range(H1):
                                    for sc in range(2):
                                        j = 2 * h + sc
                                        mm = nc.tensor.transpose(ps[:, j // 4, (j % 4) * P:(j % 4 + 1) * P],
                                                                 p[:, h, sc, :], ident[:])
                                mm.then_inc(probs_turned.up(T), 1)
                            pe.wait_ge(probs_out.sem, probs_out.at(8 * i + 4 * b + 4))
                            for h in range(H1):
                                for sc in range(2):
                                    mm = nc.tensor.matmul(ps[:, 4, 0:D], v_ones[:, sc, h, :], pT[:, h, sc, :],
                                                          start=(h == 0 and sc == 0), stop=(h == H1 - 1 and sc == 1))
                            mm.then_inc(attended.up(T), 1)
                        pe.wait_ge(attn_ready.sem, attn_ready.at(2 * i + 2))
                        for b in range(2):
                            mm = nc.tensor.matmul(ps[:, 5, 0:D], wo[:, b, :], attn[0:64, b, :],
                                                  start=(b == 0), stop=(b == 1))
                        mm.then_inc(out_made.up(T), 1)
                        router_pe(pe, layer, 2 * i + 1, i, xn, xT)

                @block.scalar
                def _(act):
                    nc.scalar.activation(table_call[:], half[:], ACT.Exp)
                    with act.Fori(0, T) as i:
                        for b in range(2):
                            for c in range(2):
                                n = 4 * i + 2 * b + c
                                act.wait_ge(shifted.sem, shifted.at(n + 1))
                                for h in range(H1):
                                    last = nc.scalar.activation(
                                        p[:, h, :, :].rearrange("p s n -> p (s n)"),
                                        ps[:, 4 + h // 2, (h % 2) * D:(h % 2 + 1) * D], ACT.Exp,
                                        bias=neg_max[:, h:h + 1])
                                last.then_inc(probs.up(T), 1)
                                act.wait_ge(probs_turned.sem, probs_turned.at(n + 1))
                                act.wait_ge(attended.sem, attended.at(2 * i + b))
                                nc.scalar.copy(pT[:, 4:8, :, c * P:(c + 1) * P].rearrange("p h s n -> p (h s) n"),
                                               ps[:, 2:4, :].rearrange("p a (j n) -> p (a j) n", n=P)
                                               ).then_inc(probs_out.up(T), 1)
                        turned_act(act, i, xT)

                @block.vector
                def _(dve):
                    nc.vector.memset(v_flat, 0.0).then_inc(ready.up(), 1)
                    dve.wait_ge(ready.sem, ready.at(1))
                    for h in range(H1):
                        o = H1 * C1 + h * C1
                        last = nc.vector.memset(v_ones[:, :, h, o:o + C1], 1.0)
                    last.then_inc(ready.up(), 1)
                    dve.wait_ge(ready.sem, ready.at(2))
                    with dve.Fori(0, T) as i:
                        dve.wait_ge(saved.sem, saved.at(i))
                        add_rows(dve, i, y_buf)
                        norm_dve(dve, 2 * i, x[:, i, :], xn, stats)
                        dve.wait_ge(projected.sem, projected.at(i + 1))
                        for j, (b_name, c_name, s_name) in enumerate((("bq", "cos_q", "sin_q"), ("bk", "cos_k", "sin_k"))):
                            nc.vector.scalar_tensor_tensor(out=rope_a[:, j], in0=ps[:, j, 0:D], scalar=col(b_name, 0),
                                                           in1=row(c_name), op0=ALU.add, op1=ALU.mult)
                            nc.vector.scalar_tensor_tensor(out=rope_b[:, j], in0=ps[:, j, D:2 * D], scalar=col(b_name, 1),
                                                           in1=row(s_name), op0=ALU.add, op1=ALU.mult
                                                           ).then_inc(norm_step.up(T), 1)
                        nc.vector.tensor_tensor(v, ps[:, 2, 0:2 * P].rearrange("p (s n) -> p s n", s=2),
                                                row("bv").unsqueeze(1).to_broadcast([P, 2, P]), ALU.add
                                                ).then_inc(proj_out.up(T), 1)
                        dve.wait_ge(norm_step.sem, norm_step.at(4 * i + 2))
                        nc.vector.tensor_tensor(qk, rope_a, rope_b, ALU.add).then_inc(proj_out.up(T), 1)
                        dve.wait_ge(proj_out.sem, proj_out.at(2 * i + 2))
                        for h in range(H1):
                            last = nc.vector.tensor_scalar(k_head[:, h, :], qk[:, 1, :], col("mask1", h), None, ALU.mult)
                        last.then_inc(masked.up(T), 1)
                        for b in range(2):
                            dve.wait_ge(attended.sem, attended.at(2 * i + b))
                            for sc in range(2):
                                o = sc * H1 * P
                                nc.vector.tensor_copy(
                                    v_flat[:, o:o + H1 * (P + C1)].rearrange("p (h n) -> p h n", h=H1)[:, :, 0:C1],
                                    v[:, sc, b * 64:(b + 1) * 64].rearrange("p (h c) -> p h c", h=H1))
                            for c in range(2):
                                n = 4 * i + 2 * b + c
                                dve.wait_ge(scored.sem, scored.at(n + 1))
                                nc.vector.tensor_reduce(neg_max, ps[:, 4:8, :].rearrange("p a (h s) -> p (a h) s", h=2),
                                                        AX.X, ALU.max, negate=True).then_inc(shifted.up(T), 1)
                                dve.wait_ge(probs_turned.sem, probs_turned.at(n + 1))
                                nc.vector.tensor_copy(pT[:, 0:4, :, c * P:(c + 1) * P].rearrange("p h s n -> p (h s) n"),
                                                      ps[:, 0:2, :].rearrange("p a (j n) -> p (a j) n", n=P)
                                                      ).then_inc(probs_out.up(T), 1)
                            dve.wait_ge(attended.sem, attended.at(2 * i + b + 1))
                            nc.vector.reciprocal(inv[0:64, :], ps[64:128, 4, 0:D]).then_inc(norm_step.up(T), 1)
                            dve.wait_ge(norm_step.sem, norm_step.at(4 * i + 3 + b))
                            nc.vector.tensor_tensor(attn[0:64, b, :], ps[0:64, 4, 0:D], inv[0:64, :], ALU.mult
                                                    ).then_inc(attn_ready.up(T), 1)
                        dve.wait_ge(out_made.sem, out_made.at(i + 1))
                        nc.vector.tensor_scalar(tmp, ps[:, 5, 0:D], col("bo"), gain[:, layer:layer + 1], ALU.add, ALU.mult
                                                ).then_inc(gate_step.up(T), 1)
                        dve.wait_ge(gate_step.sem, gate_step.at(i + 1))
                        nc.vector.tensor_tensor(x[:, i, :], x[:, i, :], tmp, ALU.add).then_inc(proj_exp.up(T), 1)
                        dve.wait_ge(proj_exp.sem, proj_exp.at(i + 1))
                        norm_dve(dve, 2 * i + 1, x[:, i, :], xn, stats)
                        router_dve(dve, i)
            end_stage()

        def attention2():
            used[0] = 0
            layer = 2
            w_in = att_w[:, 0:2 * D].rearrange("p (k n) -> p k n", k=KC)
            w_out = att_w[:, 2 * D:4 * D].rearrange("p (k n) -> p k n", k=KC)
            pick = att_w[:, 4 * D:4 * D + L]
            stats = carve_stats()
            index, y_buf = carve(TOP).bitcast(U32), carve(TOP, D)
            xn, xT, ctx_t = carve(D), carve(KC, P), carve(D)
            keep = carve(1)
            geo, geo_in = carve(L), carve(L)
            decay_sum, total = carve(1), carve(1)
            by_batch = carve(2)
            bias = carve(KC)
            ctx_sum = carve(KC, B)
            state = carve(KC, B)
            state_tok = carve(KC, 2, L)
            y2, tmp = carve(D), carve(D)
            n = [0]

            with nc.Block() as block:
                @block.sync
                def _(sp):
                    for buf, name in ((w_in, "w_in2"), (w_out, "w_out2")):
                        sp.dma_start(buf, d[name].rearrange("(k p) n -> p k n", p=P)).then_inc(att_w_in.up(), 16)
                    sp.dma_start(pick, d["pick"]).then_inc(att_w_in.up(), 16)
                    load_ffn(sp, layer)
                    with sp.Fori(0, T) as i:
                        sp.wait_ge(scored.sem, scored.at(i))
                        sp.dma_start(ctx_t, d["ctx"][i]).then_inc(ctx_in.up(T), 16)

                @block.gpsimd
                def _(pool):
                    with pool.Fori(0, T) as i:
                        gather_rows(pool, i, index, y_buf)
                        norm_pool(pool, 3 * i, stats)
                        norm_pool(pool, 3 * i + 1, stats)
                        norm_pool(pool, 3 * i + 2, stats)
                        save_norm(pool, i, 3 * i + 2, xn)

                @block.tensor
                def _(pe):
                    pe.wait_ge(att_w_in.sem, att_w_in.at(3))
                    pe.wait_ge(masked.sem, masked.at(1))
                    with pe.Fori(0, T) as i:
                        pe.wait_ge(ctx_in.sem, ctx_in.at(i + 1))
                        for k in range(KC):
                            mm = nc.tensor.matmul(ps[:, 2 + k, bass.ds(2 * i, 2)], ctx_t[:, k * P:(k + 1) * P], by_batch,
                                                  start=True, stop=True)
                        mm.then_inc(scored.up(T), 1)
                    pe.wait_ge(shifted.sem, shifted.at(1))
                    for g in range(KC):
                        for k in range(KC):
                            mm = nc.tensor.matmul(ps[:, 4, g * B:(g + 1) * B], w_in[:, k, g * P:(g + 1) * P],
                                                  ctx_sum[:, k, :], start=(k == 0), stop=(k == KC - 1))
                    mm.then_inc(projected.up(), 1)
                    with pe.Fori(0, T) as i:
                        pe.wait_ge(attn_ready.sem, attn_ready.at(i + 1))
                        for k in range(KC):
                            mm = nc.tensor.matmul(ps[:, 5, 0:D], state_tok[:, k].rearrange("p b l -> p (b l)"),
                                                  w_out[:, k, :], start=(k == 0), stop=(k == KC - 1))
                        mm.then_inc(out_made.up(T), 1)
                        router_pe(pe, layer, 3 * i + 2, i, xn, xT)

                @block.scalar
                def _(act):
                    nc.scalar.activation(keep, col("decay"), ACT.Exp, scale=-1.0).then_inc(probs.up(), 1)
                    with act.Fori(0, T) as i:
                        turned_act(act, i, xT)

                @block.vector
                def _(dve):
                    def then(ins):
                        n[0] += 1
                        ins.then_inc(step.up(), 1)
                        dve.wait_ge(step.sem, step.at(n[0]))

                    dve.wait_ge(probs.sem, probs.at(1))
                    dve.wait_ge(att_w_in.sem, att_w_in.at(3))
                    then(nc.vector.tensor_scalar(keep, keep, 1.0, None, ALU.add))
                    then(nc.vector.reciprocal(keep, keep))
                    then(nc.vector.tensor_copy(geo_in, keep.to_broadcast([P, L])))
                    then(nc.vector.tensor_tensor_scan(geo, geo_in, ones[:, 0:L], 0.0, ALU.mult, ALU.add))
                    then(nc.vector.tensor_reduce(total, geo, AX.X, ALU.add))
                    then(nc.vector.tensor_tensor(geo_in, geo, pick, ALU.mult))
                    then(nc.vector.tensor_reduce(decay_sum, geo_in, AX.X, ALU.add))
                    nc.vector.tensor_scalar(by_batch, col("batch_of", 0, 2), decay_sum, None, ALU.mult
                                            ).then_inc(masked.up(), 1)
                    then(nc.vector.tensor_scalar(bias, col("b_in", 0, 2), total, None, ALU.mult))
                    dve.wait_ge(scored.sem, scored.at(T))
                    nc.vector.tensor_copy(ctx_sum, ps[:, 2:4, 0:B]).then_inc(shifted.up(), 1)
                    dve.wait_ge(projected.sem, projected.at(1))
                    for k in range(KC):
                        last = nc.vector.tensor_scalar(state[:, k, :], ps[:, 4, k * B:(k + 1) * B], bias[:, k:k + 1], 1.0 / L,
                                                       ALU.add, ALU.mult)
                    then(last)
                    with dve.Fori(0, T) as i:
                        dve.wait_ge(saved.sem, saved.at(i))
                        nc.vector.tensor_copy(
                            state_tok, state[:, :, bass.ds(2 * i, 2)].unsqueeze(3).to_broadcast([P, KC, 2, L])
                        ).then_inc(attn_ready.up(T), 1)
                        add_rows(dve, i, y_buf)
                        norm_dve(dve, 3 * i, x[:, i, :], xn, stats)
                        dve.wait_ge(ln_done.sem, ln_done.at(3 * i + 1))
                        nc.vector.tensor_tensor(y2, xn, row("b_out"), ALU.add).then_inc(gate_step.up(T), 1)
                        dve.wait_ge(gate_step.sem, gate_step.at(4 * i + 1))
                        dve.wait_ge(out_made.sem, out_made.at(i + 1))
                        nc.vector.tensor_tensor(y2, y2, ps[:, 5, 0:D], ALU.add).then_inc(gate_step.up(T), 1)
                        dve.wait_ge(gate_step.sem, gate_step.at(4 * i + 2))
                        norm_dve(dve, 3 * i + 1, y2, tmp, stats)
                        dve.wait_ge(ln_done.sem, ln_done.at(3 * i + 2))
                        nc.vector.tensor_tensor(tmp, tmp, row("gamma"), ALU.mult).then_inc(gate_step.up(T), 1)
                        dve.wait_ge(gate_step.sem, gate_step.at(4 * i + 3))
                        nc.vector.tensor_tensor(tmp, tmp, row("beta"), ALU.add).then_inc(gate_step.up(T), 1)
                        dve.wait_ge(gate_step.sem, gate_step.at(4 * i + 4))
                        nc.vector.scalar_tensor_tensor(out=x[:, i, :], in0=tmp, scalar=gain[:, layer:layer + 1],
                                                       in1=x[:, i, :], op0=ALU.mult, op1=ALU.add
                                                       ).then_inc(proj_exp.up(T), 1)
                        dve.wait_ge(proj_exp.sem, proj_exp.at(i + 1))
                        norm_dve(dve, 3 * i + 2, x[:, i, :], xn, stats)
                        router_dve(dve, i)
            end_stage()

        def attention3():
            used[0] = 0
            layer = 3
            wq = att_w[:, 0:2 * D].rearrange("p (k n) -> p k n", k=KC)
            wk = att_w[:, 2 * D:4 * D].rearrange("p (k n) -> p k n", k=KC)
            wfc = att_w[:, 4 * D:6 * D].rearrange("p (k n) -> p k n", k=KC)
            NV = G3 * C3
            wv = att_w[:, 6 * D:6 * D + KC * NV].rearrange("p (k n) -> p k n", k=KC)
            stats = carve_stats()
            index, y_buf = carve(TOP).bitcast(U32), carve(TOP, D)
            xn, xT, cT = carve(D), carve(KC, P), carve(KC, P)
            qT, kT = carve(KC, P), carve(KC, P)
            HG = P // C3
            k_head = carve(KC, 2, HG, L)
            v_pair = carve(G3, 2, 2, C3 + 1)
            mx = carve(H3)
            p = carve(H3, L)
            pT = carve(H3 // 2, P)
            inv = carve(H3)
            o, oT = carve(H3, C3), carve(KC, P)
            tmp = carve(D)
            W = 4 * (C3 + 1)

            with nc.Block() as block:
                @block.sync
                def _(sp):
                    for buf, name in ((wq, "wq3"), (wk, "wk3"), (wfc, "wfc3"), (wv, "wv3")):
                        sp.dma_start(buf, d[name].rearrange("(k p) n -> p k n", p=P)).then_inc(att_w_in.up(), 16)
                    load_ffn(sp, layer)
                    sp.dma_start(shared_up, d["shared_up"].rearrange("(k p) n -> p k n", p=P)).then_inc(ffn_w_in.up(), 16)
                    for c, n in chunks(SHARED):
                        sp.dma_start(shared_down[0:n, c, :], d["shared_down"][c * P:c * P + n, :]).then_inc(ffn_w_in.up(), 16)
                    with sp.Fori(0, T) as i:
                        sp.wait_ge(projected.sem, projected.at(i))
                        sp.dma_start(cT, d["ctxT"][i]).then_inc(ctx_in.up(T), 16)

                @block.gpsimd
                def _(pool):
                    with pool.Fori(0, T) as i:
                        gather_rows(pool, i, index, y_buf)
                        norm_pool(pool, 2 * i, stats)
                        norm_pool(pool, 2 * i + 1, stats)
                        save_norm(pool, i, 2 * i + 1, xn)

                @block.tensor
                def _(pe):
                    pe.wait_ge(att_w_in.sem, att_w_in.at(4))
                    with pe.Fori(0, T) as i:
                        pe.wait_ge(ln_done.sem, ln_done.at(2 * i + 1))
                        turn(pe, xn, 0).then_inc(turned.up(T), 1)
                        pe.wait_ge(ctx_in.sem, ctx_in.at(i + 1))
                        pe.wait_ge(turned_out.sem, turned_out.at(2 * i + 1))
                        for w, src, at in ((wq, xT, 0), (wk, cT, D)):
                            for g in range(KC):
                                for k in range(KC):
                                    nc.tensor.matmul(ps[:, 2, at + g * P:at + (g + 1) * P], w[:, k, g * P:(g + 1) * P],
                                                     src[:, k, :], start=(k == 0), stop=(k == KC - 1))
                        for k in range(KC):
                            mm = nc.tensor.matmul(ps[:, 3, 0:NV], cT[:, k, :], wv[:, k, :], start=(k == 0), stop=(k == KC - 1))
                        mm.then_inc(projected.up(T), 1)
                        pe.wait_ge(masked.sem, masked.at(i + 1))
                        for b in range(2):
                            for g in range(KC):
                                for a in range(2):
                                    mm = nc.tensor.matmul(
                                        ps[b * L:(b + 1) * L, 4 + 2 * g + a, :], qT[:, g, b * L:(b + 1) * L],
                                        k_head[:, g, b, a * 8:(a + 1) * 8, :].rearrange("p h s -> p (h s)"),
                                        start=True, stop=True)
                        mm.then_inc(scored.up(T), 1)
                        pe.wait_ge(probs.sem, probs.at(i + 1))
                        for j in range(H3 // 2):
                            mm = nc.tensor.transpose(ps[:, j // 4, (j % 4) * P:(j % 4 + 1) * P],
                                                     p[:, 2 * j:2 * j + 2, :].rearrange("p h s -> p (h s)"), ident[:])
                        mm.then_inc(probs_turned.up(T), 1)
                        pe.wait_ge(probs_out.sem, probs_out.at(2 * i + 2))
                        for j in range(H3 // 2):
                            mm = nc.tensor.matmul(ps[:, 4 + j // 8, (j % 8) * W:(j % 8 + 1) * W], pT[:, j, :],
                                                  v_pair[:, j // 2].rearrange("p b h c -> p (b h c)"), start=True, stop=True)
                        mm.then_inc(attended.up(T), 1)
                        pe.wait_ge(attn_ready.sem, attn_ready.at(i + 1))
                        turn(pe, o.rearrange("p h c -> p (h c)"), 6).then_inc(up_made.up(T), 1)
                        pe.wait_ge(hT_ready.sem, hT_ready.at(i + 1))
                        for k in range(KC):
                            mm = nc.tensor.matmul(ps[:, 7, 0:D], oT[:, k, :], wfc[:, k, :], start=(k == 0), stop=(k == KC - 1))
                        mm.then_inc(out_made.up(T), 1)
                        router_pe(pe, layer, 2 * i + 1, 2 * i + 1, xn, xT)

                @block.scalar
                def _(act):
                    nc.scalar.activation(table_call[:], half[:], ACT.Exp)
                    with act.Fori(0, T) as i:
                        turned_act(act, 2 * i, xT)
                        act.wait_ge(projected.sem, projected.at(i + 1))
                        nc.scalar.copy(qT.rearrange("p k t -> p (k t)"), ps[:, 2, 0:D]).then_inc(proj_out.up(T), 1)
                        nc.scalar.copy(kT.rearrange("p k t -> p (k t)"), ps[:, 2, D:2 * D]).then_inc(proj_out.up(T), 1)
                        act.wait_ge(shifted.sem, shifted.at(i + 1))
                        nc.scalar.activation(p.rearrange("p h s -> p (h s)"), p.rearrange("p h s -> p (h s)"), ACT.Exp,
                                             scale=float(1.0 / np.sqrt(C3))).then_inc(probs.up(T), 1)
                        act.wait_ge(probs_turned.sem, probs_turned.at(i + 1))
                        nc.scalar.copy(pT[:, 8:16, :], ps[:, 2:4, :].rearrange("p a (j n) -> p (a j) n", n=P)
                                       ).then_inc(probs_out.up(T), 1)
                        act.wait_ge(up_made.sem, up_made.at(i + 1))
                        nc.scalar.copy(oT.rearrange("p k t -> p (k t)"), ps[:, 6, 0:D]).then_inc(hT_ready.up(T), 1)
                        turned_act(act, 2 * i + 1, xT)

                @block.vector
                def _(dve):
                    nc.vector.memset(v_pair, 0.0).then_inc(ready.up(), 1)
                    dve.wait_ge(ready.sem, ready.at(1))
                    for a in range(2):
                        last = nc.vector.memset(v_pair[a * L:(a + 1) * L, :, :, a, C3:C3 + 1], 1.0)
                    last.then_inc(ready.up(), 1)
                    dve.wait_ge(ready.sem, ready.at(2))
                    with dve.Fori(0, T) as i:
                        dve.wait_ge(saved.sem, saved.at(i))
                        add_rows(dve, i, y_buf)
                        norm_dve(dve, 2 * i, x[:, i, :], xn, stats)
                        dve.wait_ge(proj_out.sem, proj_out.at(2 * i + 2))
                        for h in range(HG):
                            nc.vector.tensor_scalar(k_head[:, :, :, h, :], kT.rearrange("p g (b s) -> p g b s", b=2),
                                                    col("mask3", h), None, ALU.mult)
                        for b in range(2):
                            for a in range(2):
                                last = nc.vector.tensor_copy(v_pair[a * L:(a + 1) * L, :, b, a, 0:C3],
                                                             ps[b * L:(b + 1) * L, 3, 0:NV].rearrange("p (g c) -> p g c", g=G3))
                        last.then_inc(masked.up(T), 1)
                        dve.wait_ge(scored.sem, scored.at(i + 1))
                        nc.vector.tensor_reduce(mx, ps[:, 4:8, :].rearrange("p a (h s) -> p (a h) s", s=L), AX.X, ALU.max
                                                ).then_inc(gate_step.up(T), 1)
                        dve.wait_ge(gate_step.sem, gate_step.at(3 * i + 1))
                        nc.vector.tensor_tensor(p, ps[:, 4:8, :].rearrange("p a (h s) -> p (a h) s", s=L),
                                                mx.unsqueeze(2).to_broadcast([P, H3, L]), ALU.subtract
                                                ).then_inc(shifted.up(T), 1)
                        dve.wait_ge(probs_turned.sem, probs_turned.at(i + 1))
                        nc.vector.tensor_copy(pT[:, 0:8, :], ps[:, 0:2, :].rearrange("p a (j n) -> p (a j) n", n=P)
                                              ).then_inc(probs_out.up(T), 1)
                        dve.wait_ge(attended.sem, attended.at(i + 1))
                        for b in range(2):
                            tok = slice(b * L, (b + 1) * L)
                            for a in range(2):
                                got = ps[tok, 4 + a, 0:8 * W].rearrange("p (j b h c) -> p j b h c", j=8, b=2, h=2)
                                last = nc.vector.reciprocal(
                                    inv[tok, a * 16:(a + 1) * 16].rearrange("p (j h) -> p j h", j=8), got[:, :, b, :, C3])
                        last.then_inc(gate_step.up(T), 1)
                        dve.wait_ge(gate_step.sem, gate_step.at(3 * i + 2))
                        for b in range(2):
                            tok = slice(b * L, (b + 1) * L)
                            for a in range(2):
                                got = ps[tok, 4 + a, 0:8 * W].rearrange("p (j b h c) -> p j b h c", j=8, b=2, h=2)
                                last = nc.vector.tensor_tensor(
                                    o[tok, a * 16:(a + 1) * 16, :].rearrange("p (j h) c -> p j h c", j=8),
                                    got[:, :, b, :, 0:C3],
                                    inv[tok, a * 16:(a + 1) * 16].rearrange("p (j h) -> p j h", j=8).unsqueeze(3)
                                    .to_broadcast([L, 8, 2, C3]), ALU.mult)
                        last.then_inc(attn_ready.up(T), 1)
                        dve.wait_ge(out_made.sem, out_made.at(i + 1))
                        nc.vector.tensor_tensor(tmp, ps[:, 7, 0:D], row("bfc"), ALU.add).then_inc(gate_step.up(T), 1)
                        dve.wait_ge(gate_step.sem, gate_step.at(3 * i + 3))
                        nc.vector.scalar_tensor_tensor(out=x[:, i, :], in0=tmp, scalar=gain[:, layer:layer + 1],
                                                       in1=x[:, i, :], op0=ALU.mult, op1=ALU.add
                                                       ).then_inc(proj_exp.up(T), 1)
                        dve.wait_ge(proj_exp.sem, proj_exp.at(i + 1))
                        norm_dve(dve, 2 * i + 1, x[:, i, :], xn, stats)
                        router_dve(dve, i)
            end_stage()

        s_at = E * (KC * 2 * HIDDEN[3] + len(chunks(HIDDEN[3])) * D)
        shared_up = ffn_w[:, s_at:s_at + KC * 2 * SHARED].rearrange("p (k m) -> p k m", k=KC)
        s_at += KC * 2 * SHARED
        n_sc = len(chunks(SHARED))
        shared_down = ffn_w[:, s_at:s_at + n_sc * D].rearrange("p (c n) -> p c n", c=n_sc)

        def shared_expert():
            used[0] = 0
            xs, xT = carve(D), carve(KC, P)
            hid, hT = carve(SHARED), carve(n_sc, P)
            with nc.Block() as block:
                @block.tensor
                def _(pe):
                    pe.wait_ge(ffn_w_in.sem, ffn_w_in.at(0))
                    with pe.Fori(0, T) as i:
                        pe.wait_ge(ln_done.sem, ln_done.at(i + 1))
                        turn(pe, xs, 0).then_inc(xT_made.up(T), 1)
                        pe.wait_ge(xT_ready.sem, xT_ready.at(i + 1))
                        for a in range(2):
                            for k in range(KC):
                                mm = nc.tensor.matmul(ps[:, 1 + a, 0:SHARED], xT[:, k, :],
                                                      shared_up[:, k, a * SHARED:(a + 1) * SHARED],
                                                      start=(k == 0), stop=(k == KC - 1))
                        mm.then_inc(up_made.up(T), 1)
                        pe.wait_ge(h_ready.sem, h_ready.at(i + 1))
                        for c, n in chunks(SHARED):
                            mm = nc.tensor.transpose(ps[0:n, 5, c * P:(c + 1) * P], hid[:, c * P:c * P + n], ident[:])
                        mm.then_inc(hT_made.up(T), 1)
                        pe.wait_ge(hT_ready.sem, hT_ready.at(i + 1))
                        for c, n in chunks(SHARED):
                            mm = nc.tensor.matmul(ps[:, 6, 0:D], hT[0:n, c, :], shared_down[0:n, c, :],
                                                  start=(c == 0), stop=(c == n_sc - 1))
                        mm.then_inc(y_made.up(T), 1)

                @block.scalar
                def _(act):
                    nc.scalar.activation(table_call[:], half[:], ACT.Silu)
                    with act.Fori(0, T) as i:
                        act.wait_ge(up_made.sem, up_made.at(i + 1))
                        nc.scalar.activation(hid, ps[:, 1, 0:SHARED], ACT.Silu).then_inc(silu_ready.up(T), 1)
                        act.wait_ge(hT_made.sem, hT_made.at(i + 1))
                        for c, n in chunks(SHARED):
                            last = nc.scalar.copy(hT[0:n, c, :], ps[0:n, 5, c * P:(c + 1) * P])
                        last.then_inc(hT_ready.up(T), 1)

                @block.vector
                def _(dve):
                    with dve.Fori(0, T) as i:
                        nc.vector.tensor_copy(xs, xn2[:, i, :]).then_inc(ln_done.up(T), 1)
                        dve.wait_ge(xT_made.sem, xT_made.at(i + 1))
                        nc.vector.tensor_copy(xT.rearrange("p k t -> p (k t)"), ps[:, 0, 0:2 * P]
                                              ).then_inc(xT_ready.up(T), 1)
                        dve.wait_ge(silu_ready.sem, silu_ready.at(i + 1))
                        nc.vector.tensor_tensor(hid, hid, ps[:, 2, 0:SHARED], ALU.mult).then_inc(h_ready.up(T), 1)
                        dve.wait_ge(y_made.sem, y_made.at(i + 1))
                        nc.vector.scalar_tensor_tensor(out=x[:, i, :], in0=ps[:, 6, 0:D], scalar=gain[:, 7:8],
                                                       in1=x[:, i, :], op0=ALU.mult, op1=ALU.add
                                                       ).then_inc(added.up(T), 1)
                        dve.wait_ge(added.sem, added.at(i + 1))
            end_stage()

        def route(layer):
            used[0] = 0
            top = carve(T, E)
            index8 = carve(T, E).bitcast(U32)
            index = carve(T, TOP)
            onehot = carve(TOP, T, E)
            chosen = carve(T, E)
            total = carve(E, T)
            scan_mask = carve(E, T)
            running = carve(E, T)
            many = carve(E, T)
            tiles_of = carve(E)
            tiles_to = carve(E)
            base = carve(E)
            grid = carve(T, E)
            picked = carve(TOP, T, E)
            slot_f = carve(TOP, T)
            passed = carve(SLOT_TILES, E)
            expert_f = carve(SLOT_TILES)
            gap, e_gap, w_sum = carve(T), carve(T), carve(T)
            rmax, prob = carve(T), carve(T, E)
            source = prob if layer == 3 else logits
            n = [0]

            with nc.Block() as block:
                @block.tensor
                def _(pe):
                    pe.wait_ge(h_ready.sem, h_ready.at(1))
                    nc.tensor.matmul(ps[:, 0, 0:P], before[:], chosen.rearrange("p t e -> p (t e)"), start=True, stop=True)
                    nc.tensor.matmul(ps[:, 1, 0:P], ones[:], chosen.rearrange("p t e -> p (t e)"), start=True, stop=True
                                     ).then_inc(y_made.up(), 1)

                @block.scalar
                def _(act):
                    if layer == 3:
                        act.wait_ge(silu_ready.sem, silu_ready.at(1))
                        nc.scalar.activation(prob, prob, ACT.Exp).then_inc(xT_ready.up(), 1)
                    else:
                        act.wait_ge(silu_ready.sem, silu_ready.at(1))
                        nc.scalar.activation(e_gap, gap, ACT.Exp).then_inc(xT_ready.up(), 1)

                @block.vector
                def _(dve):
                    def then(ins):
                        n[0] += 1
                        ins.then_inc(step.up(), 1)
                        dve.wait_ge(step.sem, step.at(n[0]))

                    if layer == 3:
                        then(nc.vector.tensor_reduce(rmax, logits[:], AX.X, ALU.max))
                        nc.vector.tensor_tensor(prob, logits[:], rmax.unsqueeze(2).to_broadcast([P, T, E]), ALU.subtract
                                                ).then_inc(silu_ready.up(), 1)
                        dve.wait_ge(xT_ready.sem, xT_ready.at(1))
                        then(nc.vector.tensor_reduce(w_sum, prob, AX.X, ALU.add))
                        then(nc.vector.reciprocal(w_sum, w_sum))
                        then(nc.vector.tensor_tensor(prob, prob, w_sum.unsqueeze(2).to_broadcast([P, T, E]), ALU.mult))
                    for t in range(T):
                        last = nc.vector.max(top[:, t, :], source[:, t, :])
                    then(last)
                    for t in range(T):
                        last = nc.vector.max_index(index8[:, t, :], top[:, t, :], source[:, t, :])
                    then(last)
                    if layer != 3:
                        nc.vector.tensor_tensor(gap, top[:, :, 1], top[:, :, 0], ALU.subtract).then_inc(silu_ready.up(), 1)
                    then(nc.vector.tensor_copy(index, index8[:, :, 0:TOP]))
                    for a in range(TOP):
                        last = nc.vector.tensor_tensor(
                            onehot[:, a], row("iota8").unsqueeze(1).to_broadcast([P, T, E]),
                            index[:, :, a:a + 1].to_broadcast([P, T, E]), ALU.is_equal)
                    then(last)
                    nc.vector.tensor_tensor(chosen, onehot[:, 0], onehot[:, 1], ALU.add).then_inc(h_ready.up(), 1)
                    nc.vector.memset(scan_mask, 1.0)
                    dve.wait_ge(y_made.sem, y_made.at(1))
                    then(nc.vector.tensor_copy(total, ps[:, 1, 0:P].rearrange("p (t e) -> p e t", e=E)))
                    then(nc.vector.memset(scan_mask[:, :, 0:1], 0.0))
                    then(nc.vector.tensor_tensor_scan(running.rearrange("p e t -> p (e t)"),
                                                      scan_mask.rearrange("p e t -> p (e t)"),
                                                      total.rearrange("p e t -> p (e t)"), 0.0, ALU.mult, ALU.add))
                    then(nc.vector.tensor_tensor(many, running[:, :, T - 1:T].to_broadcast([P, E, T]),
                                                 row("iota_k").unsqueeze(1).to_broadcast([P, E, T]), ALU.is_gt))
                    then(nc.vector.tensor_reduce(tiles_of, many, AX.X, ALU.add))
                    then(nc.vector.tensor_tensor_scan(tiles_to, ones[:, 0:E], tiles_of, 0.0, ALU.mult, ALU.add))
                    then(nc.vector.tensor_tensor(base, tiles_to, tiles_of, ALU.subtract))
                    then(nc.vector.tensor_scalar(base, base, float(P), None, ALU.mult))
                    then(nc.vector.tensor_tensor(running, running, total, ALU.subtract))
                    then(nc.vector.tensor_tensor(running, running, base.unsqueeze(2).to_broadcast([P, E, T]), ALU.add))
                    then(nc.vector.tensor_tensor(grid, ps[:, 0, 0:P].rearrange("p (t e) -> p t e", e=E),
                                                 running.rearrange("p e t -> p t e"), ALU.add))
                    for a in range(TOP):
                        last = nc.vector.tensor_tensor(picked[:, a], onehot[:, a], grid, ALU.mult)
                    then(last)
                    then(nc.vector.tensor_reduce(slot_f, picked, AX.X, ALU.add))
                    then(nc.vector.tensor_copy(slots[:], slot_f))
                    then(nc.vector.tensor_tensor(passed, row("iota_j").unsqueeze(2).to_broadcast([P, SLOT_TILES, E]),
                                                 tiles_to.unsqueeze(1).to_broadcast([P, SLOT_TILES, E]), ALU.is_ge))
                    then(nc.vector.tensor_reduce(expert_f, passed, AX.X, ALU.add))
                    then(nc.vector.tensor_scalar(expert_f, expert_f, float(E - 1), None, ALU.min))
                    then(nc.vector.tensor_copy(tile_expert[:], expert_f[0:1, :]))
                    g = gain[:, 4 + layer:5 + layer]
                    if layer == 3:
                        then(nc.vector.tensor_scalar(weight[:].rearrange("p a t -> p t a"), top[:, :, 0:TOP], g, None, ALU.mult))
                    else:
                        dve.wait_ge(xT_ready.sem, xT_ready.at(1))
                        then(nc.vector.tensor_scalar(w_sum, e_gap, 1.0, None, ALU.add))
                        then(nc.vector.reciprocal(w_sum, w_sum))
                        then(nc.vector.tensor_scalar(weight[:, 0, :], w_sum, g, None, ALU.mult))
                        then(nc.vector.tensor_tensor(weight[:, 1, :], weight[:, 0, :], e_gap, ALU.mult))
            end_stage()

        def experts(layer):
            used[0] = 0
            m = HIDDEN[layer]
            cs = chunks(m)
            NT = SLOT_TILES
            wide = 2 * m > 512
            xs = [carve(D) for _ in range(2)]
            xT = [carve(KC, P) for _ in range(2)]
            silu = [carve(m) for _ in range(2)]
            hT = [carve(len(cs), P) for _ in range(2)]
            y = [carve(D) for _ in range(2)]
            up, down = up_view(layer), down_view(layer)
            PAIRS = NT // 2

            def gate_bank(u):
                return 1 + 2 * u

            def up_part(u):
                return ps[:, 2 + 2 * u, 0:m] if wide else ps[:, 1 + 2 * u, m:2 * m]

            with nc.Block() as block:
                @block.sync
                def _(sp):
                    sp.wait_ge(scattered.sem, scattered.at(TOP * T))

                    def load(k, u):
                        sp.wait_ge(xT_made.sem, xT_made.at(2 * k + u - 1))
                        sp.dma_start(xs[u], slot_x[bass.ds((2 * k + u) * P, P), :]).then_inc(slot_in[u].sem, 16)

                    def store(k, u):
                        sp.wait_ge(y_ready.sem, y_ready.at(2 * k + u + 1))
                        sp.dma_start(slot_y[bass.ds((2 * k + u) * P, P), :], y[u]).then_inc(slot_out[u].sem, 16)

                    load(0, 0)
                    load(0, 1)
                    with sp.Fori(0, PAIRS - 1) as i:
                        for u in range(2):
                            load(i + 1, u)
                            store(i, u)
                    load(PAIRS, 0)
                    store(PAIRS - 1, 0)
                    store(PAIRS - 1, 1)
                    store(PAIRS, 0)
                    for u in range(2):
                        slot_in[u].up(PAIRS + 1 - u)
                        slot_out[u].up(PAIRS + 1 - u)
                        sp.wait_ge(slot_out[u].sem, slot_out[u].at(PAIRS + 1 - u))

                @block.gpsimd
                def _(pool):
                    for t in range(T):
                        for a in range(TOP):
                            nc.gpsimd.indirect_dma_start(
                                slot_x, bass.IndirectOffsetOnAxis(ap=slots[:, a, t:t + 1], axis=0), xn2[:, t, :], None
                            ).then_inc(scattered.up(), 16)

                @block.tensor
                def _(pe):
                    pe.wait_ge(ffn_w_in.sem, ffn_w_in.at(0))

                    def first(k, u):
                        j = 2 * k + u
                        pe.wait_ge(slot_in[u].sem, slot_in[u].at(k + 1))
                        pe.wait_ge(xT_ready.sem, xT_ready.at(j))
                        turn(pe, xs[u], 0).then_inc(xT_made.sem, 1)
                        e = pe.value_load(tile_expert[0:1, bass.ds(j, 1)], min_val=0, max_val=E - 1)
                        pe.wait_ge(xT_ready.sem, xT_ready.at(j + 1))
                        pe.wait_ge(h_ready.sem, h_ready.at(j - 1))
                        for o, n, bank in (((0, m, gate_bank(u)), (m, m, gate_bank(u) + 1)) if wide
                                           else ((0, 2 * m, gate_bank(u)),)):
                            for c in range(KC):
                                mm = nc.tensor.matmul(ps[:, bank, 0:n], xT[u][:, c, :], up[:, e, c, o:o + n],
                                                      start=(c == 0), stop=(c == KC - 1))
                        mm.then_inc(up_made.sem, 1)

                    def second(k, u):
                        j = 2 * k + u
                        pe.wait_ge(h_ready.sem, h_ready.at(j + 1))
                        pe.wait_ge(hT_ready.sem, hT_ready.at(j))
                        for c, n in cs:
                            mm = nc.tensor.transpose(ps[0:n, 5, c * P:(c + 1) * P], silu[u][:, c * P:c * P + n], ident[:])
                        mm.then_inc(hT_made.sem, 1)
                        e = pe.value_load(tile_expert[0:1, bass.ds(j, 1)], min_val=0, max_val=E - 1)
                        pe.wait_ge(hT_ready.sem, hT_ready.at(j + 1))
                        pe.wait_ge(y_ready.sem, y_ready.at(j - 1))
                        for c, n in cs:
                            mm = nc.tensor.matmul(ps[:, 6 + u, 0:D], hT[u][0:n, c, :], down[0:n, e, c, :],
                                                  start=(c == 0), stop=(c == len(cs) - 1))
                        mm.then_inc(y_made.sem, 1)

                    first(0, 0)
                    with pe.Fori(0, PAIRS) as i:
                        first(i, 1)
                        second(i, 0)
                        first(i + 1, 0)
                        second(i, 1)
                    second(PAIRS, 0)
                    for s in (xT_made, up_made, hT_made, y_made):
                        s.up(NT)

                @block.scalar
                def _(act):
                    def silu_of(k, u):
                        j = 2 * k + u
                        act.wait_ge(up_made.sem, up_made.at(j + 1))
                        act.wait_ge(hT_made.sem, hT_made.at(j - 1))
                        nc.scalar.activation(silu[u], ps[:, gate_bank(u), 0:m], ACT.Silu).then_inc(silu_ready.sem, 1)

                    def rest(k, u):
                        j = 2 * k + u
                        act.wait_ge(hT_made.sem, hT_made.at(j + 1))
                        act.wait_ge(y_made.sem, y_made.at(j - 1))
                        for c, n in cs:
                            last = nc.scalar.copy(hT[u][0:n, c, :], ps[0:n, 5, c * P:(c + 1) * P])
                        last.then_inc(hT_ready.sem, 1)
                        act.wait_ge(y_made.sem, y_made.at(j + 1))
                        act.wait_ge(slot_out[u].sem, slot_out[u].at(k))
                        nc.scalar.copy(y[u], ps[:, 6 + u, 0:D]).then_inc(y_ready.sem, 1)

                    nc.scalar.activation(table_call[:], half[:], ACT.Silu)
                    silu_of(0, 0)
                    with act.Fori(0, PAIRS) as i:
                        silu_of(i, 1)
                        rest(i, 0)
                        silu_of(i + 1, 0)
                        rest(i, 1)
                    rest(PAIRS, 0)
                    for s in (silu_ready, hT_ready, y_ready):
                        s.up(NT)

                @block.vector
                def _(dve):
                    def both(k, u):
                        j = 2 * k + u
                        dve.wait_ge(xT_made.sem, xT_made.at(j + 1))
                        dve.wait_ge(up_made.sem, up_made.at(j - 1))
                        nc.vector.tensor_copy(xT[u].rearrange("p k t -> p (k t)"), ps[:, 0, 0:2 * P]
                                              ).then_inc(xT_ready.sem, 1)
                        dve.wait_ge(silu_ready.sem, silu_ready.at(j + 1))
                        nc.vector.tensor_tensor(silu[u], silu[u], up_part(u), ALU.mult).then_inc(h_ready.sem, 1)

                    with dve.Fori(0, PAIRS) as i:
                        for u in range(2):
                            both(i, u)
                    both(PAIRS, 0)
                    for s in (xT_ready, h_ready):
                        s.up(NT)
            end_stage()

        def finish():
            used[0] = 0
            index, y_buf = carve(TOP).bitcast(U32), carve(TOP, D)
            with nc.Block() as block:
                @block.gpsimd
                def _(pool):
                    with pool.Fori(0, T) as i:
                        gather_rows(pool, i, index, y_buf)

                @block.vector
                def _(dve):
                    with dve.Fori(0, T) as i:
                        add_rows(dve, i, y_buf)
                        dve.sem_inc(tile_done.up(T), 1)

                @block.sync
                def _(sp):
                    with sp.Fori(0, T) as i:
                        sp.wait_ge(added.sem, added.at(i + 1))
                        sp.dma_start(out[bass.ds(i * P, P), :], x[:, i, :]).then_inc(out_done.up(T), 16)
                    sp.wait_ge(out_done.sem, out_done.at(T))
            end_stage()

        for layer, attention in enumerate((attention0, attention1, attention2, attention3)[:LAYERS]):
            attention()
            route(layer)
            if layer == 3:
                shared_expert()
            experts(layer)
        finish()


def host_arrays(v):
    f = np.float32
    a = {}
    a["ident"] = np.eye(P, dtype=f)
    a["before"] = np.triu(np.ones((P, P), f), 1)
    a["x"] = v["x"].reshape(T, P, D).transpose(1, 0, 2)
    a["ctx"] = v["ctx_2048"].reshape(T, P, D)
    a["ctxT"] = v["ctx_2048"].reshape(T, P, KC, P).transpose(0, 3, 2, 1)
    i = np.arange(P)
    a["mask0"] = np.tile((i[:, None] // HD0 == i[None, :] // HD0).astype(f), (1, 2))
    inv = (1.0 / 10000.0 ** (np.arange(0, C1, 2, dtype=f) / C1)).astype(f)
    pos = (np.arange(D, dtype=f)[:, None] * inv[None, :]).astype(f)
    pos = np.concatenate([pos, pos], axis=-1)
    sign = np.where(np.arange(C1) < C1 // 2, -1.0, 1.0).astype(f)
    cos = np.tile(np.cos(pos).T, (P // C1, 1)).astype(f)
    sin = np.tile((np.sin(pos) * sign).T, (P // C1, 1)).astype(f)
    scale = f(1.0 / np.sqrt(C1))

    def on_all(r):
        return np.broadcast_to(np.asarray(r, f).reshape(1, -1), (P, np.asarray(r).size))

    def vec2(b):
        return np.asarray(b).reshape(KC, P).T

    turn8 = np.arange(64).reshape(H1, 2, C1 // 2)[:, ::-1].reshape(-1)
    two = lambda b: np.concatenate([b, b]).reshape(P, 1)
    c = {"g": on_all(np.concatenate([v["g_xattn"], v["g_ffn"]])), "bg": vec2(v["L0_xattn_bg"]),
         "bq": np.concatenate([two(v["L1_xattn_bq"]), two(v["L1_xattn_bq"][turn8])], 1),
         "bk": np.concatenate([two(v["L1_xattn_bk"]), two(v["L1_xattn_bk"][turn8])], 1),
         "bo": two(v["L1_xattn_bo"]),
         "mask1": ((i[:, None] // C1) % H1 == np.arange(H1)[None, :]).astype(f),
         "mask3": (i[:, None] // C3 == np.arange(P // C3)[None, :]).astype(f),
         "decay": on_all(v["L2_xattn_decay"]), "b_in": vec2(v["L2_xattn_b_in"]),
         "batch_of": (i[:, None] // L == np.arange(2)[None, :]).astype(f)}
    a["cols"] = np.concatenate([c[n] for n, _ in COLS], 1)
    r = {"bv": on_all(np.concatenate([v["L1_xattn_bv"]] * 2)), "bfc": on_all(v["L3_xattn_bfc"]),
         "gamma": on_all(v["L2_xattn_gamma"]), "beta": on_all(v["L2_xattn_beta"]), "b_out": on_all(v["L2_xattn_b_out"]),
         "iota8": on_all(np.arange(E)), "iota_k": on_all(np.arange(T) * P), "iota_j": on_all(np.arange(SLOT_TILES)),
         "cos_q": cos * scale, "sin_q": sin * scale, "cos_k": cos, "sin_k": sin}
    a["rows"] = np.concatenate([r[n] for n, _ in ROWS], 1)
    router = [v["L0_ffn_w_gate"], v["L1_ffn_gate_w"], v["L2_ffn_Wg"].T, v["L3_ffn_W_g"]]
    a["router_w"] = np.stack(router).reshape(4, KC, P, E).transpose(2, 0, 1, 3)
    a["wq0"], a["wg0"], a["wkv0"], a["wo0"] = (v[f"L0_xattn_{n}"].T for n in ("Wq", "Wg", "Wkv", "Wo"))
    a["up0"] = np.concatenate([v["L0_ffn_wi_0"], v["L0_ffn_wi_1"]], 2)
    a["down0"] = v["L0_ffn_wo"]
    a["up1"] = np.concatenate([v["L1_ffn_w0"], v["L1_ffn_w1"]], 2)
    a["down1"] = v["L1_ffn_wo"]
    a["up2"] = np.concatenate([v["L2_ffn_W1"], v["L2_ffn_W2"]], 1).transpose(0, 2, 1)
    a["down2"] = v["L2_ffn_W3"].transpose(0, 2, 1)
    a["up3"] = np.concatenate([v["L3_ffn_Wg"], v["L3_ffn_Wu"]], 2)
    a["down3"] = v["L3_ffn_Wd"]
    a["shared_up"] = np.concatenate([v["L3_ffn_Ws_gate"], v["L3_ffn_Ws_up"]], 1)
    a["shared_down"] = v["L3_ffn_Ws_down"]

    def both(w):
        z = np.zeros((P, P), f)
        z[0:64, 0:64] = z[64:P, 64:P] = w.T
        return z

    a["wq1"], a["wq1_turned"] = both(v["L1_xattn_Wq"]), both(v["L1_xattn_Wq"][turn8])
    a["wk1"], a["wk1_turned"] = both(v["L1_xattn_Wk"]), both(v["L1_xattn_Wk"][turn8])
    a["wv1"] = both(v["L1_xattn_Wv"])
    wo1 = np.zeros((64, 2, P), f)
    wo1[:, 0, 0:64] = wo1[:, 1, 64:P] = v["L1_xattn_Wo"].T
    a["wo1"] = wo1
    a["w_in2"], a["w_out2"] = v["L2_xattn_W_in"].T, v["L2_xattn_W_out"].T
    a["pick"] = (np.arange(L)[None, :] == L - 1 - i[:, None] % L).astype(f)
    a["wq3"], a["wfc3"], a["wv3"] = (v[f"L3_xattn_{n}"].T for n in ("Wq", "Wfc", "Wv"))
    a["wk3"] = np.repeat(v["L3_xattn_Wk"].reshape(G3, C3, D), H3 // G3, 0).reshape(H3 * C3, D).T
    return {f"in_{k}": np.ascontiguousarray(b) for k, b in a.items()}


def kernel(**inputs):
    import concourse.bacc as bacc
    from concourse.bass_utils import run_bass_kernel_spmd

    nc = bacc.Bacc("TRN2", target_bir_lowering=False, num_devices=1)
    arrays = host_arrays({k: np.asarray(a) for k, a in inputs.items()})
    d = {k[3:]: nc.dram_tensor(k, a.shape, mybir.dt.from_np(a.dtype), kind="ExternalInput").ap()
         for k, a in arrays.items()}
    out = nc.dram_tensor("out", (B * L, D), F32, kind="ExternalOutput").ap()
    build(nc, d, out)
    r = run_bass_kernel_spmd(nc, [arrays], core_ids=[0])
    return r.results[0]["out"].reshape(B, L, D)
```

```python
from contextlib import ExitStack

import numpy as np

import concourse.bass as bass
from concourse import mybir

F32 = mybir.dt.float32
BF16 = mybir.dt.bfloat16
I32 = mybir.dt.int32
U32 = mybir.dt.uint32
ALU = mybir.AluOpType
ACT = mybir.ActivationFunctionType
AX = mybir.AxisListType

P = 128
B, L, D = 32, 64, 256
T = B * L // P
KC = D // P
E = 8
TOP = 2
LAYERS = 4
START = 2
SLOT_TILES = TOP * B * L // P + E - 1
WORK = 14760
LN_EPS = 1e-5
LIN_EPS = 1e-6
HIDDEN = (128, 512, 176, 176)
SHARED = 352
HD0 = 16
H1, C1 = 8, 8
H3, G3, C3 = 32, 8, 8
TW = L

COLS = (("g", 8), ("bg", 2), ("bq", 2), ("bk", 2), ("bo", 1), ("mask3", 16),
        ("decay", 1), ("b_in", 2), ("batch_of", 2))
ROWS = (("bv", 128), ("bfc", D), ("gamma", D), ("beta", D), ("b_out", D), ("iota8", E), ("iota_k", T),
        ("iota_j", SLOT_TILES), ("cos_q", D), ("sin_q", D), ("cos_k", D), ("sin_k", D))


class Signal:

    def __init__(self, sem, step, start):
        self.sem, self.step, self.start = sem, step, start
        self.base, self.raised = start * step, 0

    def up(self, times=1):
        self.raised += times
        return self.sem

    def at(self, n):
        return n * self.step + self.base

    def end_stage(self):
        self.base += self.raised * self.step
        self.raised = 0


def chunks(m):
    return [(c, min(P, m - c * P)) for c in range((m + P - 1) // P)]


def build(nc, d, out):
    ctx = ExitStack()
    with ctx:
        def sb(name, shape, dt=F32):
            return ctx.enter_context(nc.sbuf_tensor(name, shape, dt))

        signals = []

        def sig(name, step=1, start=START):
            signals.append(Signal(ctx.enter_context(nc.semaphore(name)), step, start))
            return signals[-1]

        def end_stage():
            for s in signals:
                s.end_stage()

        slot_x = nc.dram_tensor("slot_x", (SLOT_TILES * P, D), F32, kind="Internal").ap()
        slot_y = nc.dram_tensor("slot_y", (SLOT_TILES * P, D), F32, kind="Internal").ap()

        qk_parts = nc.dram_tensor("qk_parts", (2, 3, 2, C1, H1 * D), BF16, kind="Internal").ap()

        x = sb("x", [P, T, D])
        xn2 = sb("xn2", [P, T, D])
        ffn_w = sb("ffn_w", [P, E * (KC * 2 * 512 + 4 * D)])
        att_w = sb("att_w", [P, 2560])
        ident = sb("ident", [P, P])
        before = sb("before", [P, P])
        ones = sb("ones", [P, P])
        cols = sb("cols", [P, sum(n for _, n in COLS)])
        rows = sb("rows", [P, sum(n for _, n in ROWS)])
        router_w = sb("router_w", [P, 4, KC, E])
        gain = sb("gain", [P, 8])
        half = sb("half", [P, 1])
        table_call = sb("table_call", [P, 1])
        logits = sb("logits", [P, T, E])
        slots = sb("slots", [P, TOP, T], U32)
        weight = sb("weight", [P, TOP, T])
        tile_expert = sb("tile_expert", [1, SLOT_TILES], I32)
        work = sb("work", [P, WORK])
        ps = ctx.enter_context(nc.psum_tensor("ps", [P, 8, 512], F32))
        used = [0]

        def carve(*shape):
            n = int(np.prod(shape))
            v = work[:, used[0]:used[0] + n]
            used[0] += n
            assert used[0] <= WORK, used
            if len(shape) == 1:
                return v
            names = "abcdef"[:len(shape)]
            return v.rearrange(f"p ({' '.join(names)}) -> p {' '.join(names)}",
                               **dict(zip(names[1:], shape[1:])))

        def place(table):
            at, o = {}, 0
            for name, n in table:
                at[name] = (o, n)
                o += n
            return at

        col_at, row_at = place(COLS), place(ROWS)

        def col(name, j=0, n=1):
            return cols[:, col_at[name][0] + j:col_at[name][0] + j + n]

        def row(name):
            o, n = row_at[name]
            return rows[:, o:o + n]

        consts_in, ffn_w_in, att_w_in = sig("consts_in", 16), sig("ffn_w_in", 16), sig("att_w_in", 16)
        zeros_out, out_done, ctx_in = sig("zeros_out", 16), sig("out_done", 16), sig("ctx_in", 16)
        slot_in = [sig(f"slot_in{u}", 16) for u in range(2)]
        slot_out = [sig(f"slot_out{u}", 16) for u in range(2)]
        y_in, scattered = sig("y_in", 16, 0), sig("scattered", 16, 0)
        ready, index_ready, held_pool, held_dve = (sig(n) for n in ("ready", "index_ready", "held_pool", "held_dve"))
        half_added, added, tile_done = (sig(n) for n in ("half_added", "added", "tile_done"))
        saved = sig("saved")

        class Norm:
            def __init__(self, name):
                self.stats, self.mean, self.var, self.rstd, self.done = (
                    sig(f"{name}_{n}") for n in ("stats", "mean", "var", "rstd", "done"))

        norm_in, norm_out, norm_mid = Norm("norm_in"), Norm("norm_out"), Norm("norm_mid")
        copied = sig("copied")
        parts_out = sig("parts_out", 16)
        stack_in = [sig(f"stack_in{b}", 16) for b in range(2)]
        q_projected, k_projected, v_projected, roped, split_step = (
            sig(n) for n in ("q_projected", "k_projected", "v_projected", "roped", "split_step"))
        v_staged, v_placed, inv_made, inv_ready, inv_out = (
            sig(n) for n in ("v_staged", "v_placed", "inv_made", "inv_ready", "inv_out"))
        probs_by_bank = [sig(f"probs_turned{a}") for a in range(2)]
        pT_out_dve, pT_out_act = sig("pT_out_dve"), sig("pT_out_act")
        turned, turned_out = sig("turned"), sig("turned_out")
        projected, projected_kv, proj_min, proj_exp, proj_out = (
            sig(n) for n in ("projected", "projected_kv", "proj_min", "proj_exp", "proj_out"))
        gate_step, masked, scored, shifted, probs = (
            sig(n) for n in ("gate_step", "masked", "scored", "shifted", "probs"))
        probs_turned, probs_out, attended, norm_step, attn_ready, out_made = (
            sig(n) for n in ("probs_turned", "probs_out", "attended", "norm_step", "attn_ready", "out_made"))
        logits_made, step = sig("logits_made"), sig("step")
        xT_made, xT_ready, up_made, silu_ready = (sig(n) for n in ("xT_made", "xT_ready", "up_made", "silu_ready"))
        h_ready, hT_made, hT_ready, y_made, y_ready = (
            sig(n) for n in ("h_ready", "hT_made", "hT_ready", "y_made", "y_ready"))

        with nc.Block() as block:
            @block.sync
            def _(sp):
                for s in signals:
                    if s.start:
                        sp.sem_inc(s.sem, s.start * s.step)

        consts = ((ident, "ident"), (before, "before"), (cols, "cols"), (rows, "rows"),
                  (router_w, "router_w"), (x, "x"))
        zeros = work[:, 0:SLOT_TILES // 3 * D]
        with nc.Block() as block:
            @block.sync
            def _(sp):
                for buf, name in consts:
                    sp.dma_start(buf[:], d[name]).then_inc(consts_in.up(), 16)
                sp.wait_ge(ready.sem, ready.at(1))
                n = SLOT_TILES // 3
                for j in range(3):
                    sp.dma_start(slot_x[j * n * P:(j + 1) * n * P].rearrange("(t p) d -> p t d", p=P),
                                 zeros.rearrange("p (t d) -> p t d", d=D)).then_inc(zeros_out.up(), 16)
                sp.wait_ge(zeros_out.sem, zeros_out.at(3))

            @block.vector
            def _(dve):
                nc.vector.memset(zeros, 0.0).then_inc(ready.up(), 1)
                nc.vector.memset(ones[:], 1.0)
                nc.vector.memset(half[:], -0.5)

            @block.scalar
            def _(act):
                act.wait_ge(consts_in.sem, consts_in.at(len(consts)))
                nc.scalar.activation(gain[:], col("g", 0, 8), ACT.Tanh)
        end_stage()

        def gather_rows(pool, i, index, y_buf):
            pool.wait_ge(tile_done.sem, tile_done.at(i))
            nc.gpsimd.tensor_copy(index, slots[:, :, bass.ds(i, 1)].rearrange("p a b -> p (a b)")
                                  ).then_inc(index_ready.up(T), 1)
            pool.wait_ge(index_ready.sem, index_ready.at(i + 1))
            pool.sem_inc(held_pool.up(T), 1)
            for a in range(TOP):
                nc.gpsimd.indirect_dma_start(
                    y_buf[:, a, :], None, slot_y,
                    bass.IndirectOffsetOnAxis(ap=index[:, a:a + 1], axis=0)).then_inc(y_in.up(T), 16)

        def add_rows(dve, i, y_buf):
            dve.wait_ge(y_in.sem, y_in.at(TOP * i + TOP))
            nc.vector.scalar_tensor_tensor(
                out=x[:, i, :], in0=y_buf[:, 0, :], scalar=weight[:, 0, bass.ds(i, 1)], in1=x[:, i, :],
                op0=ALU.mult, op1=ALU.add).then_inc(half_added.up(T), 1)
            dve.wait_ge(half_added.sem, half_added.at(i + 1))
            nc.vector.scalar_tensor_tensor(
                out=x[:, i, :], in0=y_buf[:, 1, :], scalar=weight[:, 1, bass.ds(i, 1)], in1=x[:, i, :],
                op0=ALU.mult, op1=ALU.add).then_inc(added.up(T), 1)
            dve.wait_ge(added.sem, added.at(i + 1))

        def norm_stats(dve, n, src, stats, norm, times):
            dve.sem_inc(held_dve.up(times), 1)
            nc.vector.bn_stats(stats["bn"], src).then_inc(norm.stats.up(times), 1)
            dve.wait_ge(norm.stats.sem, norm.stats.at(n + 1))
            dve.sem_inc(held_dve.up(times), 1)
            nc.vector.bn_aggr(stats["mv"], stats["bn"]).then_inc(norm.mean.up(times), 1)
            dve.wait_ge(norm.mean.sem, norm.mean.at(n + 1))
            nc.vector.tensor_scalar(stats["var"], stats["mv"][:, 1:2], LN_EPS, None, ALU.add
                                    ).then_inc(norm.var.up(times), 1)

        def norm_apply(dve, n, src, dst, stats, norm, times):
            dve.wait_ge(norm.rstd.sem, norm.rstd.at(n + 1))
            nc.vector.tensor_scalar(dst, src, stats["mv"][:, 0:1], stats["rstd"], ALU.subtract, ALU.mult
                                    ).then_inc(norm.done.up(times), 1)

        def norm_dve(dve, n, src, dst, stats, norm, times=T):
            norm_stats(dve, n, src, stats, norm, times)
            norm_apply(dve, n, src, dst, stats, norm, times)

        def norm_pool(pool, n, stats, norm, times=T):
            pool.wait_ge(norm.var.sem, norm.var.at(n + 1))
            nc.gpsimd.tensor_tensor(stats["rstd"], stats["var"], half[:], ALU.pow).then_inc(norm.rstd.up(times), 1)

        def carve_stats():
            return {"bn": carve(6), "mv": carve(2), "var": carve(1), "rstd": carve(1)}

        def turn(pe, src, bank, at=0):
            for k in range(KC):
                mm = nc.tensor.transpose(ps[:, bank, at + k * P:at + (k + 1) * P], src[:, k * P:(k + 1) * P], ident[:])
            return mm

        def save_norm(pool, i, xn, times=T):
            pool.wait_ge(norm_out.done.sem, norm_out.done.at(i + 1))
            nc.gpsimd.tensor_copy(xn2[:, i, :], xn).then_inc(saved.up(times), 1)

        def router_pe(pe, layer, i, n_turn, xn, xT):
            pe.wait_ge(norm_out.done.sem, norm_out.done.at(i + 1))
            turn(pe, xn, 0).then_inc(turned.up(T), 1)
            pe.wait_ge(turned_out.sem, turned_out.at(n_turn + 1))
            for k in range(KC):
                mm = nc.tensor.matmul(ps[:, 1, 0:E], xT[:, k, :], router_w[:, layer, k, :],
                                      start=(k == 0), stop=(k == KC - 1))
            mm.then_inc(logits_made.up(T), 1)

        def turned_act(act, n_turn, xT, n=2 * P, at=0):
            act.wait_ge(turned.sem, turned.at(n_turn + 1))
            nc.scalar.copy(xT.rearrange("p k t -> p (k t)"), ps[:, 0, at:at + n]).then_inc(turned_out.up(T), 1)

        def router_dve(dve, i):
            dve.wait_ge(logits_made.sem, logits_made.at(i + 1))
            nc.vector.tensor_copy(logits[:, i, :], ps[:, 1, 0:E]).then_inc(tile_done.up(T), 1)

        def load_ffn(sp, layer):
            m = HIDDEN[layer]
            sp.dma_start(up_view(layer), d[f"up{layer}"].rearrange("e (k p) m -> p e k m", p=P)
                         ).then_inc(ffn_w_in.up(), 16)
            for e in range(E):
                for c, n in chunks(m):
                    sp.dma_start(down_view(layer)[0:n, e, c, :], d[f"down{layer}"][e, c * P:c * P + n, :]
                                 ).then_inc(ffn_w_in.up(), 16)

        def up_view(layer):
            m = HIDDEN[layer]
            return ffn_w[:, 0:E * KC * 2 * m].rearrange("p (e k m) -> p e k m", e=E, k=KC)

        def down_view(layer):
            m = HIDDEN[layer]
            n, o = len(chunks(m)), E * KC * 2 * m
            return ffn_w[:, o:o + E * n * D].rearrange("p (e c n) -> p e c n", e=E, c=n)

        def n_ffn_dmas(layer):
            return 1 + E * len(chunks(HIDDEN[layer]))

        def attention0():
            used[0] = 0
            layer = 0
            wq = att_w[:, 0:2 * D].rearrange("p (k n) -> p k n", k=KC)
            wg = att_w[:, 2 * D:4 * D].rearrange("p (k n) -> p k n", k=KC)
            wkv = att_w[:, 4 * D:8 * D].rearrange("p (k n) -> p k n", k=KC)
            wo = att_w[:, 8 * D:10 * D].rearrange("p (k n) -> p k n", k=KC)
            stats = carve_stats()
            head_mask = carve(2 * P)
            neg_bg = carve(2)
            xn, xT = carve(D), carve(KC, P)
            cT = carve(KC, P)
            low_q, qT = carve(KC, P), carve(KC, P)
            low_k, k_map = carve(D), carve(D)
            v_ones = carve(KC, 2, P)
            e_gate = carve(KC, P)
            state = carve(2, KC, 2 * P)
            divisor, attn = carve(KC, P), carve(KC, P)
            bank_x, bank_q, bank_g, bank_k, bank_n, bank_d = 0, 2, 3, 4, 5, 3

            with nc.Block() as block:
                @block.sync
                def _(sp):
                    for buf, name in ((wq, "wq0"), (wg, "wg0"), (wkv, "wkv0"), (wo, "wo0")):
                        sp.dma_start(buf, d[name].rearrange("(k p) n -> p k n", p=P)).then_inc(att_w_in.up(), 16)
                    sp.dma_start(head_mask, d["mask0"]).then_inc(att_w_in.up(), 16)
                    load_ffn(sp, layer)
                    with sp.Fori(0, T) as i:
                        sp.wait_ge(projected.sem, projected.at(i))
                        sp.dma_start(cT, d["ctxT"][i]).then_inc(ctx_in.up(T), 16)

                @block.gpsimd
                def _(pool):
                    with pool.Fori(0, T) as i:
                        norm_pool(pool, i, stats, norm_in)
                        norm_pool(pool, i, stats, norm_out)
                        save_norm(pool, i, xn)

                @block.tensor
                def _(pe):
                    pe.wait_ge(att_w_in.sem, att_w_in.at(5))
                    pe.wait_ge(ready.sem, ready.at(2))
                    with pe.Fori(0, T) as i:
                        pe.wait_ge(norm_in.done.sem, norm_in.done.at(i + 1))
                        turn(pe, xn, 0).then_inc(turned.up(T), 1)
                        pe.wait_ge(ctx_in.sem, ctx_in.at(i + 1))
                        pe.wait_ge(turned_out.sem, turned_out.at(2 * i + 1))
                        for w, bank in ((wq, bank_q), (wg, bank_g)):
                            for g in range(KC):
                                for k in range(KC):
                                    mm = nc.tensor.matmul(ps[:, bank, g * P:(g + 1) * P], w[:, k, g * P:(g + 1) * P],
                                                          xT[:, k, :], start=(k == 0), stop=(k == KC - 1))
                        for k in range(KC):
                            mm = nc.tensor.matmul(ps[:, bank_k, :], cT[:, k, :], wkv[:, k, :],
                                                  start=(k == 0), stop=(k == KC - 1))
                        mm.then_inc(projected.up(T), 1)
                        pe.wait_ge(proj_out.sem, proj_out.at(3 * i + 3))
                        for b in range(2):
                            for g in range(KC):
                                mm = nc.tensor.matmul(
                                    ps[:, 6 + b, g * 2 * P:(g + 1) * 2 * P], k_map[b * L:(b + 1) * L, g * P:(g + 1) * P],
                                    v_ones[b * L:(b + 1) * L, g, :, :].rearrange("p a n -> p (a n)"),
                                    start=True, stop=True)
                        mm.then_inc(scored.up(T), 1)
                        pe.wait_ge(masked.sem, masked.at(i + 1))
                        for b in range(2):
                            for g in range(KC):
                                for a, bank in ((0, bank_n), (1, bank_q)):
                                    mm = nc.tensor.matmul(
                                        ps[:, bank, g * P + b * L:g * P + (b + 1) * L],
                                        state[:, b, g, a * P:(a + 1) * P], qT[:, g, b * L:(b + 1) * L],
                                        start=True, stop=True)
                        mm.then_inc(attended.up(T), 1)
                        pe.wait_ge(attn_ready.sem, attn_ready.at(i + 1))
                        for g in range(KC):
                            mm = nc.tensor.matmul(ps[:, bank_k, 0:D], attn[:, g, :], wo[:, g, :],
                                                  start=(g == 0), stop=(g == KC - 1))
                        mm.then_inc(out_made.up(T), 1)
                        router_pe(pe, layer, i, 2 * i + 1, xn, xT)

                @block.scalar
                def _(act):
                    nc.scalar.activation(table_call[:], half[:], ACT.Exp)
                    act.wait_ge(ready.sem, ready.at(2))
                    with act.Fori(0, T) as i:
                        act.wait_ge(turned.sem, turned.at(2 * i + 1))
                        nc.scalar.copy(xT.rearrange("p k t -> p (k t)"), ps[:, 0, 0:2 * P]).then_inc(turned_out.up(T), 1)
                        act.wait_ge(projected.sem, projected.at(i + 1))
                        for g in range(KC):
                            nc.scalar.activation(e_gate[:, g, :], ps[:, bank_g, g * P:(g + 1) * P], ACT.Exp,
                                                 bias=neg_bg[:, g:g + 1], scale=-1.0).then_inc(gate_step.up(T), 1)
                        act.wait_ge(proj_min.sem, proj_min.at(2 * i + 1))
                        nc.scalar.activation(low_q, low_q, ACT.Exp).then_inc(proj_exp.up(T), 1)
                        act.wait_ge(proj_min.sem, proj_min.at(2 * i + 2))
                        nc.scalar.activation(low_k, low_k, ACT.Exp).then_inc(proj_exp.up(T), 1)
                        turned_act(act, 2 * i + 1, xT)

                @block.vector
                def _(dve):
                    nc.vector.tensor_scalar(neg_bg, col("bg", 0, 2), -1.0, None, ALU.mult).then_inc(ready.up(), 1)
                    nc.vector.memset(v_ones[:, :, 1, :], 1.0).then_inc(ready.up(), 1)
                    dve.wait_ge(att_w_in.sem, att_w_in.at(5))
                    with dve.Fori(0, T) as i:
                        dve.wait_ge(saved.sem, saved.at(i))
                        norm_dve(dve, i, x[:, i, :], xn, stats, norm_in)
                        dve.wait_ge(projected.sem, projected.at(i + 1))
                        dve.wait_ge(gate_step.sem, gate_step.at(2 * i + 2))
                        nc.vector.tensor_scalar(low_q.rearrange("p k t -> p (k t)"), ps[:, bank_q, 0:2 * P], 0.0, None,
                                                ALU.min).then_inc(proj_min.up(T), 1)
                        nc.vector.tensor_scalar(low_k, ps[:, bank_k, 0:D], 0.0, None, ALU.min).then_inc(proj_min.up(T), 1)
                        nc.vector.tensor_copy(v_ones[:, :, 0, :], ps[:, bank_k, D:2 * D].rearrange("p (g n) -> p g n", g=KC)
                                              ).then_inc(proj_out.up(T), 1)
                        dve.wait_ge(proj_exp.sem, proj_exp.at(2 * i + 1))
                        nc.vector.scalar_tensor_tensor(
                            out=qT.rearrange("p k t -> p (k t)"), in0=ps[:, bank_q, 0:2 * P], scalar=1.0,
                            in1=low_q.rearrange("p k t -> p (k t)"), op0=ALU.add, op1=ALU.max).then_inc(proj_out.up(T), 1)
                        dve.wait_ge(proj_exp.sem, proj_exp.at(2 * i + 2))
                        nc.vector.scalar_tensor_tensor(
                            out=k_map, in0=ps[:, bank_k, 0:D], scalar=1.0, in1=low_k,
                            op0=ALU.add, op1=ALU.max).then_inc(proj_out.up(T), 1)
                        dve.wait_ge(scored.sem, scored.at(i + 1))
                        nc.vector.tensor_tensor(
                            state.rearrange("p b g n -> p (b g) n"), ps[:, 6:8, :].rearrange("p b (g n) -> p (b g) n", g=KC),
                            head_mask.unsqueeze(1).to_broadcast([P, 2 * KC, 2 * P]), ALU.mult).then_inc(masked.up(T), 1)
                        dve.wait_ge(attended.sem, attended.at(i + 1))
                        nc.vector.tensor_scalar(e_gate, e_gate, 1.0, None, ALU.add).then_inc(norm_step.up(T), 1)
                        dve.wait_ge(norm_step.sem, norm_step.at(3 * i + 1))
                        nc.vector.scalar_tensor_tensor(
                            out=divisor.rearrange("p k t -> p (k t)"), in0=ps[:, bank_q, 0:2 * P], scalar=LIN_EPS,
                            in1=e_gate.rearrange("p k t -> p (k t)"), op0=ALU.add, op1=ALU.mult).then_inc(norm_step.up(T), 1)
                        dve.wait_ge(norm_step.sem, norm_step.at(3 * i + 2))
                        nc.vector.reciprocal(divisor, divisor).then_inc(norm_step.up(T), 1)
                        dve.wait_ge(norm_step.sem, norm_step.at(3 * i + 3))
                        nc.vector.tensor_tensor(attn.rearrange("p k t -> p (k t)"), ps[:, bank_n, 0:2 * P],
                                                divisor.rearrange("p k t -> p (k t)"), ALU.mult).then_inc(attn_ready.up(T), 1)
                        dve.wait_ge(out_made.sem, out_made.at(i + 1))
                        nc.vector.scalar_tensor_tensor(
                            out=x[:, i, :], in0=ps[:, bank_k, 0:D], scalar=gain[:, layer:layer + 1], in1=x[:, i, :],
                            op0=ALU.mult, op1=ALU.add).then_inc(added.up(T), 1)
                        dve.wait_ge(added.sem, added.at(i + 1))
                        norm_dve(dve, i, x[:, i, :], xn, stats, norm_out)
                        router_dve(dve, i)
            end_stage()

        def attention1():
            used[0] = 0
            layer = 1
            HH = H1 // 2
            UNITS, PAIRS = 8, 4
            names = ("wq1", "wq1_turned", "wk1", "wk1_turned", "wv1")
            wq, wq_turned, wk, wk_turned, wv = (att_w[:, j * P:(j + 1) * P] for j in range(5))
            wo = att_w[:, 5 * P:9 * P].rearrange("p (a b n) -> p a b n", a=2, b=2)
            v_pad = att_w[:, 9 * P:17 * P].rearrange("p (b h s c) -> p b h s c", b=2, h=H1, s=2)
            stats_in, stats_out = carve_stats(), carve_stats()
            index, y_buf = carve(TOP).bitcast(U32), carve(TOP, D)
            xn, ctx_t = carve(D), carve(D)
            xo, xT = carve(D), carve(KC, P)
            rope_a, rope_b = carve(2, D), carve(2, D)
            whole, rest = carve(2, D), carve(2, D)
            parts = carve(2 * 3 * D // 2).bitcast(BF16).rearrange("p (s r t) -> p s r t", s=2, r=3)
            q_stack = carve(H1 * D // 2).bitcast(BF16).rearrange("p (h t) -> p h t", h=H1)
            k_stack = carve(H1 * D // 2).bitcast(BF16).rearrange("p (h t) -> p h t", h=H1)
            v = carve(2, P)
            neg_max, sums, inv = carve(2, HH), carve(2, HH), carve(2, HH)
            inv_wide = carve(2, HH, 32)
            inv_T = carve(D)
            p = carve(2, HH, 2, P)
            pT = carve(2, HH, 2, D)
            attn = carve(2, 2, D)
            tmp = carve(D)
            TURNED, PV, MISC = 4, 6, 7
            BODIES = T - 3

            def over_tiles(eng, body):
                body(0, 1, tail=False, qkv=True, norm=True)
                with eng.Fori(1, T - 2) as i:
                    body(i, BODIES, tail=True, qkv=True, norm=True)
                body(T - 2, 1, tail=True, qkv=True, norm=False)
                body(T - 1, 1, tail=True, qkv=False, norm=False)

            with nc.Block() as block:
                @block.sync
                def _(sp):
                    def load_ctx(j, times):
                        sp.wait_ge(v_projected.sem, v_projected.at(j))
                        sp.dma_start(ctx_t, d["ctx"][j]).then_inc(ctx_in.up(times), 16)

                    def stack(j, times):
                        sp.wait_ge(split_step.sem, split_step.at(10 * j + 10))
                        if not isinstance(j, int) or j > 0:
                            for b in range(2):
                                sp.wait_ge(stack_in[b].sem, stack_in[b].at(6 * j))
                        sp.dma_start(qk_parts.rearrange("s r b c (h t) -> (b c h) s r t", h=H1), parts
                                     ).then_inc(parts_out.up(times), 16)
                        sp.wait_ge(parts_out.sem, parts_out.at(j + 1))
                        for b in range(2):
                            sp.wait_ge(scored.sem, scored.at(UNITS * (j - 1) + 4 * b + 4))
                            o = 64 * b
                            q_of, k_of = qk_parts[0, :, b], qk_parts[1, :, b]
                            for r, (row0, copies) in enumerate(((0, 3), (24, 3), (48, 2))):
                                sp.dma_start(q_stack[o + row0:o + row0 + 8 * copies].rearrange("p h t -> p (h t)"),
                                             q_of[r].unsqueeze(0).to_broadcast([copies, C1, H1 * D])
                                             ).then_inc(stack_in[b].up(times), 16)
                            for o_k in (o, o + 24):
                                sp.dma_start(k_stack[o_k:o_k + 24].rearrange("p h t -> p (h t)"), k_of
                                             ).then_inc(stack_in[b].up(times), 16)
                            sp.dma_start(k_stack[o + 48:o + 64].rearrange("p h t -> p (h t)"), k_of[0:2]
                                         ).then_inc(stack_in[b].up(times), 16)

                    for j, name in enumerate(names):
                        sp.dma_start(att_w[:, j * P:(j + 1) * P], d[name]).then_inc(att_w_in.up(), 16)
                    sp.dma_start(wo, d["wo1"]).then_inc(att_w_in.up(), 16)
                    load_ctx(0, 1)
                    load_ctx(1, 1)
                    stack(0, 1)
                    load_ffn(sp, layer)

                    def body(i, times, tail, qkv, norm):
                        if norm:
                            load_ctx(i + 2, times)
                        if qkv:
                            stack(i + 1, times)

                    over_tiles(sp, body)

                @block.gpsimd
                def _(pool):
                    def fetch(j, times):
                        pool.wait_ge(added.sem, added.at(j))
                        nc.gpsimd.tensor_copy(index, slots[:, :, bass.ds(j, 1)].rearrange("p a b -> p (a b)")
                                              ).then_inc(index_ready.up(times), 1)
                        pool.wait_ge(index_ready.sem, index_ready.at(j + 1))
                        pool.sem_inc(held_pool.up(times), 1)
                        for a in range(TOP):
                            nc.gpsimd.indirect_dma_start(
                                y_buf[:, a, :], None, slot_y,
                                bass.IndirectOffsetOnAxis(ap=index[:, a:a + 1], axis=0)).then_inc(y_in.up(times), 16)

                    def split(j, s, times):
                        n = 10 * j + 5 * s
                        pool.wait_ge(roped.sem, roped.at(2 * j + s + 1))
                        nc.gpsimd.tensor_tensor(whole[:, s], rope_a[:, s], rope_b[:, s], ALU.add
                                                ).then_inc(split_step.up(times), 1)
                        pool.wait_ge(parts_out.sem, parts_out.at(j))
                        nc.gpsimd.tensor_tensor(parts[:, s, 0, :], rope_a[:, s], rope_b[:, s], ALU.add
                                                ).then_inc(split_step.up(times), 1)
                        pool.wait_ge(split_step.sem, split_step.at(n + 2))
                        nc.gpsimd.tensor_tensor(rest[:, s], whole[:, s], parts[:, s, 0, :], ALU.subtract
                                                ).then_inc(split_step.up(times), 1)
                        pool.wait_ge(split_step.sem, split_step.at(n + 3))
                        pool.sem_inc(held_pool.up(times), 1)
                        nc.gpsimd.tensor_copy(parts[:, s, 1, :], rest[:, s]).then_inc(split_step.up(times), 1)
                        pool.wait_ge(split_step.sem, split_step.at(n + 4))
                        nc.gpsimd.tensor_tensor(parts[:, s, 2, :], rest[:, s], parts[:, s, 1, :], ALU.subtract
                                                ).then_inc(split_step.up(times), 1)

                    def place_v(j, b, times):
                        pool.wait_ge(v_staged.sem, v_staged.at(j + 1))
                        pool.wait_ge(attended.sem, attended.at(PAIRS * (j - 1) + 2 * b + 2))
                        pool.sem_inc(held_pool.up(times), 1)
                        for sc in range(2):
                            last = nc.gpsimd.tensor_copy(v_pad[:, b, :, sc, 0:C1],
                                                         v[:, sc, 64 * b:64 * b + 64].rearrange("p (h c) -> p h c", h=H1))
                        last.then_inc(v_placed.up(times), 1)

                    nc.gpsimd.memset(v_pad, 0.0).then_inc(ready.up(), 1)
                    pool.wait_ge(ready.sem, ready.at(1))
                    fetch(0, 1)
                    norm_pool(pool, 0, stats_in, norm_in, 1)
                    fetch(1, 1)
                    split(0, 0, 1)
                    split(0, 1, 1)
                    place_v(0, 0, 1)
                    norm_pool(pool, 1, stats_in, norm_in, 1)

                    def body(i, times, tail, qkv, norm):
                        place_v(i, 1, times)
                        if norm:
                            fetch(i + 2, times)
                        if qkv:
                            split(i + 1, 0, times)
                            split(i + 1, 1, times)
                        if tail:
                            norm_pool(pool, i - 1, stats_out, norm_out, times)
                            save_norm(pool, i - 1, xo, times)
                        if qkv:
                            place_v(i + 1, 0, times)
                        if norm:
                            norm_pool(pool, i + 2, stats_in, norm_in, times)

                    over_tiles(pool, body)
                    norm_pool(pool, T - 1, stats_out, norm_out, 1)
                    save_norm(pool, T - 1, xo, 1)

                @block.tensor
                def _(pe):
                    def project_q(j, times):
                        pe.wait_ge(norm_in.done.sem, norm_in.done.at(j + 1))
                        if not isinstance(j, int) or j > 2:
                            pe.wait_ge(tile_done.sem, tile_done.at(j - 2))
                        nc.tensor.matmul(ps[:, MISC, 0:D], wq, xn, start=True, stop=True)
                        nc.tensor.matmul(ps[:, MISC, D:2 * D], wq_turned, xn, start=True, stop=True
                                         ).then_inc(q_projected.up(times), 1)

                    def project_k(j, times):
                        pe.wait_ge(ctx_in.sem, ctx_in.at(j + 1))
                        pe.wait_ge(roped.sem, roped.at(2 * j + 1))
                        nc.tensor.matmul(ps[:, MISC, 0:D], wk, ctx_t, start=True, stop=True)
                        nc.tensor.matmul(ps[:, MISC, D:2 * D], wk_turned, ctx_t, start=True, stop=True
                                         ).then_inc(k_projected.up(times), 1)

                    def project_v(j, times):
                        pe.wait_ge(roped.sem, roped.at(2 * j + 2))
                        for c in range(2):
                            mm = nc.tensor.matmul(ps[:, MISC, c * P:(c + 1) * P], ctx_t[:, c * P:(c + 1) * P], wv,
                                                  start=True, stop=True)
                        mm.then_inc(v_projected.up(times), 1)

                    def score(i, n, times):
                        b, half_of, c, N = n // 4, (n // 2) % 2, n % 2, UNITS * i + n
                        pe.wait_ge(stack_in[b].sem, stack_in[b].at(6 * i + 6))
                        pe.wait_ge(probs.sem, probs.at(N - 1))
                        for j in range(HH):
                            h = HH * half_of + j
                            mm = nc.tensor.matmul(ps[:, 2 * (n % 2) + j // 2, (j % 2) * D:(j % 2 + 1) * D],
                                                  q_stack[64 * b:64 * b + 64, h, c * P:(c + 1) * P],
                                                  k_stack[64 * b:64 * b + 64, h, :], start=True, stop=True)
                        mm.then_inc(scored.up(times), 1)

                    def turn_probs(i, n, times):
                        N = UNITS * i + n
                        pe.wait_ge(probs.sem, probs.at(N + 1))
                        for a, out_of in ((0, pT_out_dve), (1, pT_out_act)):
                            pe.wait_ge(out_of.sem, out_of.at(N))
                            for j in (2 * a, 2 * a + 1):
                                for sc in range(2):
                                    o = (2 * (j % 2) + sc) * P
                                    mm = nc.tensor.transpose(ps[:, TURNED + a, o:o + P], p[:, n % 2, j, sc, :], ident[:])
                            mm.then_inc(probs_by_bank[a].up(times), 1)

                    def attend(i, pair, times):
                        m, b, half_of = PAIRS * i + pair, pair // 2, pair % 2
                        pe.wait_ge(inv_ready.sem, inv_ready.at(2 * m + 2))
                        pe.wait_ge(attn_ready.sem, attn_ready.at(m))
                        for c in range(2):
                            nc.tensor.transpose(ps[:, PV, D + c * P:D + (c + 1) * P],
                                                inv_wide[:, c].rearrange("p h c -> p (h c)"), ident[:])
                        pe.wait_ge(pT_out_dve.sem, pT_out_dve.at(2 * m + 2))
                        pe.wait_ge(pT_out_act.sem, pT_out_act.at(2 * m + 2))
                        pe.wait_ge(v_placed.sem, v_placed.at(2 * i + b + 1))
                        for sc in range(2):
                            for j in range(HH):
                                mm = nc.tensor.matmul(ps[32 * j:32 * j + 32, PV, 0:D], v_pad[:, b, HH * half_of + j, sc, :],
                                                      pT[:, pair % 2, j, sc, :], start=(sc == 0), stop=(sc == 1),
                                                      skip_group_check=True)
                        mm.then_inc(attended.up(times), 1)

                    def project_out(i, times):
                        pe.wait_ge(attn_ready.sem, attn_ready.at(PAIRS * i + PAIRS))
                        pe.wait_ge(tile_done.sem, tile_done.at(i))
                        pe.wait_ge(v_staged.sem, v_staged.at(min(i + 3, T) if isinstance(i, int) else i + 3))
                        for n, (a, b) in enumerate(((0, 0), (1, 0), (0, 1), (1, 1))):
                            mm = nc.tensor.matmul(ps[:, MISC, 0:D], wo[:, a, b, :], attn[:, a, b, :],
                                                  start=(n == 0), stop=(n == 3))
                        mm.then_inc(out_made.up(times), 1)

                    def turn_out(i, times):
                        pe.wait_ge(norm_out.done.sem, norm_out.done.at(i + 1))
                        turn(pe, xo, MISC).then_inc(turned.up(times), 1)

                    def route_out(i, times):
                        pe.wait_ge(turned_out.sem, turned_out.at(i + 1))
                        for k in range(KC):
                            mm = nc.tensor.matmul(ps[:, MISC, 0:E], xT[:, k, :], router_w[:, layer, k, :],
                                                  start=(k == 0), stop=(k == KC - 1))
                        mm.then_inc(logits_made.up(times), 1)

                    pe.wait_ge(att_w_in.sem, att_w_in.at(6))
                    project_q(0, 1)
                    project_k(0, 1)
                    project_v(0, 1)
                    score(0, 0, 1)

                    def body(i, times, tail, qkv, norm):
                        for n in range(UNITS):
                            if n < UNITS - 1:
                                score(i, n + 1, times)
                            elif qkv:
                                score(i + 1, 0, times)
                            turn_probs(i, n, times)
                            if n == 0 and tail:
                                attend(i - 1, PAIRS - 1, times)
                            elif n and n % 2 == 0:
                                attend(i, n // 2 - 1, times)
                            if qkv and n == 0:
                                project_q(i + 1, times)
                            if qkv and n == 1:
                                project_k(i + 1, times)
                            if qkv and n == 2:
                                project_v(i + 1, times)
                            if tail and n == 3:
                                project_out(i - 1, times)
                            if tail and n == 5:
                                turn_out(i - 1, times)
                            if tail and n == 6:
                                route_out(i - 1, times)

                    over_tiles(pe, body)
                    attend(T - 1, PAIRS - 1, 1)
                    project_out(T - 1, 1)
                    turn_out(T - 1, 1)
                    route_out(T - 1, 1)

                @block.scalar
                def _(act):
                    def exps(i, n, times):
                        N = UNITS * i + n
                        act.wait_ge(shifted.sem, shifted.at(N + 1))
                        act.wait_ge(probs_by_bank[1].sem, probs_by_bank[1].at(N - 1))
                        act.wait_ge(inv_ready.sem, inv_ready.at(N - 1))
                        for j in range(HH):
                            last = nc.scalar.activation(
                                p[:, n % 2, j].rearrange("p s n -> p (s n)"),
                                ps[:, 2 * (n % 2) + j // 2, (j % 2) * D:(j % 2 + 1) * D], ACT.Exp,
                                bias=neg_max[:, n % 2, j:j + 1], accum_out=sums[:, n % 2, j:j + 1])
                        last.then_inc(probs.up(times), 1)

                    def take_turned(i, n, times):
                        N, m, c = UNITS * i + n, PAIRS * i + n // 2, n % 2
                        act.wait_ge(probs_by_bank[1].sem, probs_by_bank[1].at(N + 1))
                        act.wait_ge(attended.sem, attended.at(m - 1))
                        nc.scalar.copy(pT[:, (n // 2) % 2, 2:4, :, c * P:(c + 1) * P].rearrange("p h s n -> p (h s) n"),
                                       ps[:, TURNED + 1, :].rearrange("p (j n) -> p j n", n=P)
                                       ).then_inc(pT_out_act.up(times), 1)

                    def take_inv(i, pair, times):
                        m = PAIRS * i + pair
                        act.wait_ge(attended.sem, attended.at(m + 1))
                        nc.scalar.copy(inv_T, ps[:, PV, D:2 * D]).then_inc(inv_out.up(times), 1)

                    def take_turned_out(i, times):
                        act.wait_ge(turned.sem, turned.at(i + 1))
                        act.wait_ge(logits_made.sem, logits_made.at(i))
                        nc.scalar.copy(xT.rearrange("p k t -> p (k t)"), ps[:, MISC, 0:2 * P]
                                       ).then_inc(turned_out.up(times), 1)

                    nc.scalar.activation(table_call[:], half[:], ACT.Exp)
                    exps(0, 0, 1)

                    def body(i, times, tail, qkv, norm):
                        for n in range(UNITS):
                            if n < UNITS - 1:
                                exps(i, n + 1, times)
                            elif qkv:
                                exps(i + 1, 0, times)
                            take_turned(i, n, times)
                            if n == 0 and tail:
                                take_inv(i - 1, PAIRS - 1, times)
                            elif n and n % 2 == 0:
                                take_inv(i, n // 2 - 1, times)
                            if tail and n == 5:
                                take_turned_out(i - 1, times)

                    over_tiles(act, body)
                    take_inv(T - 1, PAIRS - 1, 1)
                    take_turned_out(T - 1, 1)

                @block.vector
                def _(dve):
                    def enter(j, times):
                        dve.wait_ge(y_in.sem, y_in.at(TOP * j + TOP))
                        nc.vector.scalar_tensor_tensor(
                            out=x[:, j, :], in0=y_buf[:, 0, :], scalar=weight[:, 0, bass.ds(j, 1)], in1=x[:, j, :],
                            op0=ALU.mult, op1=ALU.add).then_inc(half_added.up(times), 1)
                        dve.wait_ge(half_added.sem, half_added.at(j + 1))
                        nc.vector.scalar_tensor_tensor(
                            out=x[:, j, :], in0=y_buf[:, 1, :], scalar=weight[:, 1, bass.ds(j, 1)], in1=x[:, j, :],
                            op0=ALU.mult, op1=ALU.add).then_inc(added.up(times), 1)
                        dve.wait_ge(added.sem, added.at(j + 1))
                        norm_stats(dve, j, x[:, j, :], stats_in, norm_in, times)

                    def enter_apply(j, times):
                        dve.wait_ge(q_projected.sem, q_projected.at(j))
                        norm_apply(dve, j, x[:, j, :], xn, stats_in, norm_in, times)

                    def rope(j, s, times):
                        made = (q_projected, k_projected)[s]
                        b_name, c_name, s_name = (("bq", "cos_q", "sin_q"), ("bk", "cos_k", "sin_k"))[s]
                        dve.wait_ge(made.sem, made.at(j + 1))
                        if not isinstance(j, int) or j > 0:
                            dve.wait_ge(split_step.sem, split_step.at(10 * (j - 1) + 5 * s + 2))
                        nc.vector.scalar_tensor_tensor(out=rope_a[:, s], in0=ps[:, MISC, 0:D], scalar=col(b_name, 0),
                                                       in1=row(c_name), op0=ALU.add, op1=ALU.mult)
                        nc.vector.scalar_tensor_tensor(out=rope_b[:, s], in0=ps[:, MISC, D:2 * D], scalar=col(b_name, 1),
                                                       in1=row(s_name), op0=ALU.add, op1=ALU.mult
                                                       ).then_inc(roped.up(times), 1)

                    def stage_v(j, times):
                        dve.wait_ge(v_projected.sem, v_projected.at(j + 1))
                        dve.wait_ge(v_placed.sem, v_placed.at(2 * j))
                        nc.vector.tensor_tensor(v, ps[:, MISC, 0:2 * P].rearrange("p (s n) -> p s n", s=2),
                                                row("bv").unsqueeze(1).to_broadcast([P, 2, P]), ALU.add
                                                ).then_inc(v_staged.up(times), 1)

                    def find_max(i, n, times):
                        N = UNITS * i + n
                        dve.wait_ge(scored.sem, scored.at(N + 1))
                        b0 = 2 * (n % 2)
                        nc.vector.tensor_reduce(neg_max[:, n % 2], ps[:, b0:b0 + 2, :].rearrange("p a (h s) -> p (a h) s", h=2),
                                                AX.X, ALU.max, negate=True).then_inc(shifted.up(times), 1)

                    def invert(i, n, times):
                        N, m, c = UNITS * i + n, PAIRS * i + n // 2, n % 2
                        dve.wait_ge(probs.sem, probs.at(N + 1))
                        nc.vector.reciprocal(inv[:, c], sums[:, c]).then_inc(inv_made.up(times), 1)
                        dve.wait_ge(inv_made.sem, inv_made.at(N + 1))
                        dve.wait_ge(attended.sem, attended.at(m))
                        nc.vector.tensor_copy(inv_wide[:, c], inv[:, c].unsqueeze(2).to_broadcast([P, HH, 32])
                                              ).then_inc(inv_ready.up(times), 1)

                    def take_turned(i, n, times):
                        N, m, c = UNITS * i + n, PAIRS * i + n // 2, n % 2
                        dve.wait_ge(probs_by_bank[0].sem, probs_by_bank[0].at(N + 1))
                        dve.wait_ge(attended.sem, attended.at(m - 1))
                        nc.vector.tensor_copy(pT[:, (n // 2) % 2, 0:2, :, c * P:(c + 1) * P].rearrange("p h s n -> p (h s) n"),
                                              ps[:, TURNED, :].rearrange("p (j n) -> p j n", n=P)
                                              ).then_inc(pT_out_dve.up(times), 1)

                    def normalise(i, pair, times):
                        m = PAIRS * i + pair
                        dve.wait_ge(inv_out.sem, inv_out.at(m + 1))
                        dve.wait_ge(out_made.sem, out_made.at(i))
                        nc.vector.tensor_tensor(attn[:, pair % 2, pair // 2], ps[:, PV, 0:D], inv_T, ALU.mult
                                                ).then_inc(attn_ready.up(times), 1)

                    def leave(i, times):
                        dve.wait_ge(out_made.sem, out_made.at(i + 1))
                        nc.vector.tensor_scalar(tmp, ps[:, MISC, 0:D], col("bo"), gain[:, layer:layer + 1],
                                                ALU.add, ALU.mult).then_inc(gate_step.up(times), 1)
                        dve.wait_ge(gate_step.sem, gate_step.at(i + 1))
                        nc.vector.tensor_tensor(x[:, i, :], x[:, i, :], tmp, ALU.add).then_inc(proj_exp.up(times), 1)
                        dve.wait_ge(proj_exp.sem, proj_exp.at(i + 1))
                        norm_stats(dve, i, x[:, i, :], stats_out, norm_out, times)

                    def leave_apply(i, times):
                        dve.wait_ge(saved.sem, saved.at(i))
                        dve.wait_ge(turned.sem, turned.at(i))
                        norm_apply(dve, i, x[:, i, :], xo, stats_out, norm_out, times)

                    def take_logits(i, times):
                        dve.wait_ge(logits_made.sem, logits_made.at(i + 1))
                        nc.vector.tensor_copy(logits[:, i, :], ps[:, MISC, 0:E]).then_inc(tile_done.up(times), 1)

                    enter(0, 1)
                    enter_apply(0, 1)
                    rope(0, 0, 1)
                    rope(0, 1, 1)
                    stage_v(0, 1)
                    enter(1, 1)
                    enter_apply(1, 1)
                    find_max(0, 0, 1)

                    def body(i, times, tail, qkv, norm):
                        for n in range(UNITS):
                            if n < UNITS - 1:
                                find_max(i, n + 1, times)
                            elif qkv:
                                find_max(i + 1, 0, times)
                            invert(i, n, times)
                            take_turned(i, n, times)
                            if qkv and n == 3:
                                stage_v(i + 1, times)
                            if n == 1 and tail:
                                normalise(i - 1, PAIRS - 1, times)
                            elif n % 2 == 1 and n > 1:
                                normalise(i, (n - 3) // 2, times)
                            if qkv and n == 1:
                                rope(i + 1, 0, times)
                            if qkv and n == 2:
                                rope(i + 1, 1, times)
                            if tail and n == 4:
                                leave(i - 1, times)
                            if tail and n == 5:
                                leave_apply(i - 1, times)
                            if norm and n == 6:
                                enter(i + 2, times)
                            if norm and n == 7:
                                enter_apply(i + 2, times)
                            if tail and n == 7:
                                take_logits(i - 1, times)

                    over_tiles(dve, body)
                    normalise(T - 1, PAIRS - 1, 1)
                    leave(T - 1, 1)
                    leave_apply(T - 1, 1)
                    take_logits(T - 1, 1)
            end_stage()

        def attention2():
            used[0] = 0
            layer = 2
            w_in = att_w[:, 0:2 * D].rearrange("p (k n) -> p k n", k=KC)
            w_out = att_w[:, 2 * D:4 * D].rearrange("p (k n) -> p k n", k=KC)
            pick = att_w[:, 4 * D:4 * D + L]
            stats = carve_stats()
            index, y_buf = carve(TOP).bitcast(U32), carve(TOP, D)
            xn, xT, ctx_t = carve(D), carve(KC, P), carve(D)
            keep = carve(1)
            geo, geo_in = carve(L), carve(L)
            decay_sum, total = carve(1), carve(1)
            by_batch = carve(2)
            bias = carve(KC)
            ctx_sum = carve(KC, B)
            state = carve(KC, B)
            state_tok = carve(KC, 2, L)
            y2, tmp = carve(D), carve(D)
            n = [0]

            with nc.Block() as block:
                @block.sync
                def _(sp):
                    for buf, name in ((w_in, "w_in2"), (w_out, "w_out2")):
                        sp.dma_start(buf, d[name].rearrange("(k p) n -> p k n", p=P)).then_inc(att_w_in.up(), 16)
                    sp.dma_start(pick, d["pick"]).then_inc(att_w_in.up(), 16)
                    load_ffn(sp, layer)
                    with sp.Fori(0, T) as i:
                        sp.wait_ge(scored.sem, scored.at(i))
                        sp.dma_start(ctx_t, d["ctx"][i]).then_inc(ctx_in.up(T), 16)

                @block.gpsimd
                def _(pool):
                    with pool.Fori(0, T) as i:
                        gather_rows(pool, i, index, y_buf)
                        norm_pool(pool, i, stats, norm_in)
                        norm_pool(pool, i, stats, norm_mid)
                        norm_pool(pool, i, stats, norm_out)
                        save_norm(pool, i, xn)

                @block.tensor
                def _(pe):
                    pe.wait_ge(att_w_in.sem, att_w_in.at(3))
                    pe.wait_ge(masked.sem, masked.at(1))
                    with pe.Fori(0, T) as i:
                        pe.wait_ge(ctx_in.sem, ctx_in.at(i + 1))
                        for k in range(KC):
                            mm = nc.tensor.matmul(ps[:, 2 + k, bass.ds(2 * i, 2)], ctx_t[:, k * P:(k + 1) * P], by_batch,
                                                  start=True, stop=True)
                        mm.then_inc(scored.up(T), 1)
                    pe.wait_ge(shifted.sem, shifted.at(1))
                    for g in range(KC):
                        for k in range(KC):
                            mm = nc.tensor.matmul(ps[:, 4, g * B:(g + 1) * B], w_in[:, k, g * P:(g + 1) * P],
                                                  ctx_sum[:, k, :], start=(k == 0), stop=(k == KC - 1))
                    mm.then_inc(projected.up(), 1)
                    with pe.Fori(0, T) as i:
                        pe.wait_ge(attn_ready.sem, attn_ready.at(i + 1))
                        for k in range(KC):
                            mm = nc.tensor.matmul(ps[:, 5, 0:D], state_tok[:, k].rearrange("p b l -> p (b l)"),
                                                  w_out[:, k, :], start=(k == 0), stop=(k == KC - 1))
                        mm.then_inc(out_made.up(T), 1)
                        router_pe(pe, layer, i, i, xn, xT)

                @block.scalar
                def _(act):
                    nc.scalar.activation(keep, col("decay"), ACT.Exp, scale=-1.0).then_inc(probs.up(), 1)
                    with act.Fori(0, T) as i:
                        turned_act(act, i, xT)

                @block.vector
                def _(dve):
                    def then(ins):
                        n[0] += 1
                        ins.then_inc(step.up(), 1)
                        dve.wait_ge(step.sem, step.at(n[0]))

                    dve.wait_ge(probs.sem, probs.at(1))
                    dve.wait_ge(att_w_in.sem, att_w_in.at(3))
                    then(nc.vector.tensor_scalar(keep, keep, 1.0, None, ALU.add))
                    then(nc.vector.reciprocal(keep, keep))
                    then(nc.vector.tensor_copy(geo_in, keep.to_broadcast([P, L])))
                    then(nc.vector.tensor_tensor_scan(geo, geo_in, ones[:, 0:L], 0.0, ALU.mult, ALU.add))
                    then(nc.vector.tensor_reduce(total, geo, AX.X, ALU.add))
                    then(nc.vector.tensor_tensor(geo_in, geo, pick, ALU.mult))
                    then(nc.vector.tensor_reduce(decay_sum, geo_in, AX.X, ALU.add))
                    nc.vector.tensor_scalar(by_batch, col("batch_of", 0, 2), decay_sum, None, ALU.mult
                                            ).then_inc(masked.up(), 1)
                    then(nc.vector.tensor_scalar(bias, col("b_in", 0, 2), total, None, ALU.mult))
                    dve.wait_ge(scored.sem, scored.at(T))
                    nc.vector.tensor_copy(ctx_sum, ps[:, 2:4, 0:B]).then_inc(shifted.up(), 1)
                    dve.wait_ge(projected.sem, projected.at(1))
                    for k in range(KC):
                        last = nc.vector.tensor_scalar(state[:, k, :], ps[:, 4, k * B:(k + 1) * B], bias[:, k:k + 1], 1.0 / L,
                                                       ALU.add, ALU.mult)
                    then(last)
                    with dve.Fori(0, T) as i:
                        dve.wait_ge(saved.sem, saved.at(i))
                        nc.vector.tensor_copy(
                            state_tok, state[:, :, bass.ds(2 * i, 2)].unsqueeze(3).to_broadcast([P, KC, 2, L])
                        ).then_inc(attn_ready.up(T), 1)
                        add_rows(dve, i, y_buf)
                        norm_dve(dve, i, x[:, i, :], xn, stats, norm_in)
                        dve.wait_ge(norm_in.done.sem, norm_in.done.at(i + 1))
                        nc.vector.tensor_tensor(y2, xn, row("b_out"), ALU.add).then_inc(gate_step.up(T), 1)
                        dve.wait_ge(gate_step.sem, gate_step.at(4 * i + 1))
                        dve.wait_ge(out_made.sem, out_made.at(i + 1))
                        nc.vector.tensor_tensor(y2, y2, ps[:, 5, 0:D], ALU.add).then_inc(gate_step.up(T), 1)
                        dve.wait_ge(gate_step.sem, gate_step.at(4 * i + 2))
                        norm_dve(dve, i, y2, tmp, stats, norm_mid)
                        dve.wait_ge(norm_mid.done.sem, norm_mid.done.at(i + 1))
                        nc.vector.tensor_tensor(tmp, tmp, row("gamma"), ALU.mult).then_inc(gate_step.up(T), 1)
                        dve.wait_ge(gate_step.sem, gate_step.at(4 * i + 3))
                        nc.vector.tensor_tensor(tmp, tmp, row("beta"), ALU.add).then_inc(gate_step.up(T), 1)
                        dve.wait_ge(gate_step.sem, gate_step.at(4 * i + 4))
                        nc.vector.scalar_tensor_tensor(out=x[:, i, :], in0=tmp, scalar=gain[:, layer:layer + 1],
                                                       in1=x[:, i, :], op0=ALU.mult, op1=ALU.add
                                                       ).then_inc(proj_exp.up(T), 1)
                        dve.wait_ge(proj_exp.sem, proj_exp.at(i + 1))
                        norm_dve(dve, i, x[:, i, :], xn, stats, norm_out)
                        router_dve(dve, i)
            end_stage()

        def attention3():
            used[0] = 0
            layer = 3
            wq = att_w[:, 0:2 * D].rearrange("p (k n) -> p k n", k=KC)
            wk = att_w[:, 2 * D:4 * D].rearrange("p (k n) -> p k n", k=KC)
            wfc = att_w[:, 4 * D:6 * D].rearrange("p (k n) -> p k n", k=KC)
            NV = G3 * C3
            wv = att_w[:, 6 * D:6 * D + KC * NV].rearrange("p (k n) -> p k n", k=KC)
            stats = carve_stats()
            index, y_buf = carve(TOP).bitcast(U32), carve(TOP, D)
            xn, xT, cT = carve(D), carve(KC, P), carve(KC, P)
            qT, kT = carve(KC, P), carve(KC, P)
            HG = P // C3
            k_head = carve(KC, 2, HG, L)
            v_pair = carve(G3, 2, 2, C3 + 1)
            mx = carve(H3)
            p = carve(H3, L)
            pT = carve(H3 // 2, P)
            inv = carve(H3)
            o, oT = carve(H3, C3), carve(KC, P)
            tmp = carve(D)
            W = 4 * (C3 + 1)

            with nc.Block() as block:
                @block.sync
                def _(sp):
                    for buf, name in ((wq, "wq3"), (wk, "wk3"), (wfc, "wfc3"), (wv, "wv3")):
                        sp.dma_start(buf, d[name].rearrange("(k p) n -> p k n", p=P)).then_inc(att_w_in.up(), 16)
                    load_ffn(sp, layer)
                    sp.dma_start(shared_up, d["shared_up"].rearrange("(k p) n -> p k n", p=P)).then_inc(ffn_w_in.up(), 16)
                    for c, n in chunks(SHARED):
                        sp.dma_start(shared_down[0:n, c, :], d["shared_down"][c * P:c * P + n, :]).then_inc(ffn_w_in.up(), 16)
                    with sp.Fori(0, T) as i:
                        sp.wait_ge(projected.sem, projected.at(i))
                        sp.dma_start(cT, d["ctxT"][i]).then_inc(ctx_in.up(T), 16)

                @block.gpsimd
                def _(pool):
                    with pool.Fori(0, T) as i:
                        gather_rows(pool, i, index, y_buf)
                        norm_pool(pool, i, stats, norm_in)
                        norm_pool(pool, i, stats, norm_out)
                        save_norm(pool, i, xn)

                @block.tensor
                def _(pe):
                    pe.wait_ge(att_w_in.sem, att_w_in.at(4))
                    with pe.Fori(0, T) as i:
                        pe.wait_ge(norm_in.done.sem, norm_in.done.at(i + 1))
                        turn(pe, xn, 0).then_inc(turned.up(T), 1)
                        pe.wait_ge(ctx_in.sem, ctx_in.at(i + 1))
                        pe.wait_ge(turned_out.sem, turned_out.at(2 * i + 1))
                        for w, src, at in ((wq, xT, 0), (wk, cT, D)):
                            for g in range(KC):
                                for k in range(KC):
                                    nc.tensor.matmul(ps[:, 2, at + g * P:at + (g + 1) * P], w[:, k, g * P:(g + 1) * P],
                                                     src[:, k, :], start=(k == 0), stop=(k == KC - 1))
                        for k in range(KC):
                            mm = nc.tensor.matmul(ps[:, 3, 0:NV], cT[:, k, :], wv[:, k, :], start=(k == 0), stop=(k == KC - 1))
                        mm.then_inc(projected.up(T), 1)
                        pe.wait_ge(masked.sem, masked.at(i + 1))
                        for b in range(2):
                            for g in range(KC):
                                for a in range(2):
                                    mm = nc.tensor.matmul(
                                        ps[b * L:(b + 1) * L, 4 + 2 * g + a, :], qT[:, g, b * L:(b + 1) * L],
                                        k_head[:, g, b, a * 8:(a + 1) * 8, :].rearrange("p h s -> p (h s)"),
                                        start=True, stop=True)
                        mm.then_inc(scored.up(T), 1)
                        pe.wait_ge(probs.sem, probs.at(i + 1))
                        for j in range(H3 // 2):
                            mm = nc.tensor.transpose(ps[:, j // 4, (j % 4) * P:(j % 4 + 1) * P],
                                                     p[:, 2 * j:2 * j + 2, :].rearrange("p h s -> p (h s)"), ident[:])
                        mm.then_inc(probs_turned.up(T), 1)
                        pe.wait_ge(probs_out.sem, probs_out.at(2 * i + 2))
                        for j in range(H3 // 2):
                            mm = nc.tensor.matmul(ps[:, 4 + j // 8, (j % 8) * W:(j % 8 + 1) * W], pT[:, j, :],
                                                  v_pair[:, j // 2].rearrange("p b h c -> p (b h c)"), start=True, stop=True)
                        mm.then_inc(attended.up(T), 1)
                        pe.wait_ge(attn_ready.sem, attn_ready.at(i + 1))
                        turn(pe, o.rearrange("p h c -> p (h c)"), 6).then_inc(up_made.up(T), 1)
                        pe.wait_ge(hT_ready.sem, hT_ready.at(i + 1))
                        for k in range(KC):
                            mm = nc.tensor.matmul(ps[:, 7, 0:D], oT[:, k, :], wfc[:, k, :], start=(k == 0), stop=(k == KC - 1))
                        mm.then_inc(out_made.up(T), 1)
                        router_pe(pe, layer, i, 2 * i + 1, xn, xT)

                @block.scalar
                def _(act):
                    nc.scalar.activation(table_call[:], half[:], ACT.Exp)
                    with act.Fori(0, T) as i:
                        turned_act(act, 2 * i, xT)
                        act.wait_ge(projected.sem, projected.at(i + 1))
                        nc.scalar.copy(qT.rearrange("p k t -> p (k t)"), ps[:, 2, 0:D]).then_inc(proj_out.up(T), 1)
                        nc.scalar.copy(kT.rearrange("p k t -> p (k t)"), ps[:, 2, D:2 * D]).then_inc(proj_out.up(T), 1)
                        act.wait_ge(shifted.sem, shifted.at(i + 1))
                        nc.scalar.activation(p.rearrange("p h s -> p (h s)"), p.rearrange("p h s -> p (h s)"), ACT.Exp,
                                             scale=float(1.0 / np.sqrt(C3))).then_inc(probs.up(T), 1)
                        act.wait_ge(probs_turned.sem, probs_turned.at(i + 1))
                        nc.scalar.copy(pT[:, 8:16, :], ps[:, 2:4, :].rearrange("p a (j n) -> p (a j) n", n=P)
                                       ).then_inc(probs_out.up(T), 1)
                        act.wait_ge(up_made.sem, up_made.at(i + 1))
                        nc.scalar.copy(oT.rearrange("p k t -> p (k t)"), ps[:, 6, 0:D]).then_inc(hT_ready.up(T), 1)
                        turned_act(act, 2 * i + 1, xT)

                @block.vector
                def _(dve):
                    nc.vector.memset(v_pair, 0.0).then_inc(ready.up(), 1)
                    dve.wait_ge(ready.sem, ready.at(1))
                    for a in range(2):
                        last = nc.vector.memset(v_pair[a * L:(a + 1) * L, :, :, a, C3:C3 + 1], 1.0)
                    last.then_inc(ready.up(), 1)
                    dve.wait_ge(ready.sem, ready.at(2))
                    with dve.Fori(0, T) as i:
                        dve.wait_ge(saved.sem, saved.at(i))
                        add_rows(dve, i, y_buf)
                        norm_dve(dve, i, x[:, i, :], xn, stats, norm_in)
                        dve.wait_ge(proj_out.sem, proj_out.at(2 * i + 2))
                        for h in range(HG):
                            nc.vector.tensor_scalar(k_head[:, :, :, h, :], kT.rearrange("p g (b s) -> p g b s", b=2),
                                                    col("mask3", h), None, ALU.mult)
                        for b in range(2):
                            for a in range(2):
                                last = nc.vector.tensor_copy(v_pair[a * L:(a + 1) * L, :, b, a, 0:C3],
                                                             ps[b * L:(b + 1) * L, 3, 0:NV].rearrange("p (g c) -> p g c", g=G3))
                        last.then_inc(masked.up(T), 1)
                        dve.wait_ge(scored.sem, scored.at(i + 1))
                        nc.vector.tensor_reduce(mx, ps[:, 4:8, :].rearrange("p a (h s) -> p (a h) s", s=L), AX.X, ALU.max
                                                ).then_inc(gate_step.up(T), 1)
                        dve.wait_ge(gate_step.sem, gate_step.at(3 * i + 1))
                        nc.vector.tensor_tensor(p, ps[:, 4:8, :].rearrange("p a (h s) -> p (a h) s", s=L),
                                                mx.unsqueeze(2).to_broadcast([P, H3, L]), ALU.subtract
                                                ).then_inc(shifted.up(T), 1)
                        dve.wait_ge(probs_turned.sem, probs_turned.at(i + 1))
                        nc.vector.tensor_copy(pT[:, 0:8, :], ps[:, 0:2, :].rearrange("p a (j n) -> p (a j) n", n=P)
                                              ).then_inc(probs_out.up(T), 1)
                        dve.wait_ge(attended.sem, attended.at(i + 1))
                        for b in range(2):
                            tok = slice(b * L, (b + 1) * L)
                            for a in range(2):
                                got = ps[tok, 4 + a, 0:8 * W].rearrange("p (j b h c) -> p j b h c", j=8, b=2, h=2)
                                last = nc.vector.reciprocal(
                                    inv[tok, a * 16:(a + 1) * 16].rearrange("p (j h) -> p j h", j=8), got[:, :, b, :, C3])
                        last.then_inc(gate_step.up(T), 1)
                        dve.wait_ge(gate_step.sem, gate_step.at(3 * i + 2))
                        for b in range(2):
                            tok = slice(b * L, (b + 1) * L)
                            for a in range(2):
                                got = ps[tok, 4 + a, 0:8 * W].rearrange("p (j b h c) -> p j b h c", j=8, b=2, h=2)
                                last = nc.vector.tensor_tensor(
                                    o[tok, a * 16:(a + 1) * 16, :].rearrange("p (j h) c -> p j h c", j=8),
                                    got[:, :, b, :, 0:C3],
                                    inv[tok, a * 16:(a + 1) * 16].rearrange("p (j h) -> p j h", j=8).unsqueeze(3)
                                    .to_broadcast([L, 8, 2, C3]), ALU.mult)
                        last.then_inc(attn_ready.up(T), 1)
                        dve.wait_ge(out_made.sem, out_made.at(i + 1))
                        nc.vector.tensor_tensor(tmp, ps[:, 7, 0:D], row("bfc"), ALU.add).then_inc(gate_step.up(T), 1)
                        dve.wait_ge(gate_step.sem, gate_step.at(3 * i + 3))
                        nc.vector.scalar_tensor_tensor(out=x[:, i, :], in0=tmp, scalar=gain[:, layer:layer + 1],
                                                       in1=x[:, i, :], op0=ALU.mult, op1=ALU.add
                                                       ).then_inc(proj_exp.up(T), 1)
                        dve.wait_ge(proj_exp.sem, proj_exp.at(i + 1))
                        norm_dve(dve, i, x[:, i, :], xn, stats, norm_out)
                        router_dve(dve, i)
            end_stage()

        s_at = E * (KC * 2 * HIDDEN[3] + len(chunks(HIDDEN[3])) * D)
        shared_up = ffn_w[:, s_at:s_at + KC * 2 * SHARED].rearrange("p (k m) -> p k m", k=KC)
        s_at += KC * 2 * SHARED
        n_sc = len(chunks(SHARED))
        shared_down = ffn_w[:, s_at:s_at + n_sc * D].rearrange("p (c n) -> p c n", c=n_sc)

        def shared_expert():
            used[0] = 0
            xs, xT = carve(D), carve(KC, P)
            hid, hT = carve(SHARED), carve(n_sc, P)
            with nc.Block() as block:
                @block.tensor
                def _(pe):
                    pe.wait_ge(ffn_w_in.sem, ffn_w_in.at(0))
                    with pe.Fori(0, T) as i:
                        pe.wait_ge(copied.sem, copied.at(i + 1))
                        turn(pe, xs, 0).then_inc(xT_made.up(T), 1)
                        pe.wait_ge(xT_ready.sem, xT_ready.at(i + 1))
                        for a in range(2):
                            for k in range(KC):
                                mm = nc.tensor.matmul(ps[:, 1 + a, 0:SHARED], xT[:, k, :],
                                                      shared_up[:, k, a * SHARED:(a + 1) * SHARED],
                                                      start=(k == 0), stop=(k == KC - 1))
                        mm.then_inc(up_made.up(T), 1)
                        pe.wait_ge(h_ready.sem, h_ready.at(i + 1))
                        for c, n in chunks(SHARED):
                            mm = nc.tensor.transpose(ps[0:n, 5, c * P:(c + 1) * P], hid[:, c * P:c * P + n], ident[:])
                        mm.then_inc(hT_made.up(T), 1)
                        pe.wait_ge(hT_ready.sem, hT_ready.at(i + 1))
                        for c, n in chunks(SHARED):
                            mm = nc.tensor.matmul(ps[:, 6, 0:D], hT[0:n, c, :], shared_down[0:n, c, :],
                                                  start=(c == 0), stop=(c == n_sc - 1))
                        mm.then_inc(y_made.up(T), 1)

                @block.scalar
                def _(act):
                    nc.scalar.activation(table_call[:], half[:], ACT.Silu)
                    with act.Fori(0, T) as i:
                        act.wait_ge(up_made.sem, up_made.at(i + 1))
                        nc.scalar.activation(hid, ps[:, 1, 0:SHARED], ACT.Silu).then_inc(silu_ready.up(T), 1)
                        act.wait_ge(hT_made.sem, hT_made.at(i + 1))
                        for c, n in chunks(SHARED):
                            last = nc.scalar.copy(hT[0:n, c, :], ps[0:n, 5, c * P:(c + 1) * P])
                        last.then_inc(hT_ready.up(T), 1)

                @block.vector
                def _(dve):
                    with dve.Fori(0, T) as i:
                        nc.vector.tensor_copy(xs, xn2[:, i, :]).then_inc(copied.up(T), 1)
                        dve.wait_ge(xT_made.sem, xT_made.at(i + 1))
                        nc.vector.tensor_copy(xT.rearrange("p k t -> p (k t)"), ps[:, 0, 0:2 * P]
                                              ).then_inc(xT_ready.up(T), 1)
                        dve.wait_ge(silu_ready.sem, silu_ready.at(i + 1))
                        nc.vector.tensor_tensor(hid, hid, ps[:, 2, 0:SHARED], ALU.mult).then_inc(h_ready.up(T), 1)
                        dve.wait_ge(y_made.sem, y_made.at(i + 1))
                        nc.vector.scalar_tensor_tensor(out=x[:, i, :], in0=ps[:, 6, 0:D], scalar=gain[:, 7:8],
                                                       in1=x[:, i, :], op0=ALU.mult, op1=ALU.add
                                                       ).then_inc(added.up(T), 1)
                        dve.wait_ge(added.sem, added.at(i + 1))
            end_stage()

        def route(layer):
            used[0] = 0
            top = carve(T, E)
            index8 = carve(T, E).bitcast(U32)
            index = carve(T, TOP)
            onehot = carve(TOP, T, E)
            chosen = carve(T, E)
            total = carve(E, T)
            scan_mask = carve(E, T)
            running = carve(E, T)
            many = carve(E, T)
            tiles_of = carve(E)
            tiles_to = carve(E)
            base = carve(E)
            grid = carve(T, E)
            picked = carve(TOP, T, E)
            slot_f = carve(TOP, T)
            passed = carve(SLOT_TILES, E)
            expert_f = carve(SLOT_TILES)
            gap, e_gap, w_sum = carve(T), carve(T), carve(T)
            rmax, prob = carve(T), carve(T, E)
            source = prob if layer == 3 else logits
            n = [0]

            with nc.Block() as block:
                @block.tensor
                def _(pe):
                    pe.wait_ge(h_ready.sem, h_ready.at(1))
                    nc.tensor.matmul(ps[:, 0, 0:P], before[:], chosen.rearrange("p t e -> p (t e)"), start=True, stop=True)
                    nc.tensor.matmul(ps[:, 1, 0:P], ones[:], chosen.rearrange("p t e -> p (t e)"), start=True, stop=True
                                     ).then_inc(y_made.up(), 1)

                @block.scalar
                def _(act):
                    if layer == 3:
                        act.wait_ge(silu_ready.sem, silu_ready.at(1))
                        nc.scalar.activation(prob, prob, ACT.Exp).then_inc(xT_ready.up(), 1)
                    else:
                        act.wait_ge(silu_ready.sem, silu_ready.at(1))
                        nc.scalar.activation(e_gap, gap, ACT.Exp).then_inc(xT_ready.up(), 1)

                @block.vector
                def _(dve):
                    def then(ins):
                        n[0] += 1
                        ins.then_inc(step.up(), 1)
                        dve.wait_ge(step.sem, step.at(n[0]))

                    if layer == 3:
                        then(nc.vector.tensor_reduce(rmax, logits[:], AX.X, ALU.max))
                        nc.vector.tensor_tensor(prob, logits[:], rmax.unsqueeze(2).to_broadcast([P, T, E]), ALU.subtract
                                                ).then_inc(silu_ready.up(), 1)
                        dve.wait_ge(xT_ready.sem, xT_ready.at(1))
                        then(nc.vector.tensor_reduce(w_sum, prob, AX.X, ALU.add))
                        then(nc.vector.reciprocal(w_sum, w_sum))
                        then(nc.vector.tensor_tensor(prob, prob, w_sum.unsqueeze(2).to_broadcast([P, T, E]), ALU.mult))
                    for t in range(T):
                        last = nc.vector.max(top[:, t, :], source[:, t, :])
                    then(last)
                    for t in range(T):
                        last = nc.vector.max_index(index8[:, t, :], top[:, t, :], source[:, t, :])
                    then(last)
                    if layer != 3:
                        nc.vector.tensor_tensor(gap, top[:, :, 1], top[:, :, 0], ALU.subtract).then_inc(silu_ready.up(), 1)
                    then(nc.vector.tensor_copy(index, index8[:, :, 0:TOP]))
                    for a in range(TOP):
                        last = nc.vector.tensor_tensor(
                            onehot[:, a], row("iota8").unsqueeze(1).to_broadcast([P, T, E]),
                            index[:, :, a:a + 1].to_broadcast([P, T, E]), ALU.is_equal)
                    then(last)
                    nc.vector.tensor_tensor(chosen, onehot[:, 0], onehot[:, 1], ALU.add).then_inc(h_ready.up(), 1)
                    nc.vector.memset(scan_mask, 1.0)
                    dve.wait_ge(y_made.sem, y_made.at(1))
                    then(nc.vector.tensor_copy(total, ps[:, 1, 0:P].rearrange("p (t e) -> p e t", e=E)))
                    then(nc.vector.memset(scan_mask[:, :, 0:1], 0.0))
                    then(nc.vector.tensor_tensor_scan(running.rearrange("p e t -> p (e t)"),
                                                      scan_mask.rearrange("p e t -> p (e t)"),
                                                      total.rearrange("p e t -> p (e t)"), 0.0, ALU.mult, ALU.add))
                    then(nc.vector.tensor_tensor(many, running[:, :, T - 1:T].to_broadcast([P, E, T]),
                                                 row("iota_k").unsqueeze(1).to_broadcast([P, E, T]), ALU.is_gt))
                    then(nc.vector.tensor_reduce(tiles_of, many, AX.X, ALU.add))
                    then(nc.vector.tensor_tensor_scan(tiles_to, ones[:, 0:E], tiles_of, 0.0, ALU.mult, ALU.add))
                    then(nc.vector.tensor_tensor(base, tiles_to, tiles_of, ALU.subtract))
                    then(nc.vector.tensor_scalar(base, base, float(P), None, ALU.mult))
                    then(nc.vector.tensor_tensor(running, running, total, ALU.subtract))
                    then(nc.vector.tensor_tensor(running, running, base.unsqueeze(2).to_broadcast([P, E, T]), ALU.add))
                    then(nc.vector.tensor_tensor(grid, ps[:, 0, 0:P].rearrange("p (t e) -> p t e", e=E),
                                                 running.rearrange("p e t -> p t e"), ALU.add))
                    for a in range(TOP):
                        last = nc.vector.tensor_tensor(picked[:, a], onehot[:, a], grid, ALU.mult)
                    then(last)
                    then(nc.vector.tensor_reduce(slot_f, picked, AX.X, ALU.add))
                    then(nc.vector.tensor_copy(slots[:], slot_f))
                    then(nc.vector.tensor_tensor(passed, row("iota_j").unsqueeze(2).to_broadcast([P, SLOT_TILES, E]),
                                                 tiles_to.unsqueeze(1).to_broadcast([P, SLOT_TILES, E]), ALU.is_ge))
                    then(nc.vector.tensor_reduce(expert_f, passed, AX.X, ALU.add))
                    then(nc.vector.tensor_scalar(expert_f, expert_f, float(E - 1), None, ALU.min))
                    then(nc.vector.tensor_copy(tile_expert[:], expert_f[0:1, :]))
                    g = gain[:, 4 + layer:5 + layer]
                    if layer == 3:
                        then(nc.vector.tensor_scalar(weight[:].rearrange("p a t -> p t a"), top[:, :, 0:TOP], g, None, ALU.mult))
                    else:
                        dve.wait_ge(xT_ready.sem, xT_ready.at(1))
                        then(nc.vector.tensor_scalar(w_sum, e_gap, 1.0, None, ALU.add))
                        then(nc.vector.reciprocal(w_sum, w_sum))
                        then(nc.vector.tensor_scalar(weight[:, 0, :], w_sum, g, None, ALU.mult))
                        then(nc.vector.tensor_tensor(weight[:, 1, :], weight[:, 0, :], e_gap, ALU.mult))
            end_stage()

        def experts(layer):
            used[0] = 0
            m = HIDDEN[layer]
            cs = chunks(m)
            NT = SLOT_TILES
            wide = 2 * m > 512
            xs = [carve(D) for _ in range(2)]
            xT = [carve(KC, P) for _ in range(2)]
            silu = [carve(m) for _ in range(2)]
            hT = [carve(len(cs), P) for _ in range(2)]
            y = [carve(D) for _ in range(2)]
            up, down = up_view(layer), down_view(layer)
            PAIRS = NT // 2

            def gate_bank(u):
                return 1 + 2 * u

            def up_part(u):
                return ps[:, 2 + 2 * u, 0:m] if wide else ps[:, 1 + 2 * u, m:2 * m]

            with nc.Block() as block:
                @block.sync
                def _(sp):
                    sp.wait_ge(scattered.sem, scattered.at(TOP * T))

                    def load(k, u):
                        sp.wait_ge(xT_made.sem, xT_made.at(2 * k + u - 1))
                        sp.dma_start(xs[u], slot_x[bass.ds((2 * k + u) * P, P), :]).then_inc(slot_in[u].sem, 16)

                    def store(k, u):
                        sp.wait_ge(y_ready.sem, y_ready.at(2 * k + u + 1))
                        sp.dma_start(slot_y[bass.ds((2 * k + u) * P, P), :], y[u]).then_inc(slot_out[u].sem, 16)

                    load(0, 0)
                    load(0, 1)
                    with sp.Fori(0, PAIRS - 1) as i:
                        for u in range(2):
                            load(i + 1, u)
                            store(i, u)
                    load(PAIRS, 0)
                    store(PAIRS - 1, 0)
                    store(PAIRS - 1, 1)
                    store(PAIRS, 0)
                    for u in range(2):
                        slot_in[u].up(PAIRS + 1 - u)
                        slot_out[u].up(PAIRS + 1 - u)
                        sp.wait_ge(slot_out[u].sem, slot_out[u].at(PAIRS + 1 - u))

                @block.gpsimd
                def _(pool):
                    for t in range(T):
                        for a in range(TOP):
                            nc.gpsimd.indirect_dma_start(
                                slot_x, bass.IndirectOffsetOnAxis(ap=slots[:, a, t:t + 1], axis=0), xn2[:, t, :], None
                            ).then_inc(scattered.up(), 16)

                @block.tensor
                def _(pe):
                    pe.wait_ge(ffn_w_in.sem, ffn_w_in.at(0))

                    def first(k, u):
                        j = 2 * k + u
                        pe.wait_ge(slot_in[u].sem, slot_in[u].at(k + 1))
                        pe.wait_ge(xT_ready.sem, xT_ready.at(j))
                        turn(pe, xs[u], 0).then_inc(xT_made.sem, 1)
                        e = pe.value_load(tile_expert[0:1, bass.ds(j, 1)], min_val=0, max_val=E - 1)
                        pe.wait_ge(xT_ready.sem, xT_ready.at(j + 1))
                        pe.wait_ge(h_ready.sem, h_ready.at(j - 1))
                        for o, n, bank in (((0, m, gate_bank(u)), (m, m, gate_bank(u) + 1)) if wide
                                           else ((0, 2 * m, gate_bank(u)),)):
                            for c in range(KC):
                                mm = nc.tensor.matmul(ps[:, bank, 0:n], xT[u][:, c, :], up[:, e, c, o:o + n],
                                                      start=(c == 0), stop=(c == KC - 1))
                        mm.then_inc(up_made.sem, 1)

                    def second(k, u):
                        j = 2 * k + u
                        pe.wait_ge(h_ready.sem, h_ready.at(j + 1))
                        pe.wait_ge(hT_ready.sem, hT_ready.at(j))
                        for c, n in cs:
                            mm = nc.tensor.transpose(ps[0:n, 5, c * P:(c + 1) * P], silu[u][:, c * P:c * P + n], ident[:])
                        mm.then_inc(hT_made.sem, 1)
                        e = pe.value_load(tile_expert[0:1, bass.ds(j, 1)], min_val=0, max_val=E - 1)
                        pe.wait_ge(hT_ready.sem, hT_ready.at(j + 1))
                        pe.wait_ge(y_ready.sem, y_ready.at(j - 1))
                        for c, n in cs:
                            mm = nc.tensor.matmul(ps[:, 6 + u, 0:D], hT[u][0:n, c, :], down[0:n, e, c, :],
                                                  start=(c == 0), stop=(c == len(cs) - 1))
                        mm.then_inc(y_made.sem, 1)

                    first(0, 0)
                    with pe.Fori(0, PAIRS) as i:
                        first(i, 1)
                        second(i, 0)
                        first(i + 1, 0)
                        second(i, 1)
                    second(PAIRS, 0)
                    for s in (xT_made, up_made, hT_made, y_made):
                        s.up(NT)

                @block.scalar
                def _(act):
                    def silu_of(k, u):
                        j = 2 * k + u
                        act.wait_ge(up_made.sem, up_made.at(j + 1))
                        act.wait_ge(hT_made.sem, hT_made.at(j - 1))
                        nc.scalar.activation(silu[u], ps[:, gate_bank(u), 0:m], ACT.Silu).then_inc(silu_ready.sem, 1)

                    def rest(k, u):
                        j = 2 * k + u
                        act.wait_ge(hT_made.sem, hT_made.at(j + 1))
                        act.wait_ge(y_made.sem, y_made.at(j - 1))
                        for c, n in cs:
                            last = nc.scalar.copy(hT[u][0:n, c, :], ps[0:n, 5, c * P:(c + 1) * P])
                        last.then_inc(hT_ready.sem, 1)
                        act.wait_ge(y_made.sem, y_made.at(j + 1))
                        act.wait_ge(slot_out[u].sem, slot_out[u].at(k))
                        nc.scalar.copy(y[u], ps[:, 6 + u, 0:D]).then_inc(y_ready.sem, 1)

                    nc.scalar.activation(table_call[:], half[:], ACT.Silu)
                    silu_of(0, 0)
                    with act.Fori(0, PAIRS) as i:
                        silu_of(i, 1)
                        rest(i, 0)
                        silu_of(i + 1, 0)
                        rest(i, 1)
                    rest(PAIRS, 0)
                    for s in (silu_ready, hT_ready, y_ready):
                        s.up(NT)

                @block.vector
                def _(dve):
                    def both(k, u):
                        j = 2 * k + u
                        dve.wait_ge(xT_made.sem, xT_made.at(j + 1))
                        dve.wait_ge(up_made.sem, up_made.at(j - 1))
                        nc.vector.tensor_copy(xT[u].rearrange("p k t -> p (k t)"), ps[:, 0, 0:2 * P]
                                              ).then_inc(xT_ready.sem, 1)
                        dve.wait_ge(silu_ready.sem, silu_ready.at(j + 1))
                        nc.vector.tensor_tensor(silu[u], silu[u], up_part(u), ALU.mult).then_inc(h_ready.sem, 1)

                    with dve.Fori(0, PAIRS) as i:
                        for u in range(2):
                            both(i, u)
                    both(PAIRS, 0)
                    for s in (xT_ready, h_ready):
                        s.up(NT)
            end_stage()

        def finish():
            used[0] = 0
            index, y_buf = carve(TOP).bitcast(U32), carve(TOP, D)
            with nc.Block() as block:
                @block.gpsimd
                def _(pool):
                    with pool.Fori(0, T) as i:
                        gather_rows(pool, i, index, y_buf)

                @block.vector
                def _(dve):
                    with dve.Fori(0, T) as i:
                        add_rows(dve, i, y_buf)
                        dve.sem_inc(tile_done.up(T), 1)

                @block.sync
                def _(sp):
                    with sp.Fori(0, T) as i:
                        sp.wait_ge(added.sem, added.at(i + 1))
                        sp.dma_start(out[bass.ds(i * P, P), :], x[:, i, :]).then_inc(out_done.up(T), 16)
                    sp.wait_ge(out_done.sem, out_done.at(T))
            end_stage()

        for layer, attention in enumerate((attention0, attention1, attention2, attention3)[:LAYERS]):
            attention()
            route(layer)
            if layer == 3:
                shared_expert()
            experts(layer)
        finish()


def host_arrays(v):
    f = np.float32
    a = {}
    a["ident"] = np.eye(P, dtype=f)
    a["before"] = np.triu(np.ones((P, P), f), 1)
    a["x"] = v["x"].reshape(T, P, D).transpose(1, 0, 2)
    a["ctx"] = v["ctx_2048"].reshape(T, P, D)
    a["ctxT"] = v["ctx_2048"].reshape(T, P, KC, P).transpose(0, 3, 2, 1)
    i = np.arange(P)
    a["mask0"] = np.tile((i[:, None] // HD0 == i[None, :] // HD0).astype(f), (1, 2))
    inv = (1.0 / 10000.0 ** (np.arange(0, C1, 2, dtype=f) / C1)).astype(f)
    pos = (np.arange(D, dtype=f)[:, None] * inv[None, :]).astype(f)
    pos = np.concatenate([pos, pos], axis=-1)
    sign = np.where(np.arange(C1) < C1 // 2, -1.0, 1.0).astype(f)
    cos = np.tile(np.repeat(np.cos(pos).T, H1, 0), (2, 1)).astype(f)
    sin = np.tile(np.repeat((np.sin(pos) * sign).T, H1, 0), (2, 1)).astype(f)
    scale = f(1.0 / np.sqrt(C1))

    def on_all(r):
        return np.broadcast_to(np.asarray(r, f).reshape(1, -1), (P, np.asarray(r).size))

    def vec2(b):
        return np.asarray(b).reshape(KC, P).T

    plain = np.arange(64).reshape(H1, C1).T.reshape(-1)
    turn8 = np.arange(64).reshape(H1, 2, C1 // 2)[:, ::-1].reshape(H1, C1).T.reshape(-1)
    two = lambda b: np.concatenate([b, b]).reshape(P, 1)
    c = {"g": on_all(np.concatenate([v["g_xattn"], v["g_ffn"]])), "bg": vec2(v["L0_xattn_bg"]),
         "bq": np.concatenate([two(v["L1_xattn_bq"][plain]), two(v["L1_xattn_bq"][turn8])], 1),
         "bk": np.concatenate([two(v["L1_xattn_bk"][plain]), two(v["L1_xattn_bk"][turn8])], 1),
         "bo": two(v["L1_xattn_bo"]),
         "mask3": (i[:, None] // C3 == np.arange(P // C3)[None, :]).astype(f),
         "decay": on_all(v["L2_xattn_decay"]), "b_in": vec2(v["L2_xattn_b_in"]),
         "batch_of": (i[:, None] // L == np.arange(2)[None, :]).astype(f)}
    a["cols"] = np.concatenate([c[n] for n, _ in COLS], 1)
    r = {"bv": on_all(np.concatenate([v["L1_xattn_bv"]] * 2)), "bfc": on_all(v["L3_xattn_bfc"]),
         "gamma": on_all(v["L2_xattn_gamma"]), "beta": on_all(v["L2_xattn_beta"]), "b_out": on_all(v["L2_xattn_b_out"]),
         "iota8": on_all(np.arange(E)), "iota_k": on_all(np.arange(T) * P), "iota_j": on_all(np.arange(SLOT_TILES)),
         "cos_q": cos * scale, "sin_q": sin * scale, "cos_k": cos, "sin_k": sin}
    a["rows"] = np.concatenate([r[n] for n, _ in ROWS], 1)
    router = [v["L0_ffn_w_gate"], v["L1_ffn_gate_w"], v["L2_ffn_Wg"].T, v["L3_ffn_W_g"]]
    a["router_w"] = np.stack(router).reshape(4, KC, P, E).transpose(2, 0, 1, 3)
    a["wq0"], a["wg0"], a["wkv0"], a["wo0"] = (v[f"L0_xattn_{n}"].T for n in ("Wq", "Wg", "Wkv", "Wo"))
    a["up0"] = np.concatenate([v["L0_ffn_wi_0"], v["L0_ffn_wi_1"]], 2)
    a["down0"] = v["L0_ffn_wo"]
    a["up1"] = np.concatenate([v["L1_ffn_w0"], v["L1_ffn_w1"]], 2)
    a["down1"] = v["L1_ffn_wo"]
    a["up2"] = np.concatenate([v["L2_ffn_W1"], v["L2_ffn_W2"]], 1).transpose(0, 2, 1)
    a["down2"] = v["L2_ffn_W3"].transpose(0, 2, 1)
    a["up3"] = np.concatenate([v["L3_ffn_Wg"], v["L3_ffn_Wu"]], 2)
    a["down3"] = v["L3_ffn_Wd"]
    a["shared_up"] = np.concatenate([v["L3_ffn_Ws_gate"], v["L3_ffn_Ws_up"]], 1)
    a["shared_down"] = v["L3_ffn_Ws_down"]

    def both(w):
        z = np.zeros((P, P), f)
        z[0:64, 0:64] = z[64:P, 64:P] = w.T
        return z

    a["wq1"], a["wq1_turned"] = both(v["L1_xattn_Wq"][plain]), both(v["L1_xattn_Wq"][turn8])
    a["wk1"], a["wk1_turned"] = both(v["L1_xattn_Wk"][plain]), both(v["L1_xattn_Wk"][turn8])
    a["wv1"] = both(v["L1_xattn_Wv"])
    wo1 = np.zeros((4, 32, 2, 2, 2, 64), f)
    per_head = v["L1_xattn_Wo"].T.reshape(2, 4, C1, 64).transpose(1, 2, 0, 3)
    wo1[:, 0:C1, :, 0, 0] = wo1[:, 0:C1, :, 1, 1] = per_head
    wo1 = wo1.reshape(P, 2, 2, P)
    a["wo1"] = wo1
    a["w_in2"], a["w_out2"] = v["L2_xattn_W_in"].T, v["L2_xattn_W_out"].T
    a["pick"] = (np.arange(L)[None, :] == L - 1 - i[:, None] % L).astype(f)
    a["wq3"], a["wfc3"], a["wv3"] = (v[f"L3_xattn_{n}"].T for n in ("Wq", "Wfc", "Wv"))
    a["wk3"] = np.repeat(v["L3_xattn_Wk"].reshape(G3, C3, D), H3 // G3, 0).reshape(H3 * C3, D).T
    return {f"in_{k}": np.ascontiguousarray(b) for k, b in a.items()}


def kernel(**inputs):
    import concourse.bacc as bacc
    from concourse.bass_utils import run_bass_kernel_spmd

    nc = bacc.Bacc("TRN2", target_bir_lowering=False, num_devices=1)
    arrays = host_arrays({k: np.asarray(a) for k, a in inputs.items()})
    d = {k[3:]: nc.dram_tensor(k, a.shape, mybir.dt.from_np(a.dtype), kind="ExternalInput").ap()
         for k, a in arrays.items()}
    out = nc.dram_tensor("out", (B * L, D), F32, kind="ExternalOutput").ap()
    build(nc, d, out)
    r = run_bass_kernel_spmd(nc, [arrays], core_ids=[0])
    return r.results[0]["out"].reshape(B, L, D)
```

```python
from contextlib import ExitStack

import numpy as np

import concourse.bass as bass
from concourse import mybir

F32 = mybir.dt.float32
BF16 = mybir.dt.bfloat16
I32 = mybir.dt.int32
U32 = mybir.dt.uint32
ALU = mybir.AluOpType
ACT = mybir.ActivationFunctionType
AX = mybir.AxisListType

P = 128
B, L, D = 32, 64, 256
T = B * L // P
KC = D // P
E = 8
TOP = 2
LANES = 4
LAYERS = 4
START = 2
SLOT_TILES = TOP * B * L // P + E - 1
WORK = 14760
LN_EPS = 1e-5
LIN_EPS = 1e-6
HIDDEN = (128, 512, 176, 176)
SHARED = 352
HD0 = 16
H1, C1 = 8, 8
H3, G3, C3 = 32, 8, 8
TW = L

COLS = (("g", 8), ("bg", 2), ("bq", 2), ("bk", 2), ("bo", 1), ("mask3", 16),
        ("decay", 1), ("b_in", 2), ("batch_of", 2))
ROWS = (("bv", 128), ("bfc", D), ("gamma", D), ("beta", D), ("b_out", D), ("iota8", E), ("iota_k", T),
        ("iota_j", SLOT_TILES), ("cos_q", D), ("sin_q", D), ("cos_k", D), ("sin_k", D))


class Signal:

    def __init__(self, sem, step, start):
        self.sem, self.step, self.start = sem, step, start
        self.base, self.raised = start * step, 0

    def up(self, times=1):
        self.raised += times
        return self.sem

    def at(self, n):
        return n * self.step + self.base

    def end_stage(self):
        self.base += self.raised * self.step
        self.raised = 0


def chunks(m):
    return [(c, min(P, m - c * P)) for c in range((m + P - 1) // P)]


def build(nc, d, out):
    ctx = ExitStack()
    with ctx:
        def sb(name, shape, dt=F32):
            return ctx.enter_context(nc.sbuf_tensor(name, shape, dt))

        signals = []

        def sig(name, step=1, start=START):
            signals.append(Signal(ctx.enter_context(nc.semaphore(name)), step, start))
            return signals[-1]

        def end_stage():
            for s in signals:
                s.end_stage()

        slot_x = nc.dram_tensor("slot_x", (SLOT_TILES * P, D), F32, kind="Internal").ap()
        slot_y = nc.dram_tensor("slot_y", (SLOT_TILES * P, D), F32, kind="Internal").ap()

        qk_parts = nc.dram_tensor("qk_parts", (2, 3, 2, C1, H1 * D), BF16, kind="Internal").ap()

        x = sb("x", [P, T, D])
        xn2 = sb("xn2", [P, T, D])
        ffn_w = sb("ffn_w", [P, E * (KC * 2 * 512 + 4 * D)])
        att_w = sb("att_w", [P, 2560])
        ident = sb("ident", [P, P])
        before = sb("before", [P, P])
        ones = sb("ones", [P, P])
        cols = sb("cols", [P, sum(n for _, n in COLS)])
        rows = sb("rows", [P, sum(n for _, n in ROWS)])
        router_w = sb("router_w", [P, 4, KC, E])
        gain = sb("gain", [P, 8])
        half = sb("half", [P, 1])
        table_call = sb("table_call", [P, 1])
        logits = sb("logits", [P, T, E])
        slots = sb("slots", [P, TOP, T], U32)
        weight = sb("weight", [P, TOP, T])
        tile_expert = sb("tile_expert", [1, SLOT_TILES], I32)
        work = sb("work", [P, WORK])
        ps = ctx.enter_context(nc.psum_tensor("ps", [P, 8, 512], F32))
        used = [0]

        def carve(*shape):
            n = int(np.prod(shape))
            v = work[:, used[0]:used[0] + n]
            used[0] += n
            assert used[0] <= WORK, used
            if len(shape) == 1:
                return v
            names = "abcdef"[:len(shape)]
            return v.rearrange(f"p ({' '.join(names)}) -> p {' '.join(names)}",
                               **dict(zip(names[1:], shape[1:])))

        def place(table):
            at, o = {}, 0
            for name, n in table:
                at[name] = (o, n)
                o += n
            return at

        col_at, row_at = place(COLS), place(ROWS)

        def col(name, j=0, n=1):
            return cols[:, col_at[name][0] + j:col_at[name][0] + j + n]

        def row(name):
            o, n = row_at[name]
            return rows[:, o:o + n]

        consts_in, ffn_w_in, att_w_in = sig("consts_in", 16), sig("ffn_w_in", 16), sig("att_w_in", 16)
        zeros_out, out_done, ctx_in = sig("zeros_out", 16), sig("out_done", 16), sig("ctx_in", 16)
        slot_in = [sig(f"slot_in{u}", 16) for u in range(2)]
        slot_out = [sig(f"slot_out{u}", 16) for u in range(2)]
        y_in, scattered = sig("y_in", 16, 0), sig("scattered", 16, 0)
        y_in_lane = [sig(f"y_in_lane{u}", 16, 0) for u in range(LANES)]
        ready, index_ready, held_pool, held_dve = (sig(n) for n in ("ready", "index_ready", "held_pool", "held_dve"))
        half_added, added, tile_done = (sig(n) for n in ("half_added", "added", "tile_done"))
        saved = sig("saved")

        class Norm:
            def __init__(self, name):
                self.stats, self.mean, self.var, self.rstd, self.done = (
                    sig(f"{name}_{n}") for n in ("stats", "mean", "var", "rstd", "done"))

        norm_in, norm_out, norm_mid = Norm("norm_in"), Norm("norm_out"), Norm("norm_mid")
        copied = sig("copied")
        q_out, gate_out = sig("q_out"), sig("gate_out")
        parts_out = sig("parts_out", 16)
        stack_in = [sig(f"stack_in{b}", 16) for b in range(2)]
        q_projected, k_projected, v_projected, roped, split_step = (
            sig(n) for n in ("q_projected", "k_projected", "v_projected", "roped", "split_step"))
        v_staged, v_placed, inv_made, inv_ready, inv_out = (
            sig(n) for n in ("v_staged", "v_placed", "inv_made", "inv_ready", "inv_out"))
        probs_by_bank = [sig(f"probs_turned{a}") for a in range(2)]
        pT_out_dve, pT_out_act = sig("pT_out_dve"), sig("pT_out_act")
        turned, turned_out = sig("turned"), sig("turned_out")
        masked_act, k_out, max_found, o_turned, oT_ready = (
            sig(n) for n in ("masked_act", "k_out", "max_found", "o_turned", "oT_ready"))
        projected, projected_kv, proj_min, proj_exp, proj_out = (
            sig(n) for n in ("projected", "projected_kv", "proj_min", "proj_exp", "proj_out"))
        gate_step, masked, scored, shifted, probs = (
            sig(n) for n in ("gate_step", "masked", "scored", "shifted", "probs"))
        probs_turned, probs_out, attended, norm_step, attn_ready, out_made = (
            sig(n) for n in ("probs_turned", "probs_out", "attended", "norm_step", "attn_ready", "out_made"))
        logits_made, step = sig("logits_made"), sig("step")
        xT_made, xT_ready, up_made, silu_ready = (sig(n) for n in ("xT_made", "xT_ready", "up_made", "silu_ready"))
        h_ready, hT_made, hT_ready, y_made, y_ready = (
            sig(n) for n in ("h_ready", "hT_made", "hT_ready", "y_made", "y_ready"))

        with nc.Block() as block:
            @block.sync
            def _(sp):
                for s in signals:
                    if s.start:
                        sp.sem_inc(s.sem, s.start * s.step)

        consts = ((ident, "ident"), (before, "before"), (cols, "cols"), (rows, "rows"),
                  (router_w, "router_w"), (x, "x"))
        zeros = work[:, 0:SLOT_TILES // 3 * D]
        with nc.Block() as block:
            @block.sync
            def _(sp):
                for buf, name in consts:
                    sp.dma_start(buf[:], d[name]).then_inc(consts_in.up(), 16)
                sp.wait_ge(ready.sem, ready.at(1))
                n = SLOT_TILES // 3
                for j in range(3):
                    sp.dma_start(slot_x[j * n * P:(j + 1) * n * P].rearrange("(t p) d -> p t d", p=P),
                                 zeros.rearrange("p (t d) -> p t d", d=D)).then_inc(zeros_out.up(), 16)
                sp.wait_ge(zeros_out.sem, zeros_out.at(3))

            @block.vector
            def _(dve):
                nc.vector.memset(zeros, 0.0).then_inc(ready.up(), 1)
                nc.vector.memset(ones[:], 1.0)
                nc.vector.memset(half[:], -0.5)

            @block.scalar
            def _(act):
                act.wait_ge(consts_in.sem, consts_in.at(len(consts)))
                nc.scalar.activation(gain[:], col("g", 0, 8), ACT.Tanh)
        end_stage()

        def gather_rows(pool, i, index, y_buf):
            pool.wait_ge(tile_done.sem, tile_done.at(i))
            nc.gpsimd.tensor_copy(index, slots[:, :, bass.ds(i, 1)].rearrange("p a b -> p (a b)")
                                  ).then_inc(index_ready.up(T), 1)
            pool.wait_ge(index_ready.sem, index_ready.at(i + 1))
            pool.sem_inc(held_pool.up(T), 1)
            for a in range(TOP):
                nc.gpsimd.indirect_dma_start(
                    y_buf[:, a, :], None, slot_y,
                    bass.IndirectOffsetOnAxis(ap=index[:, a:a + 1], axis=0)).then_inc(y_in.up(T), 16)

        def add_rows(dve, i, y_buf):
            dve.wait_ge(y_in.sem, y_in.at(TOP * i + TOP))
            nc.vector.scalar_tensor_tensor(
                out=x[:, i, :], in0=y_buf[:, 0, :], scalar=weight[:, 0, bass.ds(i, 1)], in1=x[:, i, :],
                op0=ALU.mult, op1=ALU.add).then_inc(half_added.up(T), 1)
            dve.wait_ge(half_added.sem, half_added.at(i + 1))
            nc.vector.scalar_tensor_tensor(
                out=x[:, i, :], in0=y_buf[:, 1, :], scalar=weight[:, 1, bass.ds(i, 1)], in1=x[:, i, :],
                op0=ALU.mult, op1=ALU.add).then_inc(added.up(T), 1)
            dve.wait_ge(added.sem, added.at(i + 1))

        def norm_stats(dve, n, src, stats, norm, times):
            dve.sem_inc(held_dve.up(times), 1)
            nc.vector.bn_stats(stats["bn"], src).then_inc(norm.stats.up(times), 1)
            dve.wait_ge(norm.stats.sem, norm.stats.at(n + 1))
            dve.sem_inc(held_dve.up(times), 1)
            nc.vector.bn_aggr(stats["mv"], stats["bn"]).then_inc(norm.mean.up(times), 1)
            dve.wait_ge(norm.mean.sem, norm.mean.at(n + 1))
            nc.vector.tensor_scalar(stats["var"], stats["mv"][:, 1:2], LN_EPS, None, ALU.add
                                    ).then_inc(norm.var.up(times), 1)

        def norm_apply(dve, n, src, dst, stats, norm, times):
            dve.wait_ge(norm.rstd.sem, norm.rstd.at(n + 1))
            nc.vector.tensor_scalar(dst, src, stats["mv"][:, 0:1], stats["rstd"], ALU.subtract, ALU.mult
                                    ).then_inc(norm.done.up(times), 1)

        def norm_dve(dve, n, src, dst, stats, norm, times=T):
            norm_stats(dve, n, src, stats, norm, times)
            norm_apply(dve, n, src, dst, stats, norm, times)

        def norm_pool(pool, n, stats, norm, times=T):
            pool.wait_ge(norm.var.sem, norm.var.at(n + 1))
            nc.gpsimd.tensor_tensor(stats["rstd"], stats["var"], half[:], ALU.pow).then_inc(norm.rstd.up(times), 1)

        def carve_stats():
            return {"bn": carve(6), "mv": carve(2), "var": carve(1), "rstd": carve(1)}

        def turn(pe, src, bank, at=0):
            for k in range(KC):
                mm = nc.tensor.transpose(ps[:, bank, at + k * P:at + (k + 1) * P], src[:, k * P:(k + 1) * P], ident[:])
            return mm

        def save_norm(pool, i, xn, times=T):
            pool.wait_ge(norm_out.done.sem, norm_out.done.at(i + 1))
            nc.gpsimd.tensor_copy(xn2[:, i, :], xn).then_inc(saved.up(times), 1)

        def router_pe(pe, layer, i, n_turn, xn, xT):
            pe.wait_ge(norm_out.done.sem, norm_out.done.at(i + 1))
            turn(pe, xn, 0).then_inc(turned.up(T), 1)
            pe.wait_ge(turned_out.sem, turned_out.at(n_turn + 1))
            for k in range(KC):
                mm = nc.tensor.matmul(ps[:, 1, 0:E], xT[:, k, :], router_w[:, layer, k, :],
                                      start=(k == 0), stop=(k == KC - 1))
            mm.then_inc(logits_made.up(T), 1)

        def turned_act(act, n_turn, xT, n=2 * P, at=0):
            act.wait_ge(turned.sem, turned.at(n_turn + 1))
            nc.scalar.copy(xT.rearrange("p k t -> p (k t)"), ps[:, 0, at:at + n]).then_inc(turned_out.up(T), 1)

        def router_dve(dve, i):
            dve.wait_ge(logits_made.sem, logits_made.at(i + 1))
            nc.vector.tensor_copy(logits[:, i, :], ps[:, 1, 0:E]).then_inc(tile_done.up(T), 1)

        def load_ffn(sp, layer):
            m = HIDDEN[layer]
            sp.dma_start(up_view(layer), d[f"up{layer}"].rearrange("e (k p) m -> p e k m", p=P)
                         ).then_inc(ffn_w_in.up(), 16)
            for e in range(E):
                for c, n in chunks(m):
                    sp.dma_start(down_view(layer)[0:n, e, c, :], d[f"down{layer}"][e, c * P:c * P + n, :]
                                 ).then_inc(ffn_w_in.up(), 16)

        def up_view(layer):
            m = HIDDEN[layer]
            return ffn_w[:, 0:E * KC * 2 * m].rearrange("p (e k m) -> p e k m", e=E, k=KC)

        def down_view(layer):
            m = HIDDEN[layer]
            n, o = len(chunks(m)), E * KC * 2 * m
            return ffn_w[:, o:o + E * n * D].rearrange("p (e c n) -> p e c n", e=E, c=n)

        def n_ffn_dmas(layer):
            return 1 + E * len(chunks(HIDDEN[layer]))

        def attention0():
            used[0] = 0
            layer = 0
            wq = att_w[:, 0:2 * D].rearrange("p (k n) -> p k n", k=KC)
            wg = att_w[:, 2 * D:4 * D].rearrange("p (k n) -> p k n", k=KC)
            wkv = att_w[:, 4 * D:8 * D].rearrange("p (k n) -> p k n", k=KC)
            wo = att_w[:, 8 * D:10 * D].rearrange("p (k n) -> p k n", k=KC)
            stats_in, stats_out = carve_stats(), carve_stats()
            head_mask = carve(2 * P)
            neg_bg = carve(2)
            xn, xT = carve(D), carve(KC, P)
            xo, xoT = carve(D), carve(KC, P)
            cT = carve(KC, P)
            low_q, qT = carve(KC, P), carve(KC, P)
            low_k, k_map = carve(D), carve(D)
            v_ones = carve(KC, 2, P)
            e_gate = carve(KC, P)
            state = carve(2, KC, 2 * P)
            divisor, attn = carve(KC, P), carve(KC, P)
            X, Q, GATE, KV, STATE, ND, OUT = 0, 1, 2, 3, 4, 6, 7

            def flat(t):
                return t.rearrange("p k t -> p (k t)")

            def over_tiles(eng, body):
                with eng.Fori(0, T - 2) as i:
                    body(i, T - 2, qkv=True, norm=True)
                body(T - 2, 1, qkv=True, norm=False)
                body(T - 1, 1, qkv=False, norm=False)

            with nc.Block() as block:
                @block.sync
                def _(sp):
                    for buf, name in ((wq, "wq0"), (wg, "wg0"), (wkv, "wkv0"), (wo, "wo0")):
                        sp.dma_start(buf, d[name].rearrange("(k p) n -> p k n", p=P)).then_inc(att_w_in.up(), 16)
                    sp.dma_start(head_mask, d["mask0"]).then_inc(att_w_in.up(), 16)
                    sp.dma_start(cT, d["ctxT"][0]).then_inc(ctx_in.up(), 16)
                    load_ffn(sp, layer)
                    with sp.Fori(1, T) as j:
                        sp.wait_ge(projected.sem, projected.at(j))
                        sp.dma_start(cT, d["ctxT"][j]).then_inc(ctx_in.up(T - 1), 16)

                @block.gpsimd
                def _(pool):
                    def gate_plus_one(j, times):
                        pool.wait_ge(gate_step.sem, gate_step.at(2 * j + 2))
                        pool.sem_inc(held_pool.up(times), 1)
                        nc.gpsimd.tensor_scalar(flat(e_gate), flat(e_gate), 1.0, None, ALU.add).then_inc(gate_out.up(times), 1)

                    norm_pool(pool, 0, stats_in, norm_in, 1)
                    norm_pool(pool, 1, stats_in, norm_in, 1)
                    gate_plus_one(0, 1)

                    def body(i, times, qkv, norm):
                        if qkv:
                            gate_plus_one(i + 1, times)
                        norm_pool(pool, i, stats_out, norm_out, times)
                        if norm:
                            norm_pool(pool, i + 2, stats_in, norm_in, times)
                        save_norm(pool, i, xo, times)

                    over_tiles(pool, body)

                @block.tensor
                def _(pe):
                    def turn_in(j, times):
                        pe.wait_ge(norm_in.done.sem, norm_in.done.at(j + 1))
                        turn(pe, xn, X).then_inc(xT_made.up(times), 1)

                    def project(j, times):
                        pe.wait_ge(ctx_in.sem, ctx_in.at(j + 1))
                        pe.wait_ge(xT_ready.sem, xT_ready.at(j + 1))
                        pe.wait_ge(q_out.sem, q_out.at(j))
                        for w, bank in ((wq, Q), (wg, GATE)):
                            for g in range(KC):
                                for k in range(KC):
                                    mm = nc.tensor.matmul(ps[:, bank, g * P:(g + 1) * P], w[:, k, g * P:(g + 1) * P],
                                                          xT[:, k, :], start=(k == 0), stop=(k == KC - 1))
                            if bank == Q:
                                mm.then_inc(q_projected.up(times), 1)
                                pe.wait_ge(gate_step.sem, gate_step.at(2 * j))
                        pe.wait_ge(proj_out.sem, proj_out.at(2 * j))
                        for k in range(KC):
                            mm = nc.tensor.matmul(ps[:, KV, :], cT[:, k, :], wkv[:, k, :],
                                                  start=(k == 0), stop=(k == KC - 1))
                        mm.then_inc(projected.up(times), 1)

                    def sum_state(j, times):
                        pe.wait_ge(proj_out.sem, proj_out.at(2 * j + 2))
                        pe.wait_ge(masked.sem, masked.at(j))
                        for b in range(2):
                            for g in range(KC):
                                mm = nc.tensor.matmul(
                                    ps[:, STATE + b, g * 2 * P:(g + 1) * 2 * P], k_map[b * L:(b + 1) * L, g * P:(g + 1) * P],
                                    v_ones[b * L:(b + 1) * L, g, :, :].rearrange("p a n -> p (a n)"),
                                    start=True, stop=True)
                        mm.then_inc(scored.up(times), 1)

                    def read_state(i, times):
                        pe.wait_ge(masked.sem, masked.at(i + 1))
                        pe.wait_ge(q_out.sem, q_out.at(i + 1))
                        pe.wait_ge(attn_ready.sem, attn_ready.at(i))
                        for b in range(2):
                            for g in range(KC):
                                for a in range(2):
                                    mm = nc.tensor.matmul(
                                        ps[:, ND, a * D + g * P + b * L:a * D + g * P + (b + 1) * L],
                                        state[:, b, g, a * P:(a + 1) * P], qT[:, g, b * L:(b + 1) * L],
                                        start=True, stop=True)
                        mm.then_inc(attended.up(times), 1)

                    def project_out(i, times):
                        pe.wait_ge(attn_ready.sem, attn_ready.at(i + 1))
                        pe.wait_ge(tile_done.sem, tile_done.at(i))
                        for g in range(KC):
                            mm = nc.tensor.matmul(ps[:, OUT, 0:D], attn[:, g, :], wo[:, g, :],
                                                  start=(g == 0), stop=(g == KC - 1))
                        mm.then_inc(out_made.up(times), 1)

                    def route_out(i, times):
                        pe.wait_ge(norm_out.done.sem, norm_out.done.at(i + 1))
                        turn(pe, xo, OUT).then_inc(turned.up(times), 1)
                        pe.wait_ge(turned_out.sem, turned_out.at(i + 1))
                        for k in range(KC):
                            mm = nc.tensor.matmul(ps[:, OUT, 0:E], xoT[:, k, :], router_w[:, layer, k, :],
                                                  start=(k == 0), stop=(k == KC - 1))
                        mm.then_inc(logits_made.up(times), 1)

                    pe.wait_ge(att_w_in.sem, att_w_in.at(5))
                    turn_in(0, 1)
                    project(0, 1)
                    sum_state(0, 1)

                    def body(i, times, qkv, norm):
                        if qkv:
                            turn_in(i + 1, times)
                        read_state(i, times)
                        if qkv:
                            project(i + 1, times)
                        project_out(i, times)
                        if qkv:
                            sum_state(i + 1, times)
                        route_out(i, times)

                    over_tiles(pe, body)

                @block.scalar
                def _(act):
                    nc.scalar.activation(table_call[:], half[:], ACT.Exp)
                    act.wait_ge(ready.sem, ready.at(2))

                    def take_in(j, times):
                        act.wait_ge(xT_made.sem, xT_made.at(j + 1))
                        act.wait_ge(projected.sem, projected.at(j))
                        nc.scalar.copy(flat(xT), ps[:, X, 0:D]).then_inc(xT_ready.up(times), 1)

                    def exps(j, times):
                        act.wait_ge(proj_min.sem, proj_min.at(2 * j + 1))
                        nc.scalar.activation(low_q, low_q, ACT.Exp).then_inc(proj_exp.up(times), 1)
                        act.wait_ge(projected.sem, projected.at(j + 1))
                        act.wait_ge(attn_ready.sem, attn_ready.at(j))
                        for g in range(KC):
                            nc.scalar.activation(e_gate[:, g, :], ps[:, GATE, g * P:(g + 1) * P], ACT.Exp,
                                                 bias=neg_bg[:, g:g + 1], scale=-1.0).then_inc(gate_step.up(times), 1)
                        act.wait_ge(proj_min.sem, proj_min.at(2 * j + 2))
                        nc.scalar.activation(low_k, low_k, ACT.Exp).then_inc(proj_exp.up(times), 1)

                    def take_turned_out(i, times):
                        act.wait_ge(turned.sem, turned.at(i + 1))
                        act.wait_ge(logits_made.sem, logits_made.at(i))
                        nc.scalar.copy(flat(xoT), ps[:, OUT, 0:D]).then_inc(turned_out.up(times), 1)

                    take_in(0, 1)
                    exps(0, 1)

                    def body(i, times, qkv, norm):
                        if qkv:
                            take_in(i + 1, times)
                            exps(i + 1, times)
                        take_turned_out(i, times)

                    over_tiles(act, body)

                @block.vector
                def _(dve):
                    def enter(j, times):
                        norm_stats(dve, j, x[:, j, :], stats_in, norm_in, times)

                    def enter_apply(j, times):
                        dve.wait_ge(xT_made.sem, xT_made.at(j))
                        norm_apply(dve, j, x[:, j, :], xn, stats_in, norm_in, times)

                    def low_of_q(j, times):
                        dve.wait_ge(q_projected.sem, q_projected.at(j + 1))
                        nc.vector.tensor_scalar(flat(low_q), ps[:, Q, 0:D], 0.0, None, ALU.min).then_inc(proj_min.up(times), 1)

                    def low_of_k(j, times):
                        dve.wait_ge(projected.sem, projected.at(j + 1))
                        nc.vector.tensor_scalar(low_k, ps[:, KV, 0:D], 0.0, None, ALU.min).then_inc(proj_min.up(times), 1)

                    def take_v(j, times):
                        dve.wait_ge(scored.sem, scored.at(j))
                        nc.vector.tensor_copy(v_ones[:, :, 0, :], ps[:, KV, D:2 * D].rearrange("p (g n) -> p g n", g=KC)
                                              ).then_inc(proj_out.up(times), 1)

                    def maps(j, times):
                        dve.wait_ge(proj_exp.sem, proj_exp.at(2 * j + 1))
                        dve.wait_ge(attended.sem, attended.at(j))
                        nc.vector.scalar_tensor_tensor(out=flat(qT), in0=ps[:, Q, 0:D], scalar=1.0, in1=flat(low_q),
                                                       op0=ALU.add, op1=ALU.max).then_inc(q_out.up(times), 1)
                        dve.wait_ge(proj_exp.sem, proj_exp.at(2 * j + 2))
                        nc.vector.scalar_tensor_tensor(out=k_map, in0=ps[:, KV, 0:D], scalar=1.0, in1=low_k,
                                                       op0=ALU.add, op1=ALU.max).then_inc(proj_out.up(times), 1)

                    def mask(i, times):
                        dve.wait_ge(scored.sem, scored.at(i + 1))
                        dve.wait_ge(attended.sem, attended.at(i))
                        nc.vector.tensor_tensor(
                            state.rearrange("p b g n -> p (b g) n"),
                            ps[:, STATE:STATE + 2, :].rearrange("p b (g n) -> p (b g) n", g=KC),
                            head_mask.unsqueeze(1).to_broadcast([P, 2 * KC, 2 * P]), ALU.mult).then_inc(masked.up(times), 1)

                    def divide(i, times):
                        dve.wait_ge(attended.sem, attended.at(i + 1))
                        dve.wait_ge(gate_out.sem, gate_out.at(i + 1))
                        nc.vector.scalar_tensor_tensor(out=flat(divisor), in0=ps[:, ND, D:2 * D], scalar=LIN_EPS,
                                                       in1=flat(e_gate), op0=ALU.add, op1=ALU.mult
                                                       ).then_inc(norm_step.up(times), 1)
                        dve.wait_ge(norm_step.sem, norm_step.at(2 * i + 1))
                        nc.vector.reciprocal(divisor, divisor).then_inc(norm_step.up(times), 1)
                        dve.wait_ge(norm_step.sem, norm_step.at(2 * i + 2))
                        dve.wait_ge(out_made.sem, out_made.at(i))
                        nc.vector.tensor_tensor(flat(attn), ps[:, ND, 0:D], flat(divisor), ALU.mult
                                                ).then_inc(attn_ready.up(times), 1)

                    def leave(i, times):
                        dve.wait_ge(out_made.sem, out_made.at(i + 1))
                        nc.vector.scalar_tensor_tensor(
                            out=x[:, i, :], in0=ps[:, OUT, 0:D], scalar=gain[:, layer:layer + 1], in1=x[:, i, :],
                            op0=ALU.mult, op1=ALU.add).then_inc(added.up(times), 1)
                        dve.wait_ge(added.sem, added.at(i + 1))
                        norm_stats(dve, i, x[:, i, :], stats_out, norm_out, times)

                    def leave_apply(i, times):
                        dve.wait_ge(saved.sem, saved.at(i))
                        dve.wait_ge(turned.sem, turned.at(i))
                        norm_apply(dve, i, x[:, i, :], xo, stats_out, norm_out, times)

                    def take_logits(i, times):
                        dve.wait_ge(logits_made.sem, logits_made.at(i + 1))
                        nc.vector.tensor_copy(logits[:, i, :], ps[:, OUT, 0:E]).then_inc(tile_done.up(times), 1)

                    nc.vector.tensor_scalar(neg_bg, col("bg", 0, 2), -1.0, None, ALU.mult).then_inc(ready.up(), 1)
                    nc.vector.memset(v_ones[:, :, 1, :], 1.0).then_inc(ready.up(), 1)
                    dve.wait_ge(ready.sem, ready.at(2))
                    enter(0, 1)
                    enter_apply(0, 1)
                    enter(1, 1)
                    dve.wait_ge(att_w_in.sem, att_w_in.at(5))
                    low_of_q(0, 1)
                    low_of_k(0, 1)
                    take_v(0, 1)
                    maps(0, 1)
                    enter_apply(1, 1)

                    def body(i, times, qkv, norm):
                        mask(i, times)
                        divide(i, times)
                        if qkv:
                            low_of_q(i + 1, times)
                            low_of_k(i + 1, times)
                            take_v(i + 1, times)
                            maps(i + 1, times)
                        leave(i, times)
                        if norm:
                            enter(i + 2, times)
                        leave_apply(i, times)
                        if norm:
                            enter_apply(i + 2, times)
                        take_logits(i, times)

                    over_tiles(dve, body)
            end_stage()

        def attention1():
            used[0] = 0
            layer = 1
            HH = H1 // 2
            UNITS, PAIRS = 8, 4
            names = ("wq1", "wq1_turned", "wk1", "wk1_turned", "wv1")
            wq, wq_turned, wk, wk_turned, wv = (att_w[:, j * P:(j + 1) * P] for j in range(5))
            wo = att_w[:, 5 * P:9 * P].rearrange("p (a b n) -> p a b n", a=2, b=2)
            v_pad = att_w[:, 9 * P:17 * P].rearrange("p (b h s c) -> p b h s c", b=2, h=H1, s=2)
            stats_in, stats_out = carve_stats(), carve_stats()
            index, y_buf = carve(TOP).bitcast(U32), carve(TOP, D)
            xn, ctx_t = carve(D), carve(D)
            xo, xT = carve(D), carve(KC, P)
            rope_a, rope_b = carve(2, D), carve(2, D)
            whole, rest = carve(2, D), carve(2, D)
            parts = carve(2 * 3 * D // 2).bitcast(BF16).rearrange("p (s r t) -> p s r t", s=2, r=3)
            q_stack = carve(H1 * D // 2).bitcast(BF16).rearrange("p (h t) -> p h t", h=H1)
            k_stack = carve(H1 * D // 2).bitcast(BF16).rearrange("p (h t) -> p h t", h=H1)
            v = carve(2, P)
            neg_max, sums, inv = carve(2, HH), carve(2, HH), carve(2, HH)
            inv_wide = carve(2, HH, 32)
            inv_T = carve(D)
            p = carve(2, HH, 2, P)
            pT = carve(2, HH, 2, D)
            attn = carve(2, 2, D)
            tmp = carve(D)
            TURNED, PV, MISC = 4, 6, 7
            BODIES = T - 3

            def over_tiles(eng, body):
                body(0, 1, tail=False, qkv=True, norm=True)
                with eng.Fori(1, T - 2) as i:
                    body(i, BODIES, tail=True, qkv=True, norm=True)
                body(T - 2, 1, tail=True, qkv=True, norm=False)
                body(T - 1, 1, tail=True, qkv=False, norm=False)

            with nc.Block() as block:
                @block.sync
                def _(sp):
                    def load_ctx(j, times):
                        sp.wait_ge(v_projected.sem, v_projected.at(j))
                        sp.dma_start(ctx_t, d["ctx"][j]).then_inc(ctx_in.up(times), 16)

                    def stack(j, times):
                        sp.wait_ge(split_step.sem, split_step.at(10 * j + 10))
                        if not isinstance(j, int) or j > 0:
                            for b in range(2):
                                sp.wait_ge(stack_in[b].sem, stack_in[b].at(6 * j))
                        sp.dma_start(qk_parts.rearrange("s r b c (h t) -> (b c h) s r t", h=H1), parts
                                     ).then_inc(parts_out.up(times), 16)
                        sp.wait_ge(parts_out.sem, parts_out.at(j + 1))
                        for b in range(2):
                            sp.wait_ge(scored.sem, scored.at(UNITS * (j - 1) + 4 * b + 4))
                            o = 64 * b
                            q_of, k_of = qk_parts[0, :, b], qk_parts[1, :, b]
                            for r, (row0, copies) in enumerate(((0, 3), (24, 3), (48, 2))):
                                sp.dma_start(q_stack[o + row0:o + row0 + 8 * copies].rearrange("p h t -> p (h t)"),
                                             q_of[r].unsqueeze(0).to_broadcast([copies, C1, H1 * D])
                                             ).then_inc(stack_in[b].up(times), 16)
                            for o_k in (o, o + 24):
                                sp.dma_start(k_stack[o_k:o_k + 24].rearrange("p h t -> p (h t)"), k_of
                                             ).then_inc(stack_in[b].up(times), 16)
                            sp.dma_start(k_stack[o + 48:o + 64].rearrange("p h t -> p (h t)"), k_of[0:2]
                                         ).then_inc(stack_in[b].up(times), 16)

                    for j, name in enumerate(names):
                        sp.dma_start(att_w[:, j * P:(j + 1) * P], d[name]).then_inc(att_w_in.up(), 16)
                    sp.dma_start(wo, d["wo1"]).then_inc(att_w_in.up(), 16)
                    load_ctx(0, 1)
                    load_ctx(1, 1)
                    stack(0, 1)
                    load_ffn(sp, layer)
                    stack(1, 1)

                    def body(i, times, tail, qkv, norm):
                        if norm:
                            load_ctx(i + 2, times)
                            stack(i + 2, times)

                    over_tiles(sp, body)

                @block.gpsimd
                def _(pool):
                    def fetch(j, times):
                        pool.wait_ge(added.sem, added.at(j))
                        nc.gpsimd.tensor_copy(index, slots[:, :, bass.ds(j, 1)].rearrange("p a b -> p (a b)")
                                              ).then_inc(index_ready.up(times), 1)
                        pool.wait_ge(index_ready.sem, index_ready.at(j + 1))
                        pool.sem_inc(held_pool.up(times), 1)
                        for a in range(TOP):
                            nc.gpsimd.indirect_dma_start(
                                y_buf[:, a, :], None, slot_y,
                                bass.IndirectOffsetOnAxis(ap=index[:, a:a + 1], axis=0)).then_inc(y_in.up(times), 16)

                    def split(j, s, times):
                        n = 10 * j + 5 * s
                        pool.wait_ge(roped.sem, roped.at(2 * j + s + 1))
                        nc.gpsimd.tensor_tensor(whole[:, s], rope_a[:, s], rope_b[:, s], ALU.add
                                                ).then_inc(split_step.up(times), 1)
                        pool.wait_ge(parts_out.sem, parts_out.at(j))
                        nc.gpsimd.tensor_tensor(parts[:, s, 0, :], rope_a[:, s], rope_b[:, s], ALU.add
                                                ).then_inc(split_step.up(times), 1)
                        pool.wait_ge(split_step.sem, split_step.at(n + 2))
                        nc.gpsimd.tensor_tensor(rest[:, s], whole[:, s], parts[:, s, 0, :], ALU.subtract
                                                ).then_inc(split_step.up(times), 1)
                        pool.wait_ge(split_step.sem, split_step.at(n + 3))
                        pool.sem_inc(held_pool.up(times), 1)
                        nc.gpsimd.tensor_copy(parts[:, s, 1, :], rest[:, s]).then_inc(split_step.up(times), 1)
                        pool.wait_ge(split_step.sem, split_step.at(n + 4))
                        nc.gpsimd.tensor_tensor(parts[:, s, 2, :], rest[:, s], parts[:, s, 1, :], ALU.subtract
                                                ).then_inc(split_step.up(times), 1)

                    def place_v(j, b, times):
                        pool.wait_ge(v_staged.sem, v_staged.at(j + 1))
                        pool.wait_ge(attended.sem, attended.at(PAIRS * (j - 1) + 2 * b + 2))
                        pool.sem_inc(held_pool.up(times), 1)
                        for sc in range(2):
                            last = nc.gpsimd.tensor_copy(v_pad[:, b, :, sc, 0:C1],
                                                         v[:, sc, 64 * b:64 * b + 64].rearrange("p (h c) -> p h c", h=H1))
                        last.then_inc(v_placed.up(times), 1)

                    nc.gpsimd.memset(v_pad, 0.0).then_inc(ready.up(), 1)
                    pool.wait_ge(ready.sem, ready.at(1))
                    fetch(0, 1)
                    norm_pool(pool, 0, stats_in, norm_in, 1)
                    fetch(1, 1)
                    split(0, 0, 1)
                    split(0, 1, 1)
                    place_v(0, 0, 1)
                    norm_pool(pool, 1, stats_in, norm_in, 1)
                    split(1, 0, 1)
                    split(1, 1, 1)

                    def body(i, times, tail, qkv, norm):
                        place_v(i, 1, times)
                        if norm:
                            fetch(i + 2, times)
                        if tail:
                            norm_pool(pool, i - 1, stats_out, norm_out, times)
                            save_norm(pool, i - 1, xo, times)
                        if norm:
                            norm_pool(pool, i + 2, stats_in, norm_in, times)
                        if qkv:
                            place_v(i + 1, 0, times)
                        if norm:
                            split(i + 2, 0, times)
                            split(i + 2, 1, times)

                    over_tiles(pool, body)
                    norm_pool(pool, T - 1, stats_out, norm_out, 1)
                    save_norm(pool, T - 1, xo, 1)

                @block.tensor
                def _(pe):
                    def project_q(j, times):
                        pe.wait_ge(norm_in.done.sem, norm_in.done.at(j + 1))
                        if not isinstance(j, int) or j > 2:
                            pe.wait_ge(tile_done.sem, tile_done.at(j - 2))
                        nc.tensor.matmul(ps[:, MISC, 0:D], wq, xn, start=True, stop=True)
                        nc.tensor.matmul(ps[:, MISC, D:2 * D], wq_turned, xn, start=True, stop=True
                                         ).then_inc(q_projected.up(times), 1)

                    def project_k(j, times):
                        pe.wait_ge(ctx_in.sem, ctx_in.at(j + 1))
                        pe.wait_ge(roped.sem, roped.at(2 * j + 1))
                        nc.tensor.matmul(ps[:, MISC, 0:D], wk, ctx_t, start=True, stop=True)
                        nc.tensor.matmul(ps[:, MISC, D:2 * D], wk_turned, ctx_t, start=True, stop=True
                                         ).then_inc(k_projected.up(times), 1)

                    def project_v(j, times):
                        pe.wait_ge(roped.sem, roped.at(2 * j + 2))
                        for c in range(2):
                            mm = nc.tensor.matmul(ps[:, MISC, c * P:(c + 1) * P], ctx_t[:, c * P:(c + 1) * P], wv,
                                                  start=True, stop=True)
                        mm.then_inc(v_projected.up(times), 1)

                    def score(i, n, times):
                        b, half_of, c, N = n // 4, (n // 2) % 2, n % 2, UNITS * i + n
                        pe.wait_ge(stack_in[b].sem, stack_in[b].at(6 * i + 6))
                        pe.wait_ge(probs.sem, probs.at(N - 1))
                        for j in range(HH):
                            h = HH * half_of + j
                            mm = nc.tensor.matmul(ps[:, 2 * (n % 2) + j // 2, (j % 2) * D:(j % 2 + 1) * D],
                                                  q_stack[64 * b:64 * b + 64, h, c * P:(c + 1) * P],
                                                  k_stack[64 * b:64 * b + 64, h, :], start=True, stop=True)
                        mm.then_inc(scored.up(times), 1)

                    def turn_probs(i, n, times):
                        N = UNITS * i + n
                        pe.wait_ge(probs.sem, probs.at(N + 1))
                        for a, out_of in ((0, pT_out_dve), (1, pT_out_act)):
                            pe.wait_ge(out_of.sem, out_of.at(N))
                            for j in (2 * a, 2 * a + 1):
                                for sc in range(2):
                                    o = (2 * (j % 2) + sc) * P
                                    mm = nc.tensor.transpose(ps[:, TURNED + a, o:o + P], p[:, n % 2, j, sc, :], ident[:])
                            mm.then_inc(probs_by_bank[a].up(times), 1)

                    def attend(i, pair, times):
                        m, b, half_of = PAIRS * i + pair, pair // 2, pair % 2
                        pe.wait_ge(inv_ready.sem, inv_ready.at(2 * m + 2))
                        pe.wait_ge(attn_ready.sem, attn_ready.at(m))
                        for c in range(2):
                            nc.tensor.transpose(ps[:, PV, D + c * P:D + (c + 1) * P],
                                                inv_wide[:, c].rearrange("p h c -> p (h c)"), ident[:])
                        pe.wait_ge(pT_out_dve.sem, pT_out_dve.at(2 * m + 2))
                        pe.wait_ge(pT_out_act.sem, pT_out_act.at(2 * m + 2))
                        pe.wait_ge(v_placed.sem, v_placed.at(2 * i + b + 1))
                        for sc in range(2):
                            for j in range(HH):
                                mm = nc.tensor.matmul(ps[32 * j:32 * j + 32, PV, 0:D], v_pad[:, b, HH * half_of + j, sc, :],
                                                      pT[:, pair % 2, j, sc, :], start=(sc == 0), stop=(sc == 1),
                                                      skip_group_check=True)
                        mm.then_inc(attended.up(times), 1)

                    def project_out(i, times):
                        pe.wait_ge(attn_ready.sem, attn_ready.at(PAIRS * i + PAIRS))
                        pe.wait_ge(tile_done.sem, tile_done.at(i))
                        pe.wait_ge(v_staged.sem, v_staged.at(min(i + 3, T) if isinstance(i, int) else i + 3))
                        for n, (a, b) in enumerate(((0, 0), (1, 0), (0, 1), (1, 1))):
                            mm = nc.tensor.matmul(ps[:, MISC, 0:D], wo[:, a, b, :], attn[:, a, b, :],
                                                  start=(n == 0), stop=(n == 3))
                        mm.then_inc(out_made.up(times), 1)

                    def turn_out(i, times):
                        pe.wait_ge(norm_out.done.sem, norm_out.done.at(i + 1))
                        turn(pe, xo, MISC).then_inc(turned.up(times), 1)

                    def route_out(i, times):
                        pe.wait_ge(turned_out.sem, turned_out.at(i + 1))
                        for k in range(KC):
                            mm = nc.tensor.matmul(ps[:, MISC, 0:E], xT[:, k, :], router_w[:, layer, k, :],
                                                  start=(k == 0), stop=(k == KC - 1))
                        mm.then_inc(logits_made.up(times), 1)

                    pe.wait_ge(att_w_in.sem, att_w_in.at(6))
                    project_q(0, 1)
                    project_k(0, 1)
                    project_v(0, 1)
                    pe.wait_ge(v_staged.sem, v_staged.at(1))
                    project_q(1, 1)
                    project_k(1, 1)
                    score(0, 0, 1)
                    score(0, 1, 1)

                    def body(i, times, tail, qkv, norm):
                        for n in range(UNITS):
                            turn_probs(i, n, times)
                            if n < UNITS - 2:
                                score(i, n + 2, times)
                            elif qkv:
                                score(i + 1, n + 2 - UNITS, times)
                            if n == 0 and tail:
                                attend(i - 1, PAIRS - 1, times)
                            elif n and n % 2 == 0:
                                attend(i, n // 2 - 1, times)
                            if qkv and n == 1:
                                project_v(i + 1, times)
                            if tail and n == 2:
                                project_out(i - 1, times)
                            if tail and n == 4:
                                turn_out(i - 1, times)
                            if tail and n == 5:
                                route_out(i - 1, times)
                            if norm and n == 6:
                                project_q(i + 2, times)
                            if norm and n == 7:
                                project_k(i + 2, times)

                    over_tiles(pe, body)
                    attend(T - 1, PAIRS - 1, 1)
                    project_out(T - 1, 1)
                    turn_out(T - 1, 1)
                    route_out(T - 1, 1)

                @block.scalar
                def _(act):
                    def exps(i, n, times):
                        N = UNITS * i + n
                        act.wait_ge(shifted.sem, shifted.at(N + 1))
                        act.wait_ge(probs_by_bank[1].sem, probs_by_bank[1].at(N - 1))
                        act.wait_ge(inv_ready.sem, inv_ready.at(N - 1))
                        for j in range(HH):
                            last = nc.scalar.activation(
                                p[:, n % 2, j].rearrange("p s n -> p (s n)"),
                                ps[:, 2 * (n % 2) + j // 2, (j % 2) * D:(j % 2 + 1) * D], ACT.Exp,
                                bias=neg_max[:, n % 2, j:j + 1], accum_out=sums[:, n % 2, j:j + 1])
                        last.then_inc(probs.up(times), 1)

                    def take_turned(i, n, times):
                        N, m, c = UNITS * i + n, PAIRS * i + n // 2, n % 2
                        act.wait_ge(probs_by_bank[1].sem, probs_by_bank[1].at(N + 1))
                        act.wait_ge(attended.sem, attended.at(m - 1))
                        nc.scalar.copy(pT[:, (n // 2) % 2, 2:4, :, c * P:(c + 1) * P].rearrange("p h s n -> p (h s) n"),
                                       ps[:, TURNED + 1, :].rearrange("p (j n) -> p j n", n=P)
                                       ).then_inc(pT_out_act.up(times), 1)

                    def take_inv(i, pair, times):
                        m = PAIRS * i + pair
                        act.wait_ge(attended.sem, attended.at(m + 1))
                        nc.scalar.copy(inv_T, ps[:, PV, D:2 * D]).then_inc(inv_out.up(times), 1)

                    def take_turned_out(i, times):
                        act.wait_ge(turned.sem, turned.at(i + 1))
                        act.wait_ge(logits_made.sem, logits_made.at(i))
                        nc.scalar.copy(xT.rearrange("p k t -> p (k t)"), ps[:, MISC, 0:2 * P]
                                       ).then_inc(turned_out.up(times), 1)

                    nc.scalar.activation(table_call[:], half[:], ACT.Exp)
                    exps(0, 0, 1)

                    def body(i, times, tail, qkv, norm):
                        for n in range(UNITS):
                            if n < UNITS - 1:
                                exps(i, n + 1, times)
                            elif qkv:
                                exps(i + 1, 0, times)
                            take_turned(i, n, times)
                            if n == 0 and tail:
                                take_inv(i - 1, PAIRS - 1, times)
                            elif n and n % 2 == 0:
                                take_inv(i, n // 2 - 1, times)
                            if tail and n == 4:
                                take_turned_out(i - 1, times)

                    over_tiles(act, body)
                    take_inv(T - 1, PAIRS - 1, 1)
                    take_turned_out(T - 1, 1)

                @block.vector
                def _(dve):
                    def enter(j, times):
                        dve.wait_ge(y_in.sem, y_in.at(TOP * j + TOP))
                        nc.vector.scalar_tensor_tensor(
                            out=x[:, j, :], in0=y_buf[:, 0, :], scalar=weight[:, 0, bass.ds(j, 1)], in1=x[:, j, :],
                            op0=ALU.mult, op1=ALU.add).then_inc(half_added.up(times), 1)
                        dve.wait_ge(half_added.sem, half_added.at(j + 1))
                        nc.vector.scalar_tensor_tensor(
                            out=x[:, j, :], in0=y_buf[:, 1, :], scalar=weight[:, 1, bass.ds(j, 1)], in1=x[:, j, :],
                            op0=ALU.mult, op1=ALU.add).then_inc(added.up(times), 1)
                        dve.wait_ge(added.sem, added.at(j + 1))
                        norm_stats(dve, j, x[:, j, :], stats_in, norm_in, times)

                    def enter_apply(j, times):
                        dve.wait_ge(q_projected.sem, q_projected.at(j))
                        norm_apply(dve, j, x[:, j, :], xn, stats_in, norm_in, times)

                    def rope(j, s, times):
                        made = (q_projected, k_projected)[s]
                        b_name, c_name, s_name = (("bq", "cos_q", "sin_q"), ("bk", "cos_k", "sin_k"))[s]
                        dve.wait_ge(made.sem, made.at(j + 1))
                        if not isinstance(j, int) or j > 0:
                            dve.wait_ge(split_step.sem, split_step.at(10 * (j - 1) + 5 * s + 2))
                        nc.vector.scalar_tensor_tensor(out=rope_a[:, s], in0=ps[:, MISC, 0:D], scalar=col(b_name, 0),
                                                       in1=row(c_name), op0=ALU.add, op1=ALU.mult)
                        nc.vector.scalar_tensor_tensor(out=rope_b[:, s], in0=ps[:, MISC, D:2 * D], scalar=col(b_name, 1),
                                                       in1=row(s_name), op0=ALU.add, op1=ALU.mult
                                                       ).then_inc(roped.up(times), 1)

                    def stage_v(j, times):
                        dve.wait_ge(v_projected.sem, v_projected.at(j + 1))
                        dve.wait_ge(v_placed.sem, v_placed.at(2 * j))
                        nc.vector.tensor_tensor(v, ps[:, MISC, 0:2 * P].rearrange("p (s n) -> p s n", s=2),
                                                row("bv").unsqueeze(1).to_broadcast([P, 2, P]), ALU.add
                                                ).then_inc(v_staged.up(times), 1)

                    def find_max(i, n, times):
                        N = UNITS * i + n
                        dve.wait_ge(scored.sem, scored.at(N + 1))
                        b0 = 2 * (n % 2)
                        nc.vector.tensor_reduce(neg_max[:, n % 2], ps[:, b0:b0 + 2, :].rearrange("p a (h s) -> p (a h) s", h=2),
                                                AX.X, ALU.max, negate=True).then_inc(shifted.up(times), 1)

                    def invert(i, n, times):
                        N, m, c = UNITS * i + n, PAIRS * i + n // 2, n % 2
                        dve.wait_ge(probs.sem, probs.at(N + 1))
                        nc.vector.reciprocal(inv[:, c], sums[:, c]).then_inc(inv_made.up(times), 1)
                        dve.wait_ge(inv_made.sem, inv_made.at(N + 1))
                        dve.wait_ge(attended.sem, attended.at(m))
                        nc.vector.tensor_copy(inv_wide[:, c], inv[:, c].unsqueeze(2).to_broadcast([P, HH, 32])
                                              ).then_inc(inv_ready.up(times), 1)

                    def take_turned(i, n, times):
                        N, m, c = UNITS * i + n, PAIRS * i + n // 2, n % 2
                        dve.wait_ge(probs_by_bank[0].sem, probs_by_bank[0].at(N + 1))
                        dve.wait_ge(attended.sem, attended.at(m - 1))
                        nc.vector.tensor_copy(pT[:, (n // 2) % 2, 0:2, :, c * P:(c + 1) * P].rearrange("p h s n -> p (h s) n"),
                                              ps[:, TURNED, :].rearrange("p (j n) -> p j n", n=P)
                                              ).then_inc(pT_out_dve.up(times), 1)

                    def normalise(i, pair, times):
                        m = PAIRS * i + pair
                        dve.wait_ge(inv_out.sem, inv_out.at(m + 1))
                        dve.wait_ge(out_made.sem, out_made.at(i))
                        nc.vector.tensor_tensor(attn[:, pair % 2, pair // 2], ps[:, PV, 0:D], inv_T, ALU.mult
                                                ).then_inc(attn_ready.up(times), 1)

                    def leave(i, times):
                        dve.wait_ge(out_made.sem, out_made.at(i + 1))
                        nc.vector.tensor_scalar(tmp, ps[:, MISC, 0:D], col("bo"), gain[:, layer:layer + 1],
                                                ALU.add, ALU.mult).then_inc(gate_step.up(times), 1)
                        dve.wait_ge(gate_step.sem, gate_step.at(i + 1))
                        nc.vector.tensor_tensor(x[:, i, :], x[:, i, :], tmp, ALU.add).then_inc(proj_exp.up(times), 1)
                        dve.wait_ge(proj_exp.sem, proj_exp.at(i + 1))
                        norm_stats(dve, i, x[:, i, :], stats_out, norm_out, times)

                    def leave_apply(i, times):
                        dve.wait_ge(saved.sem, saved.at(i))
                        dve.wait_ge(turned.sem, turned.at(i))
                        norm_apply(dve, i, x[:, i, :], xo, stats_out, norm_out, times)

                    def take_logits(i, times):
                        dve.wait_ge(logits_made.sem, logits_made.at(i + 1))
                        nc.vector.tensor_copy(logits[:, i, :], ps[:, MISC, 0:E]).then_inc(tile_done.up(times), 1)

                    enter(0, 1)
                    enter_apply(0, 1)
                    rope(0, 0, 1)
                    rope(0, 1, 1)
                    stage_v(0, 1)
                    enter(1, 1)
                    enter_apply(1, 1)
                    rope(1, 0, 1)
                    rope(1, 1, 1)
                    find_max(0, 0, 1)
                    find_max(0, 1, 1)

                    def body(i, times, tail, qkv, norm):
                        for n in range(UNITS):
                            take_turned(i, n, times)
                            if n < UNITS - 2:
                                find_max(i, n + 2, times)
                            elif qkv:
                                find_max(i + 1, n + 2 - UNITS, times)
                            invert(i, n, times)
                            if n == 1 and tail:
                                normalise(i - 1, PAIRS - 1, times)
                            elif n % 2 == 1 and n > 1:
                                normalise(i, (n - 3) // 2, times)
                            if qkv and n == 1:
                                stage_v(i + 1, times)
                            if tail and n == 2:
                                leave(i - 1, times)
                            if tail and n == 3:
                                leave_apply(i - 1, times)
                            if norm and n == 4:
                                enter(i + 2, times)
                            if norm and n == 5:
                                enter_apply(i + 2, times)
                            if tail and n == 5:
                                take_logits(i - 1, times)
                            if norm and n == 6:
                                rope(i + 2, 0, times)
                            if norm and n == 7:
                                rope(i + 2, 1, times)

                    over_tiles(dve, body)
                    normalise(T - 1, PAIRS - 1, 1)
                    leave(T - 1, 1)
                    leave_apply(T - 1, 1)
                    take_logits(T - 1, 1)
            end_stage()

        def attention2():
            used[0] = 0
            layer = 2
            w_in = att_w[:, 0:2 * D].rearrange("p (k n) -> p k n", k=KC)
            w_out = att_w[:, 2 * D:4 * D].rearrange("p (k n) -> p k n", k=KC)
            pick = att_w[:, 4 * D:4 * D + L]
            lanes = range(LANES)
            GROUPS = T // LANES
            stats = [carve_stats() for _ in lanes]
            index, y_buf = [carve(TOP).bitcast(U32) for _ in lanes], [carve(TOP, D) for _ in lanes]
            xn, xT = [carve(D) for _ in lanes], [carve(KC, P) for _ in lanes]
            y2, tmp = [carve(D) for _ in lanes], [carve(D) for _ in lanes]
            state_tok = [carve(KC, 2, L) for _ in lanes]
            ctx_all = carve(T, D)
            keep = carve(1)
            geo, geo_in = carve(L), carve(L)
            decay_sum, total = carve(1), carve(1)
            by_batch = carve(2)
            bias = carve(KC)
            ctx_sum = carve(KC, B)
            state = carve(KC, B)
            n = [0]
            SUM, STATE = 4, 6

            def nth(of, s, g, u):
                return (of * g + s) * LANES + u + 1

            with nc.Block() as block:
                @block.sync
                def _(sp):
                    sp.dma_start(pick, d["pick"]).then_inc(att_w_in.up(), 16)
                    sp.dma_start(ctx_all, d["ctx"].rearrange("t p n -> p t n")).then_inc(ctx_in.up(), 16)
                    for buf, name in ((w_in, "w_in2"), (w_out, "w_out2")):
                        sp.dma_start(buf, d[name].rearrange("(k p) n -> p k n", p=P)).then_inc(att_w_in.up(), 16)
                    load_ffn(sp, layer)

                @block.gpsimd
                def _(pool):
                    def fetch(g, u, times):
                        j = LANES * g + u
                        if not isinstance(g, int) or g > 0:
                            pool.wait_ge(added.sem, added.at(j - LANES + 1))
                        nc.gpsimd.tensor_copy(index[u], slots[:, :, bass.ds(j, 1)].rearrange("p a b -> p (a b)")
                                              ).then_inc(index_ready.up(times), 1)
                        pool.wait_ge(index_ready.sem, index_ready.at(j + 1))
                        pool.sem_inc(held_pool.up(times), 1)
                        for a in range(TOP):
                            nc.gpsimd.indirect_dma_start(
                                y_buf[u][:, a, :], None, slot_y,
                                bass.IndirectOffsetOnAxis(ap=index[u][:, a:a + 1], axis=0)).then_inc(y_in_lane[u].up(times), 16)

                    def body(g, times, more):
                        for k, norm in enumerate((norm_in, norm_mid, norm_out)):
                            for u in lanes:
                                norm_pool(pool, LANES * g + u, stats[u], norm, times)
                            if more and k < 2:
                                for u in (2 * k, 2 * k + 1):
                                    fetch(g + 1, u, times)
                        for u in lanes:
                            save_norm(pool, LANES * g + u, xn[u], times)

                    for u in lanes:
                        fetch(0, u, 1)
                    with pool.Fori(0, GROUPS - 1) as g:
                        body(g, GROUPS - 1, True)
                    body(GROUPS - 1, 1, False)

                @block.tensor
                def _(pe):
                    pe.wait_ge(att_w_in.sem, att_w_in.at(3))
                    pe.wait_ge(masked.sem, masked.at(1))
                    pe.wait_ge(ctx_in.sem, ctx_in.at(1))
                    for t in range(T):
                        for k in range(KC):
                            mm = nc.tensor.matmul(ps[:, SUM + k, 2 * t:2 * t + 2], ctx_all[:, t, k * P:(k + 1) * P], by_batch,
                                                  start=True, stop=True)
                    mm.then_inc(scored.up(), 1)
                    pe.wait_ge(shifted.sem, shifted.at(1))
                    for g in range(KC):
                        for k in range(KC):
                            mm = nc.tensor.matmul(ps[:, STATE, g * B:(g + 1) * B], w_in[:, k, g * P:(g + 1) * P],
                                                  ctx_sum[:, k, :], start=(k == 0), stop=(k == KC - 1))
                    mm.then_inc(projected.up(), 1)
                    with pe.Fori(0, GROUPS) as g:
                        for u in lanes:
                            pe.wait_ge(attn_ready.sem, attn_ready.at(LANES * g + u + 1))
                            pe.wait_ge(tile_done.sem, tile_done.at(LANES * (g - 1) + u + 1))
                            for k in range(KC):
                                mm = nc.tensor.matmul(ps[:, u, 0:D], state_tok[u][:, k].rearrange("p b l -> p (b l)"),
                                                      w_out[:, k, :], start=(k == 0), stop=(k == KC - 1))
                            mm.then_inc(out_made.up(T // LANES), 1)
                        for u in lanes:
                            pe.wait_ge(norm_out.done.sem, norm_out.done.at(LANES * g + u + 1))
                            turn(pe, xn[u], u).then_inc(turned.up(T // LANES), 1)
                        for u in lanes:
                            pe.wait_ge(turned_out.sem, turned_out.at(LANES * g + u + 1))
                            for k in range(KC):
                                mm = nc.tensor.matmul(ps[:, u, 0:E], xT[u][:, k, :], router_w[:, layer, k, :],
                                                      start=(k == 0), stop=(k == KC - 1))
                            mm.then_inc(logits_made.up(T // LANES), 1)

                @block.scalar
                def _(act):
                    nc.scalar.activation(keep, col("decay"), ACT.Exp, scale=-1.0).then_inc(probs.up(), 1)
                    with act.Fori(0, GROUPS) as g:
                        for u in lanes:
                            act.wait_ge(turned.sem, turned.at(LANES * g + u + 1))
                            nc.scalar.copy(xT[u].rearrange("p k t -> p (k t)"), ps[:, u, 0:2 * P]
                                           ).then_inc(turned_out.up(T // LANES), 1)

                @block.vector
                def _(dve):
                    def then(ins):
                        n[0] += 1
                        ins.then_inc(step.up(), 1)
                        dve.wait_ge(step.sem, step.at(n[0]))

                    dve.wait_ge(probs.sem, probs.at(1))
                    dve.wait_ge(att_w_in.sem, att_w_in.at(3))
                    then(nc.vector.tensor_scalar(keep, keep, 1.0, None, ALU.add))
                    then(nc.vector.reciprocal(keep, keep))
                    then(nc.vector.tensor_copy(geo_in, keep.to_broadcast([P, L])))
                    then(nc.vector.tensor_tensor_scan(geo, geo_in, ones[:, 0:L], 0.0, ALU.mult, ALU.add))
                    then(nc.vector.tensor_reduce(total, geo, AX.X, ALU.add))
                    then(nc.vector.tensor_tensor(geo_in, geo, pick, ALU.mult))
                    then(nc.vector.tensor_reduce(decay_sum, geo_in, AX.X, ALU.add))
                    nc.vector.tensor_scalar(by_batch, col("batch_of", 0, 2), decay_sum, None, ALU.mult
                                            ).then_inc(masked.up(), 1)
                    then(nc.vector.tensor_scalar(bias, col("b_in", 0, 2), total, None, ALU.mult))
                    dve.wait_ge(scored.sem, scored.at(1))
                    nc.vector.tensor_copy(ctx_sum, ps[:, SUM:SUM + 2, 0:B]).then_inc(shifted.up(), 1)
                    dve.wait_ge(projected.sem, projected.at(1))
                    for k in range(KC):
                        last = nc.vector.tensor_scalar(state[:, k, :], ps[:, STATE, k * B:(k + 1) * B], bias[:, k:k + 1],
                                                       1.0 / L, ALU.add, ALU.mult)
                    then(last)

                    times = GROUPS
                    with dve.Fori(0, GROUPS) as g:
                        def tile(u):
                            return LANES * g + u

                        def x_of(u):
                            return x[:, LANES * g + u, :]

                        def stats_of(src, norm):
                            for u in lanes:
                                dve.sem_inc(held_dve.up(times), 1)
                                nc.vector.bn_stats(stats[u]["bn"], src(u)).then_inc(norm.stats.up(times), 1)
                            for u in lanes:
                                dve.wait_ge(norm.stats.sem, norm.stats.at(tile(u) + 1))
                                dve.sem_inc(held_dve.up(times), 1)
                                nc.vector.bn_aggr(stats[u]["mv"], stats[u]["bn"]).then_inc(norm.mean.up(times), 1)
                            for u in lanes:
                                dve.wait_ge(norm.mean.sem, norm.mean.at(tile(u) + 1))
                                nc.vector.tensor_scalar(stats[u]["var"], stats[u]["mv"][:, 1:2], LN_EPS, None, ALU.add
                                                        ).then_inc(norm.var.up(times), 1)

                        for u in lanes:
                            nc.vector.tensor_copy(
                                state_tok[u], state[:, :, bass.ds(2 * tile(u), 2)].unsqueeze(3).to_broadcast([P, KC, 2, L])
                            ).then_inc(attn_ready.up(times), 1)
                        for u in lanes:
                            dve.wait_ge(y_in_lane[u].sem, y_in_lane[u].at(TOP * g + TOP))
                            nc.vector.scalar_tensor_tensor(
                                out=x_of(u), in0=y_buf[u][:, 0, :], scalar=weight[:, 0, bass.ds(tile(u), 1)], in1=x_of(u),
                                op0=ALU.mult, op1=ALU.add).then_inc(half_added.up(times), 1)
                        for u in lanes:
                            dve.wait_ge(half_added.sem, half_added.at(tile(u) + 1))
                            nc.vector.scalar_tensor_tensor(
                                out=x_of(u), in0=y_buf[u][:, 1, :], scalar=weight[:, 1, bass.ds(tile(u), 1)], in1=x_of(u),
                                op0=ALU.mult, op1=ALU.add).then_inc(added.up(times), 1)
                        dve.wait_ge(added.sem, added.at(tile(LANES)))
                        stats_of(x_of, norm_in)
                        dve.wait_ge(saved.sem, saved.at(tile(0)))
                        for u in lanes:
                            norm_apply(dve, tile(u), x_of(u), xn[u], stats[u], norm_in, times)
                        for u in lanes:
                            dve.wait_ge(norm_in.done.sem, norm_in.done.at(tile(u) + 1))
                            nc.vector.tensor_tensor(y2[u], xn[u], row("b_out"), ALU.add).then_inc(gate_step.up(times), 1)
                        for u in lanes:
                            dve.wait_ge(gate_step.sem, gate_step.at(nth(4, 0, g, u)))
                            dve.wait_ge(out_made.sem, out_made.at(tile(u) + 1))
                            nc.vector.tensor_tensor(y2[u], y2[u], ps[:, u, 0:D], ALU.add).then_inc(gate_step.up(times), 1)
                        dve.wait_ge(gate_step.sem, gate_step.at(nth(4, 1, g, LANES - 1)))
                        stats_of(lambda u: y2[u], norm_mid)
                        for u in lanes:
                            norm_apply(dve, tile(u), y2[u], tmp[u], stats[u], norm_mid, times)
                        for u in lanes:
                            dve.wait_ge(norm_mid.done.sem, norm_mid.done.at(tile(u) + 1))
                            nc.vector.tensor_tensor(tmp[u], tmp[u], row("gamma"), ALU.mult).then_inc(gate_step.up(times), 1)
                        for u in lanes:
                            dve.wait_ge(gate_step.sem, gate_step.at(nth(4, 2, g, u)))
                            nc.vector.tensor_tensor(tmp[u], tmp[u], row("beta"), ALU.add).then_inc(gate_step.up(times), 1)
                        for u in lanes:
                            dve.wait_ge(gate_step.sem, gate_step.at(nth(4, 3, g, u)))
                            nc.vector.scalar_tensor_tensor(out=x_of(u), in0=tmp[u], scalar=gain[:, layer:layer + 1],
                                                           in1=x_of(u), op0=ALU.mult, op1=ALU.add
                                                           ).then_inc(proj_exp.up(times), 1)
                        dve.wait_ge(proj_exp.sem, proj_exp.at(tile(LANES)))
                        stats_of(x_of, norm_out)
                        for u in lanes:
                            norm_apply(dve, tile(u), x_of(u), xn[u], stats[u], norm_out, times)
                        for u in lanes:
                            dve.wait_ge(logits_made.sem, logits_made.at(tile(u) + 1))
                            nc.vector.tensor_copy(logits[:, tile(u), :], ps[:, u, 0:E]).then_inc(tile_done.up(times), 1)
            end_stage()

        def attention3():
            used[0] = 0
            layer = 3
            wq = att_w[:, 0:2 * D].rearrange("p (k n) -> p k n", k=KC)
            wk = att_w[:, 2 * D:4 * D].rearrange("p (k n) -> p k n", k=KC)
            wfc = att_w[:, 4 * D:6 * D].rearrange("p (k n) -> p k n", k=KC)
            NV = G3 * C3
            wv = att_w[:, 6 * D:6 * D + KC * NV].rearrange("p (k n) -> p k n", k=KC)
            stats_in, stats_out = carve_stats(), carve_stats()
            index, y_buf = carve(TOP).bitcast(U32), carve(TOP, D)
            xn, xo, xT, xoT, cT = carve(D), carve(D), carve(KC, P), carve(KC, P), carve(KC, P)
            qT, kT = carve(KC, P), carve(KC, P)
            HG = P // C3
            k_head = carve(KC, 2, HG, L)
            v = carve(NV)
            v_pair = carve(G3, 2, 2, C3 + 1)
            mx = carve(KC, HG)
            p = carve(KC, HG, L)
            pT = carve(KC, HG // 2, P)
            inv = carve(KC, HG)
            o, oT = carve(KC, HG, C3), carve(KC, P)
            tmp = carve(D)
            W = 4 * (C3 + 1)
            TURNED, PV, MISC, SCORES = 0, 2, 3, 4
            SC = float(1.0 / np.sqrt(C3))
            BODIES = T - 3

            def over_tiles(eng, body):
                body(0, 1, tail=False, qkv=True, norm=True)
                with eng.Fori(1, T - 2) as i:
                    body(i, BODIES, tail=True, qkv=True, norm=True)
                body(T - 2, 1, tail=True, qkv=True, norm=False)
                body(T - 1, 1, tail=True, qkv=False, norm=False)

            with nc.Block() as block:
                @block.sync
                def _(sp):
                    def load_ctx(j, times):
                        sp.wait_ge(v_projected.sem, v_projected.at(j))
                        sp.dma_start(cT, d["ctxT"][j]).then_inc(ctx_in.up(times), 16)

                    for buf, name in ((wq, "wq3"), (wk, "wk3"), (wfc, "wfc3"), (wv, "wv3")):
                        sp.dma_start(buf, d[name].rearrange("(k p) n -> p k n", p=P)).then_inc(att_w_in.up(), 16)
                    load_ctx(0, 1)
                    load_ffn(sp, layer)
                    sp.dma_start(shared_up, d["shared_up"].rearrange("(k p) n -> p k n", p=P)).then_inc(ffn_w_in.up(), 16)
                    for c, n in chunks(SHARED):
                        sp.dma_start(shared_down[0:n, c, :], d["shared_down"][c * P:c * P + n, :]).then_inc(ffn_w_in.up(), 16)
                    load_ctx(1, 1)
                    with sp.Fori(2, T) as j:
                        load_ctx(j, T - 2)

                @block.gpsimd
                def _(pool):
                    def fetch(j, times):
                        pool.wait_ge(added.sem, added.at(j))
                        nc.gpsimd.tensor_copy(index, slots[:, :, bass.ds(j, 1)].rearrange("p a b -> p (a b)")
                                              ).then_inc(index_ready.up(times), 1)
                        pool.wait_ge(index_ready.sem, index_ready.at(j + 1))
                        pool.sem_inc(held_pool.up(times), 1)
                        for a in range(TOP):
                            nc.gpsimd.indirect_dma_start(
                                y_buf[:, a, :], None, slot_y,
                                bass.IndirectOffsetOnAxis(ap=index[:, a:a + 1], axis=0)).then_inc(y_in.up(times), 16)

                    fetch(0, 1)
                    norm_pool(pool, 0, stats_in, norm_in, 1)
                    fetch(1, 1)
                    norm_pool(pool, 1, stats_in, norm_in, 1)

                    def body(i, times, tail, qkv, norm):
                        if norm:
                            fetch(i + 2, times)
                        if tail:
                            norm_pool(pool, i - 1, stats_out, norm_out, times)
                            save_norm(pool, i - 1, xo, times)
                        if norm:
                            norm_pool(pool, i + 2, stats_in, norm_in, times)

                    over_tiles(pool, body)
                    norm_pool(pool, T - 1, stats_out, norm_out, 1)
                    save_norm(pool, T - 1, xo, 1)

                @block.tensor
                def _(pe):
                    def turn_in(j, times):
                        pe.wait_ge(norm_in.done.sem, norm_in.done.at(j + 1))
                        if not isinstance(j, int) or j > 2:
                            pe.wait_ge(tile_done.sem, tile_done.at(j - 2))
                        turn(pe, xn, MISC).then_inc(xT_made.up(times), 1)

                    def project_qk(j, times):
                        pe.wait_ge(ctx_in.sem, ctx_in.at(j + 1))
                        pe.wait_ge(xT_ready.sem, xT_ready.at(j + 1))
                        for w, src, at in ((wq, xT, 0), (wk, cT, D)):
                            for g in range(KC):
                                for k in range(KC):
                                    mm = nc.tensor.matmul(ps[:, MISC, at + g * P:at + (g + 1) * P],
                                                          w[:, k, g * P:(g + 1) * P], src[:, k, :],
                                                          start=(k == 0), stop=(k == KC - 1))
                        mm.then_inc(projected.up(times), 1)

                    def project_v(j, times):
                        pe.wait_ge(proj_out.sem, proj_out.at(j + 1))
                        for k in range(KC):
                            mm = nc.tensor.matmul(ps[:, MISC, 0:NV], cT[:, k, :], wv[:, k, :],
                                                  start=(k == 0), stop=(k == KC - 1))
                        mm.then_inc(v_projected.up(times), 1)

                    def score(i, g, times):
                        pe.wait_ge(masked.sem, masked.at(i + 1))
                        pe.wait_ge(masked_act.sem, masked_act.at(i + 1))
                        pe.wait_ge(shifted.sem, shifted.at(2 * i + g - 1))
                        for b in range(2):
                            for a in range(2):
                                mm = nc.tensor.matmul(
                                    ps[b * L:(b + 1) * L, SCORES + 2 * g + a, :], qT[:, g, b * L:(b + 1) * L],
                                    k_head[:, g, b, a * 8:(a + 1) * 8, :].rearrange("p h s -> p (h s)"),
                                    start=True, stop=True)
                        mm.then_inc(scored.up(times), 1)

                    def turn_probs(i, g, times):
                        N = 2 * i + g
                        pe.wait_ge(probs.sem, probs.at(N + 1))
                        for a, out_of in ((0, pT_out_dve), (1, pT_out_act)):
                            pe.wait_ge(out_of.sem, out_of.at(N))
                            for j in range(4):
                                h = 8 * a + 2 * j
                                mm = nc.tensor.transpose(ps[:, TURNED + a, j * P:(j + 1) * P],
                                                         p[:, g, h:h + 2, :].rearrange("p h s -> p (h s)"), ident[:])
                            mm.then_inc(probs_by_bank[a].up(times), 1)

                    def attend(i, g, times):
                        N = 2 * i + g
                        pe.wait_ge(pT_out_dve.sem, pT_out_dve.at(N + 1))
                        pe.wait_ge(pT_out_act.sem, pT_out_act.at(N + 1))
                        pe.wait_ge(v_placed.sem, v_placed.at(i + 1))
                        pe.wait_ge(attn_ready.sem, attn_ready.at(N))
                        for j in range(HG // 2):
                            mm = nc.tensor.matmul(ps[:, PV, j * W:(j + 1) * W], pT[:, g, j, :],
                                                  v_pair[:, (HG // 2 * g + j) // 2].rearrange("p b h c -> p (b h c)"),
                                                  start=True, stop=True)
                        mm.then_inc(attended.up(times), 1)

                    def turn_o(i, after, times):
                        pe.wait_ge(attn_ready.sem, attn_ready.at(2 * i + 2))
                        pe.wait_ge(v_staged.sem, v_staged.at(after + 1))
                        pe.wait_ge(tile_done.sem, tile_done.at(i))
                        turn(pe, o.rearrange("p g h c -> p (g h c)"), MISC).then_inc(o_turned.up(times), 1)

                    def project_out(i, times):
                        pe.wait_ge(oT_ready.sem, oT_ready.at(i + 1))
                        for k in range(KC):
                            mm = nc.tensor.matmul(ps[:, MISC, 0:D], oT[:, k, :], wfc[:, k, :], start=(k == 0), stop=(k == KC - 1))
                        mm.then_inc(out_made.up(times), 1)

                    def route_out(i, times):
                        pe.wait_ge(norm_out.done.sem, norm_out.done.at(i + 1))
                        turn(pe, xo, MISC).then_inc(turned.up(times), 1)
                        pe.wait_ge(turned_out.sem, turned_out.at(i + 1))
                        for k in range(KC):
                            mm = nc.tensor.matmul(ps[:, MISC, 0:E], xoT[:, k, :], router_w[:, layer, k, :],
                                                  start=(k == 0), stop=(k == KC - 1))
                        mm.then_inc(logits_made.up(times), 1)

                    pe.wait_ge(att_w_in.sem, att_w_in.at(4))
                    turn_in(0, 1)
                    project_qk(0, 1)
                    project_v(0, 1)
                    score(0, 0, 1)

                    def body(i, times, tail, qkv, norm):
                        if qkv:
                            pe.wait_ge(v_staged.sem, v_staged.at(i + 1))
                            turn_in(i + 1, times)
                        score(i, 1, times)
                        if qkv:
                            project_qk(i + 1, times)
                        turn_probs(i, 0, times)
                        attend(i, 0, times)
                        if qkv:
                            project_v(i + 1, times)
                        if tail:
                            turn_o(i - 1, i + 1 if qkv else i, times)
                        if qkv:
                            score(i + 1, 0, times)
                        if tail:
                            project_out(i - 1, times)
                        turn_probs(i, 1, times)
                        attend(i, 1, times)
                        if tail:
                            route_out(i - 1, times)

                    over_tiles(pe, body)
                    turn_o(T - 1, T - 1, 1)
                    project_out(T - 1, 1)
                    route_out(T - 1, 1)

                @block.scalar
                def _(act):
                    def flat(t):
                        return t.rearrange("p k t -> p (k t)")

                    def take_in(j, times):
                        act.wait_ge(xT_made.sem, xT_made.at(j + 1))
                        nc.scalar.copy(flat(xT), ps[:, MISC, 0:D]).then_inc(xT_ready.up(times), 1)

                    def take_qk(j, times):
                        act.wait_ge(projected.sem, projected.at(j + 1))
                        act.wait_ge(masked.sem, masked.at(j))
                        nc.scalar.copy(flat(kT), ps[:, MISC, D:2 * D]).then_inc(k_out.up(times), 1)
                        act.wait_ge(scored.sem, scored.at(2 * j))
                        nc.scalar.copy(flat(qT), ps[:, MISC, 0:D]).then_inc(proj_out.up(times), 1)

                    def spread_k(j, times):
                        act.wait_ge(k_out.sem, k_out.at(j + 1))
                        for h in range(10, HG):
                            last = nc.scalar.mul(k_head[:, :, :, h, :], kT.rearrange("p g (b s) -> p g b s", b=2),
                                                 col("mask3", h))
                        last.then_inc(masked_act.up(times), 1)

                    def exps(i, g, times):
                        act.wait_ge(shifted.sem, shifted.at(2 * i + g + 1))
                        one = p[:, g].rearrange("p h s -> p (h s)")
                        nc.scalar.activation(one, one, ACT.Exp, scale=SC).then_inc(probs.up(times), 1)

                    def take_turned(i, g, times):
                        N = 2 * i + g
                        act.wait_ge(probs_by_bank[1].sem, probs_by_bank[1].at(N + 1))
                        act.wait_ge(attended.sem, attended.at(N - 1))
                        nc.scalar.copy(pT[:, g, 4:8, :], ps[:, TURNED + 1, :].rearrange("p (j n) -> p j n", n=P)
                                       ).then_inc(pT_out_act.up(times), 1)

                    def take_o(i, times):
                        act.wait_ge(o_turned.sem, o_turned.at(i + 1))
                        act.wait_ge(out_made.sem, out_made.at(i))
                        nc.scalar.copy(flat(oT), ps[:, MISC, 0:D]).then_inc(oT_ready.up(times), 1)

                    def take_turned_out(i, times):
                        act.wait_ge(turned.sem, turned.at(i + 1))
                        act.wait_ge(logits_made.sem, logits_made.at(i))
                        nc.scalar.copy(flat(xoT), ps[:, MISC, 0:D]).then_inc(turned_out.up(times), 1)

                    nc.scalar.activation(table_call[:], half[:], ACT.Exp)
                    take_in(0, 1)
                    take_qk(0, 1)
                    spread_k(0, 1)
                    exps(0, 0, 1)

                    def body(i, times, tail, qkv, norm):
                        if qkv:
                            take_in(i + 1, times)
                            take_qk(i + 1, times)
                        exps(i, 1, times)
                        take_turned(i, 0, times)
                        if qkv:
                            spread_k(i + 1, times)
                        if tail:
                            take_o(i - 1, times)
                        take_turned(i, 1, times)
                        if qkv:
                            exps(i + 1, 0, times)
                        if tail:
                            take_turned_out(i - 1, times)

                    over_tiles(act, body)
                    take_o(T - 1, 1)
                    take_turned_out(T - 1, 1)

                @block.vector
                def _(dve):
                    def enter(j, times):
                        dve.wait_ge(y_in.sem, y_in.at(TOP * j + TOP))
                        nc.vector.scalar_tensor_tensor(
                            out=x[:, j, :], in0=y_buf[:, 0, :], scalar=weight[:, 0, bass.ds(j, 1)], in1=x[:, j, :],
                            op0=ALU.mult, op1=ALU.add).then_inc(half_added.up(times), 1)
                        dve.wait_ge(half_added.sem, half_added.at(j + 1))
                        nc.vector.scalar_tensor_tensor(
                            out=x[:, j, :], in0=y_buf[:, 1, :], scalar=weight[:, 1, bass.ds(j, 1)], in1=x[:, j, :],
                            op0=ALU.mult, op1=ALU.add).then_inc(added.up(times), 1)
                        dve.wait_ge(added.sem, added.at(j + 1))
                        norm_stats(dve, j, x[:, j, :], stats_in, norm_in, times)

                    def enter_apply(j, times):
                        dve.wait_ge(xT_made.sem, xT_made.at(j))
                        norm_apply(dve, j, x[:, j, :], xn, stats_in, norm_in, times)

                    def spread_k(j, times):
                        dve.wait_ge(k_out.sem, k_out.at(j + 1))
                        dve.wait_ge(scored.sem, scored.at(2 * j))
                        for h in range(10):
                            last = nc.vector.tensor_scalar(k_head[:, :, :, h, :], kT.rearrange("p g (b s) -> p g b s", b=2),
                                                           col("mask3", h), None, ALU.mult)
                        last.then_inc(masked.up(times), 1)

                    def stage_v(j, times):
                        dve.wait_ge(v_projected.sem, v_projected.at(j + 1))
                        dve.wait_ge(v_placed.sem, v_placed.at(j))
                        nc.vector.tensor_copy(v, ps[:, MISC, 0:NV]).then_inc(v_staged.up(times), 1)

                    def place_v(j, times):
                        dve.wait_ge(v_staged.sem, v_staged.at(j + 1))
                        dve.wait_ge(attended.sem, attended.at(2 * j))
                        for b in range(2):
                            for a in range(2):
                                last = nc.vector.tensor_copy(v_pair[a * L:(a + 1) * L, :, b, a, 0:C3],
                                                             v[b * L:(b + 1) * L].rearrange("p (g c) -> p g c", g=G3))
                        last.then_inc(v_placed.up(times), 1)

                    def shift(i, g, times):
                        N = 2 * i + g
                        scores = ps[:, SCORES + 2 * g:SCORES + 2 * g + 2, :].rearrange("p a (h s) -> p (a h) s", s=L)
                        dve.wait_ge(scored.sem, scored.at(N + 1))
                        nc.vector.tensor_reduce(mx[:, g], scores, AX.X, ALU.max).then_inc(max_found.up(times), 1)
                        dve.wait_ge(max_found.sem, max_found.at(N + 1))
                        dve.wait_ge(probs_by_bank[1].sem, probs_by_bank[1].at(N - 1))
                        nc.vector.tensor_tensor(p[:, g], scores, mx[:, g].unsqueeze(2).to_broadcast([P, HG, L]), ALU.subtract
                                                ).then_inc(shifted.up(times), 1)

                    def take_turned(i, g, times):
                        N = 2 * i + g
                        dve.wait_ge(probs_by_bank[0].sem, probs_by_bank[0].at(N + 1))
                        dve.wait_ge(attended.sem, attended.at(N - 1))
                        nc.vector.tensor_copy(pT[:, g, 0:4, :], ps[:, TURNED, :].rearrange("p (j n) -> p j n", n=P)
                                              ).then_inc(pT_out_dve.up(times), 1)

                    def normalise(i, g, times):
                        N = 2 * i + g
                        dve.wait_ge(attended.sem, attended.at(N + 1))
                        toks = [slice(b * L, (b + 1) * L) for b in range(2)]
                        got = [ps[tok, PV, 0:8 * W].rearrange("p (j b h c) -> p j b h c", j=8, b=2, h=2) for tok in toks]
                        for b, tok in enumerate(toks):
                            last = nc.vector.reciprocal(inv[tok, g].rearrange("p (j h) -> p j h", j=8), got[b][:, :, b, :, C3])
                        last.then_inc(inv_made.up(times), 1)
                        dve.wait_ge(inv_made.sem, inv_made.at(N + 1))
                        dve.wait_ge(o_turned.sem, o_turned.at(i))
                        for b, tok in enumerate(toks):
                            last = nc.vector.tensor_tensor(
                                o[tok, g].rearrange("p (j h) c -> p j h c", j=8), got[b][:, :, b, :, 0:C3],
                                inv[tok, g].rearrange("p (j h) -> p j h", j=8).unsqueeze(3)
                                .to_broadcast([L, 8, 2, C3]), ALU.mult)
                        last.then_inc(attn_ready.up(times), 1)

                    def leave(i, times):
                        dve.wait_ge(out_made.sem, out_made.at(i + 1))
                        nc.vector.tensor_tensor(tmp, ps[:, MISC, 0:D], row("bfc"), ALU.add).then_inc(gate_step.up(times), 1)
                        dve.wait_ge(gate_step.sem, gate_step.at(i + 1))
                        nc.vector.scalar_tensor_tensor(out=x[:, i, :], in0=tmp, scalar=gain[:, layer:layer + 1],
                                                       in1=x[:, i, :], op0=ALU.mult, op1=ALU.add
                                                       ).then_inc(proj_exp.up(times), 1)
                        dve.wait_ge(proj_exp.sem, proj_exp.at(i + 1))
                        norm_stats(dve, i, x[:, i, :], stats_out, norm_out, times)

                    def leave_apply(i, times):
                        dve.wait_ge(saved.sem, saved.at(i))
                        dve.wait_ge(turned.sem, turned.at(i))
                        norm_apply(dve, i, x[:, i, :], xo, stats_out, norm_out, times)

                    def take_logits(i, times):
                        dve.wait_ge(logits_made.sem, logits_made.at(i + 1))
                        nc.vector.tensor_copy(logits[:, i, :], ps[:, MISC, 0:E]).then_inc(tile_done.up(times), 1)

                    nc.vector.memset(v_pair, 0.0).then_inc(ready.up(), 1)
                    dve.wait_ge(ready.sem, ready.at(1))
                    for a in range(2):
                        last = nc.vector.memset(v_pair[a * L:(a + 1) * L, :, :, a, C3:C3 + 1], 1.0)
                    last.then_inc(ready.up(), 1)
                    enter(0, 1)
                    enter_apply(0, 1)
                    spread_k(0, 1)
                    stage_v(0, 1)
                    enter(1, 1)
                    enter_apply(1, 1)
                    shift(0, 0, 1)

                    dve.wait_ge(ready.sem, ready.at(2))

                    def body(i, times, tail, qkv, norm):
                        place_v(i, times)
                        shift(i, 1, times)
                        if qkv:
                            spread_k(i + 1, times)
                        take_turned(i, 0, times)
                        if qkv:
                            stage_v(i + 1, times)
                        normalise(i, 0, times)
                        if qkv:
                            shift(i + 1, 0, times)
                        take_turned(i, 1, times)
                        if tail:
                            leave(i - 1, times)
                            leave_apply(i - 1, times)
                        if norm:
                            enter(i + 2, times)
                        normalise(i, 1, times)
                        if norm:
                            enter_apply(i + 2, times)
                        if tail:
                            take_logits(i - 1, times)

                    over_tiles(dve, body)
                    leave(T - 1, 1)
                    leave_apply(T - 1, 1)
                    take_logits(T - 1, 1)
            end_stage()

        s_at = E * (KC * 2 * HIDDEN[3] + len(chunks(HIDDEN[3])) * D)
        shared_up = ffn_w[:, s_at:s_at + KC * 2 * SHARED].rearrange("p (k m) -> p k m", k=KC)
        s_at += KC * 2 * SHARED
        n_sc = len(chunks(SHARED))
        shared_down = ffn_w[:, s_at:s_at + n_sc * D].rearrange("p (c n) -> p c n", c=n_sc)

        def route(layer):
            used[0] = 0
            top = carve(T, E)
            index8 = carve(T, E).bitcast(U32)
            index = carve(T, TOP)
            onehot = carve(TOP, T, E)
            chosen = carve(T, E)
            total = carve(E, T)
            scan_mask = carve(E, T)
            running = carve(E, T)
            many = carve(E, T)
            tiles_of = carve(E)
            tiles_to = carve(E)
            base = carve(E)
            grid = carve(T, E)
            picked = carve(TOP, T, E)
            slot_f = carve(TOP, T)
            passed = carve(SLOT_TILES, E)
            expert_f = carve(SLOT_TILES)
            gap, e_gap, w_sum = carve(T), carve(T), carve(T)
            rmax, prob = carve(T), carve(T, E)
            source = prob if layer == 3 else logits
            n = [0]

            with nc.Block() as block:
                @block.tensor
                def _(pe):
                    pe.wait_ge(h_ready.sem, h_ready.at(1))
                    nc.tensor.matmul(ps[:, 0, 0:P], before[:], chosen.rearrange("p t e -> p (t e)"), start=True, stop=True)
                    nc.tensor.matmul(ps[:, 1, 0:P], ones[:], chosen.rearrange("p t e -> p (t e)"), start=True, stop=True
                                     ).then_inc(y_made.up(), 1)

                @block.scalar
                def _(act):
                    if layer == 3:
                        act.wait_ge(silu_ready.sem, silu_ready.at(1))
                        nc.scalar.activation(prob, prob, ACT.Exp).then_inc(xT_ready.up(), 1)
                    else:
                        act.wait_ge(silu_ready.sem, silu_ready.at(1))
                        nc.scalar.activation(e_gap, gap, ACT.Exp).then_inc(xT_ready.up(), 1)

                @block.vector
                def _(dve):
                    def then(ins):
                        n[0] += 1
                        ins.then_inc(step.up(), 1)
                        dve.wait_ge(step.sem, step.at(n[0]))

                    if layer == 3:
                        then(nc.vector.tensor_reduce(rmax, logits[:], AX.X, ALU.max))
                        nc.vector.tensor_tensor(prob, logits[:], rmax.unsqueeze(2).to_broadcast([P, T, E]), ALU.subtract
                                                ).then_inc(silu_ready.up(), 1)
                        dve.wait_ge(xT_ready.sem, xT_ready.at(1))
                        then(nc.vector.tensor_reduce(w_sum, prob, AX.X, ALU.add))
                        then(nc.vector.reciprocal(w_sum, w_sum))
                        then(nc.vector.tensor_tensor(prob, prob, w_sum.unsqueeze(2).to_broadcast([P, T, E]), ALU.mult))
                    for t in range(T):
                        last = nc.vector.max(top[:, t, :], source[:, t, :])
                    then(last)
                    for t in range(T):
                        last = nc.vector.max_index(index8[:, t, :], top[:, t, :], source[:, t, :])
                    then(last)
                    if layer != 3:
                        nc.vector.tensor_tensor(gap, top[:, :, 1], top[:, :, 0], ALU.subtract).then_inc(silu_ready.up(), 1)
                    then(nc.vector.tensor_copy(index, index8[:, :, 0:TOP]))
                    for a in range(TOP):
                        last = nc.vector.tensor_tensor(
                            onehot[:, a], row("iota8").unsqueeze(1).to_broadcast([P, T, E]),
                            index[:, :, a:a + 1].to_broadcast([P, T, E]), ALU.is_equal)
                    then(last)
                    nc.vector.tensor_tensor(chosen, onehot[:, 0], onehot[:, 1], ALU.add).then_inc(h_ready.up(), 1)
                    nc.vector.memset(scan_mask, 1.0)
                    dve.wait_ge(y_made.sem, y_made.at(1))
                    then(nc.vector.tensor_copy(total, ps[:, 1, 0:P].rearrange("p (t e) -> p e t", e=E)))
                    then(nc.vector.memset(scan_mask[:, :, 0:1], 0.0))
                    then(nc.vector.tensor_tensor_scan(running.rearrange("p e t -> p (e t)"),
                                                      scan_mask.rearrange("p e t -> p (e t)"),
                                                      total.rearrange("p e t -> p (e t)"), 0.0, ALU.mult, ALU.add))
                    then(nc.vector.tensor_tensor(many, running[:, :, T - 1:T].to_broadcast([P, E, T]),
                                                 row("iota_k").unsqueeze(1).to_broadcast([P, E, T]), ALU.is_gt))
                    then(nc.vector.tensor_reduce(tiles_of, many, AX.X, ALU.add))
                    then(nc.vector.tensor_tensor_scan(tiles_to, ones[:, 0:E], tiles_of, 0.0, ALU.mult, ALU.add))
                    then(nc.vector.tensor_tensor(base, tiles_to, tiles_of, ALU.subtract))
                    then(nc.vector.tensor_scalar(base, base, float(P), None, ALU.mult))
                    then(nc.vector.tensor_tensor(running, running, total, ALU.subtract))
                    then(nc.vector.tensor_tensor(running, running, base.unsqueeze(2).to_broadcast([P, E, T]), ALU.add))
                    then(nc.vector.tensor_tensor(grid, ps[:, 0, 0:P].rearrange("p (t e) -> p t e", e=E),
                                                 running.rearrange("p e t -> p t e"), ALU.add))
                    for a in range(TOP):
                        last = nc.vector.tensor_tensor(picked[:, a], onehot[:, a], grid, ALU.mult)
                    then(last)
                    then(nc.vector.tensor_reduce(slot_f, picked, AX.X, ALU.add))
                    then(nc.vector.tensor_copy(slots[:], slot_f))
                    then(nc.vector.tensor_tensor(passed, row("iota_j").unsqueeze(2).to_broadcast([P, SLOT_TILES, E]),
                                                 tiles_to.unsqueeze(1).to_broadcast([P, SLOT_TILES, E]), ALU.is_ge))
                    then(nc.vector.tensor_reduce(expert_f, passed, AX.X, ALU.add))
                    then(nc.vector.tensor_scalar(expert_f, expert_f, float(E - 1), None, ALU.min))
                    then(nc.vector.tensor_copy(tile_expert[:], expert_f[0:1, :]))
                    g = gain[:, 4 + layer:5 + layer]
                    if layer == 3:
                        then(nc.vector.tensor_scalar(weight[:].rearrange("p a t -> p t a"), top[:, :, 0:TOP], g, None, ALU.mult))
                    else:
                        dve.wait_ge(xT_ready.sem, xT_ready.at(1))
                        then(nc.vector.tensor_scalar(w_sum, e_gap, 1.0, None, ALU.add))
                        then(nc.vector.reciprocal(w_sum, w_sum))
                        then(nc.vector.tensor_scalar(weight[:, 0, :], w_sum, g, None, ALU.mult))
                        then(nc.vector.tensor_tensor(weight[:, 1, :], weight[:, 0, :], e_gap, ALU.mult))
            end_stage()

        def scatter(pool):
            for t in range(T):
                for a in range(TOP):
                    nc.gpsimd.indirect_dma_start(
                        slot_x, bass.IndirectOffsetOnAxis(ap=slots[:, a, t:t + 1], axis=0), xn2[:, t, :], None
                    ).then_inc(scattered.up(), 16)

        def feed_forward(layer, shared=False):
            used[0] = 0
            m = SHARED if shared else HIDDEN[layer]
            cs = chunks(m)
            NT = T if shared else SLOT_TILES
            wide = 2 * m > 512
            xs = [carve(D) for _ in range(2)]
            xT = [carve(KC, P) for _ in range(2)]
            silu = [carve(m) for _ in range(2)]
            hT = [carve(len(cs), P) for _ in range(2)]
            y = [carve(D) for _ in range(2)]
            PAIRS = (NT - 3) // 2
            X, TURNED, Y = 0, 5, 6

            def gate_bank(u):
                return 1 + 2 * u

            def up_part(u):
                return ps[:, 2 + 2 * u, 0:m] if wide else ps[:, 1 + 2 * u, m:2 * m]

            def over_steps(eng, step_of):
                step_of(0, 0, range(NT))
                with eng.Fori(0, PAIRS) as i:
                    for c in (1, 2):
                        step_of(i, c, None)
                for c in range(2 * PAIRS + 1, NT):
                    step_of(0, c, range(NT))

            def there(c, tiles):
                return tiles is None or c in tiles

            with nc.Block() as block:
                @block.sync
                def _(sp):
                    if shared:
                        return
                    sp.wait_ge(scattered.sem, scattered.at(0 if layer == 3 else TOP * T))

                    def load(i, c):
                        if not (isinstance(i, int) and c < 2):
                            sp.wait_ge(xT_made.sem, xT_made.at(2 * i + c - 1))
                        sp.dma_start(xs[c % 2], slot_x[bass.ds((2 * i + c) * P, P), :]).then_inc(slot_in[c % 2].sem, 16)

                    def store(i, c):
                        sp.wait_ge(y_ready.sem, y_ready.at(2 * i + c + 1))
                        sp.dma_start(slot_y[bass.ds((2 * i + c) * P, P), :], y[c % 2]).then_inc(slot_out[c % 2].sem, 16)

                    for c in range(4):
                        load(0, c)

                    def step_of(i, c, tiles):
                        if there(c + 4, tiles):
                            load(i, c + 4)
                        store(i, c)

                    step_of(0, 0, range(NT))
                    with sp.Fori(0, (NT - 5) // 2) as i:
                        for c in (1, 2):
                            step_of(i, c, None)
                    for c in range(2 * ((NT - 5) // 2) + 1, NT):
                        step_of(0, c, range(NT))
                    for u in range(2):
                        n = (NT + 1 - u) // 2
                        slot_in[u].up(n)
                        slot_out[u].up(n)
                        sp.wait_ge(slot_out[u].sem, slot_out[u].at(n))

                @block.gpsimd
                def _(pool):
                    if shared or layer != 3:
                        scatter(pool)

                @block.tensor
                def _(pe):
                    pe.wait_ge(ffn_w_in.sem, ffn_w_in.at(0))

                    def expert_of(i, c):
                        return pe.value_load(tile_expert[0:1, bass.ds(2 * i + c, 1)], min_val=0, max_val=E - 1)

                    def turn_rows(i, c):
                        j, u = 2 * i + c, c % 2
                        if shared:
                            pe.wait_ge(copied.sem, copied.at(j + 1))
                        else:
                            pe.wait_ge(slot_in[u].sem, slot_in[u].at(i + c // 2 + 1))
                        pe.wait_ge(xT_ready.sem, xT_ready.at(j))
                        turn(pe, xs[u], X).then_inc(xT_made.sem, 1)

                    def up_rows(i, c):
                        j, u = 2 * i + c, c % 2
                        e = None if shared else expert_of(i, c)
                        pe.wait_ge(xT_ready.sem, xT_ready.at(j + 1))
                        pe.wait_ge(h_ready.sem, h_ready.at(j - 1))
                        for o, n, bank in (((0, m, gate_bank(u)), (m, m, gate_bank(u) + 1)) if wide
                                           else ((0, 2 * m, gate_bank(u)),)):
                            for k in range(KC):
                                w = shared_up[:, k, o:o + n] if shared else up_view(layer)[:, e, k, o:o + n]
                                mm = nc.tensor.matmul(ps[:, bank, 0:n], xT[u][:, k, :], w,
                                                      start=(k == 0), stop=(k == KC - 1))
                        mm.then_inc(up_made.sem, 1)

                    def turn_hidden(i, c):
                        j, u = 2 * i + c, c % 2
                        pe.wait_ge(h_ready.sem, h_ready.at(j + 1))
                        pe.wait_ge(hT_ready.sem, hT_ready.at(j))
                        for k, n in cs:
                            mm = nc.tensor.transpose(ps[0:n, TURNED, k * P:(k + 1) * P], silu[u][:, k * P:k * P + n], ident[:])
                        mm.then_inc(hT_made.sem, 1)

                    def down_rows(i, c):
                        j, u = 2 * i + c, c % 2
                        e = None if shared else expert_of(i, c)
                        pe.wait_ge(hT_ready.sem, hT_ready.at(j + 1))
                        pe.wait_ge(y_ready.sem, y_ready.at(j - 1))
                        for k, n in cs:
                            w = shared_down[0:n, k, :] if shared else down_view(layer)[0:n, e, k, :]
                            mm = nc.tensor.matmul(ps[:, Y + u, 0:D], hT[u][0:n, k, :], w,
                                                  start=(k == 0), stop=(k == len(cs) - 1))
                        mm.then_inc(y_made.sem, 1)

                    def step_of(i, c, tiles):
                        if there(c + 2, tiles):
                            turn_rows(i, c + 2)
                        if there(c + 1, tiles):
                            up_rows(i, c + 1)
                        turn_hidden(i, c)
                        if there(c - 1, tiles):
                            down_rows(i, c - 1)

                    turn_rows(0, 0)
                    turn_rows(0, 1)
                    up_rows(0, 0)
                    over_steps(pe, step_of)
                    down_rows(0, NT - 1)
                    for s in (xT_made, up_made, hT_made, y_made):
                        s.up(NT)

                @block.scalar
                def _(act):
                    def silu_of(i, c):
                        j, u = 2 * i + c, c % 2
                        act.wait_ge(up_made.sem, up_made.at(j + 1))
                        act.wait_ge(hT_made.sem, hT_made.at(j - 1))
                        nc.scalar.activation(silu[u], ps[:, gate_bank(u), 0:m], ACT.Silu).then_inc(silu_ready.sem, 1)

                    def take_turned(i, c):
                        j, u = 2 * i + c, c % 2
                        act.wait_ge(hT_made.sem, hT_made.at(j + 1))
                        act.wait_ge(y_made.sem, y_made.at(j - 1))
                        whole = m // P
                        last = nc.scalar.copy(hT[u][:, 0:whole, :].rearrange("p k t -> p (k t)"), ps[:, TURNED, 0:whole * P])
                        if m % P:
                            n = m % P
                            last = nc.scalar.copy(hT[u][0:n, whole, :], ps[0:n, TURNED, whole * P:(whole + 1) * P])
                        last.then_inc(hT_ready.sem, 1)

                    def take_rows(i, c):
                        j, u = 2 * i + c, c % 2
                        act.wait_ge(y_made.sem, y_made.at(j + 1))
                        act.wait_ge(slot_out[u].sem, slot_out[u].at(i + c // 2))
                        nc.scalar.copy(y[u], ps[:, Y + u, 0:D]).then_inc(y_ready.sem, 1)

                    def step_of(i, c, tiles):
                        if there(c + 1, tiles):
                            silu_of(i, c + 1)
                        take_turned(i, c)
                        if there(c - 1, tiles) and not shared:
                            take_rows(i, c - 1)

                    nc.scalar.activation(table_call[:], half[:], ACT.Silu)
                    silu_of(0, 0)
                    over_steps(act, step_of)
                    if not shared:
                        take_rows(0, NT - 1)
                        y_ready.up(NT)
                    for s in (silu_ready, hT_ready):
                        s.up(NT)

                @block.vector
                def _(dve):
                    def fetch(i, c):
                        j, u = 2 * i + c, c % 2
                        dve.wait_ge(xT_made.sem, xT_made.at(j - 1))
                        nc.vector.tensor_copy(xs[u], xn2[:, j, :]).then_inc(copied.sem, 1)

                    def take_turned(i, c):
                        j, u = 2 * i + c, c % 2
                        dve.wait_ge(xT_made.sem, xT_made.at(j + 1))
                        dve.wait_ge(up_made.sem, up_made.at(j - 1))
                        nc.vector.tensor_copy(xT[u].rearrange("p k t -> p (k t)"), ps[:, X, 0:D]).then_inc(xT_ready.sem, 1)

                    def multiply(i, c):
                        j, u = 2 * i + c, c % 2
                        dve.wait_ge(silu_ready.sem, silu_ready.at(j + 1))
                        nc.vector.tensor_tensor(silu[u], silu[u], up_part(u), ALU.mult).then_inc(h_ready.sem, 1)

                    def add_to_x(i, c):
                        j, u = 2 * i + c, c % 2
                        dve.wait_ge(y_made.sem, y_made.at(j + 1))
                        nc.vector.scalar_tensor_tensor(out=x[:, j, :], in0=ps[:, Y + u, 0:D], scalar=gain[:, 4 + layer:5 + layer],
                                                       in1=x[:, j, :], op0=ALU.mult, op1=ALU.add).then_inc(y_ready.sem, 1)

                    def step_of(i, c, tiles):
                        if there(c + 2, tiles):
                            take_turned(i, c + 2)
                        if shared and there(c + 3, tiles):
                            fetch(i, c + 3)
                        if there(c + 1, tiles):
                            multiply(i, c + 1)
                        if shared and there(c - 1, tiles):
                            add_to_x(i, c - 1)

                    if shared:
                        fetch(0, 0)
                        fetch(0, 1)
                    take_turned(0, 0)
                    take_turned(0, 1)
                    if shared:
                        fetch(0, 2)
                    multiply(0, 0)
                    over_steps(dve, step_of)
                    if shared:
                        add_to_x(0, NT - 1)
                        y_ready.up(NT)
                        copied.up(NT)
                    for s in (xT_ready, h_ready):
                        s.up(NT)
            end_stage()

        def finish():
            used[0] = 0
            y_buf = [carve(TOP, D) for _ in range(T)]
            with nc.Block() as block:
                @block.gpsimd
                def _(pool):
                    for t in range(T):
                        u = t % LANES
                        if t >= LANES:
                            pool.wait_ge(y_in_lane[u].sem, y_in_lane[u].at(TOP * (t // LANES)))
                        for a in range(TOP):
                            nc.gpsimd.indirect_dma_start(
                                y_buf[t][:, a, :], None, slot_y,
                                bass.IndirectOffsetOnAxis(ap=slots[:, a, t:t + 1], axis=0)).then_inc(y_in_lane[u].up(), 16)

                @block.vector
                def _(dve):
                    for t in range(T):
                        dve.wait_ge(y_in_lane[t % LANES].sem, y_in_lane[t % LANES].at(TOP * (t // LANES) + TOP))
                        for a, signal in ((0, half_added), (1, added)):
                            nc.vector.scalar_tensor_tensor(
                                out=x[:, t, :], in0=y_buf[t][:, a, :], scalar=weight[:, a, t:t + 1], in1=x[:, t, :],
                                op0=ALU.mult, op1=ALU.add).then_inc(signal.up(), 1)
                            if a == 0:
                                dve.wait_ge(half_added.sem, half_added.at(t + 1))

                @block.sync
                def _(sp):
                    for t in range(T):
                        sp.wait_ge(added.sem, added.at(t + 1))
                        sp.dma_start(out[t * P:(t + 1) * P, :], x[:, t, :]).then_inc(out_done.up(), 16)
                    sp.wait_ge(out_done.sem, out_done.at(T))
            end_stage()

        for layer, attention in enumerate((attention0, attention1, attention2, attention3)[:LAYERS]):
            attention()
            route(layer)
            if layer == 3:
                feed_forward(layer, shared=True)
            feed_forward(layer)
        finish()


def host_arrays(v):
    f = np.float32
    a = {}
    a["ident"] = np.eye(P, dtype=f)
    a["before"] = np.triu(np.ones((P, P), f), 1)
    a["x"] = v["x"].reshape(T, P, D).transpose(1, 0, 2)
    a["ctx"] = v["ctx_2048"].reshape(T, P, D)
    a["ctxT"] = v["ctx_2048"].reshape(T, P, KC, P).transpose(0, 3, 2, 1)
    i = np.arange(P)
    a["mask0"] = np.tile((i[:, None] // HD0 == i[None, :] // HD0).astype(f), (1, 2))
    inv = (1.0 / 10000.0 ** (np.arange(0, C1, 2, dtype=f) / C1)).astype(f)
    pos = (np.arange(D, dtype=f)[:, None] * inv[None, :]).astype(f)
    pos = np.concatenate([pos, pos], axis=-1)
    sign = np.where(np.arange(C1) < C1 // 2, -1.0, 1.0).astype(f)
    cos = np.tile(np.repeat(np.cos(pos).T, H1, 0), (2, 1)).astype(f)
    sin = np.tile(np.repeat((np.sin(pos) * sign).T, H1, 0), (2, 1)).astype(f)
    scale = f(1.0 / np.sqrt(C1))

    def on_all(r):
        return np.broadcast_to(np.asarray(r, f).reshape(1, -1), (P, np.asarray(r).size))

    def vec2(b):
        return np.asarray(b).reshape(KC, P).T

    plain = np.arange(64).reshape(H1, C1).T.reshape(-1)
    turn8 = np.arange(64).reshape(H1, 2, C1 // 2)[:, ::-1].reshape(H1, C1).T.reshape(-1)
    two = lambda b: np.concatenate([b, b]).reshape(P, 1)
    c = {"g": on_all(np.concatenate([v["g_xattn"], v["g_ffn"]])), "bg": vec2(v["L0_xattn_bg"]),
         "bq": np.concatenate([two(v["L1_xattn_bq"][plain]), two(v["L1_xattn_bq"][turn8])], 1),
         "bk": np.concatenate([two(v["L1_xattn_bk"][plain]), two(v["L1_xattn_bk"][turn8])], 1),
         "bo": two(v["L1_xattn_bo"]),
         "mask3": (i[:, None] // C3 == np.arange(P // C3)[None, :]).astype(f),
         "decay": on_all(v["L2_xattn_decay"]), "b_in": vec2(v["L2_xattn_b_in"]),
         "batch_of": (i[:, None] // L == np.arange(2)[None, :]).astype(f)}
    a["cols"] = np.concatenate([c[n] for n, _ in COLS], 1)
    r = {"bv": on_all(np.concatenate([v["L1_xattn_bv"]] * 2)), "bfc": on_all(v["L3_xattn_bfc"]),
         "gamma": on_all(v["L2_xattn_gamma"]), "beta": on_all(v["L2_xattn_beta"]), "b_out": on_all(v["L2_xattn_b_out"]),
         "iota8": on_all(np.arange(E)), "iota_k": on_all(np.arange(T) * P), "iota_j": on_all(np.arange(SLOT_TILES)),
         "cos_q": cos * scale, "sin_q": sin * scale, "cos_k": cos, "sin_k": sin}
    a["rows"] = np.concatenate([r[n] for n, _ in ROWS], 1)
    router = [v["L0_ffn_w_gate"], v["L1_ffn_gate_w"], v["L2_ffn_Wg"].T, v["L3_ffn_W_g"]]
    a["router_w"] = np.stack(router).reshape(4, KC, P, E).transpose(2, 0, 1, 3)
    a["wq0"], a["wg0"], a["wkv0"], a["wo0"] = (v[f"L0_xattn_{n}"].T for n in ("Wq", "Wg", "Wkv", "Wo"))
    a["up0"] = np.concatenate([v["L0_ffn_wi_0"], v["L0_ffn_wi_1"]], 2)
    a["down0"] = v["L0_ffn_wo"]
    a["up1"] = np.concatenate([v["L1_ffn_w0"], v["L1_ffn_w1"]], 2)
    a["down1"] = v["L1_ffn_wo"]
    a["up2"] = np.concatenate([v["L2_ffn_W1"], v["L2_ffn_W2"]], 1).transpose(0, 2, 1)
    a["down2"] = v["L2_ffn_W3"].transpose(0, 2, 1)
    a["up3"] = np.concatenate([v["L3_ffn_Wg"], v["L3_ffn_Wu"]], 2)
    a["down3"] = v["L3_ffn_Wd"]
    a["shared_up"] = np.concatenate([v["L3_ffn_Ws_gate"], v["L3_ffn_Ws_up"]], 1)
    a["shared_down"] = v["L3_ffn_Ws_down"]

    def both(w):
        z = np.zeros((P, P), f)
        z[0:64, 0:64] = z[64:P, 64:P] = w.T
        return z

    a["wq1"], a["wq1_turned"] = both(v["L1_xattn_Wq"][plain]), both(v["L1_xattn_Wq"][turn8])
    a["wk1"], a["wk1_turned"] = both(v["L1_xattn_Wk"][plain]), both(v["L1_xattn_Wk"][turn8])
    a["wv1"] = both(v["L1_xattn_Wv"])
    wo1 = np.zeros((4, 32, 2, 2, 2, 64), f)
    per_head = v["L1_xattn_Wo"].T.reshape(2, 4, C1, 64).transpose(1, 2, 0, 3)
    wo1[:, 0:C1, :, 0, 0] = wo1[:, 0:C1, :, 1, 1] = per_head
    wo1 = wo1.reshape(P, 2, 2, P)
    a["wo1"] = wo1
    a["w_in2"], a["w_out2"] = v["L2_xattn_W_in"].T, v["L2_xattn_W_out"].T
    a["pick"] = (np.arange(L)[None, :] == L - 1 - i[:, None] % L).astype(f)
    a["wq3"], a["wfc3"], a["wv3"] = (v[f"L3_xattn_{n}"].T for n in ("Wq", "Wfc", "Wv"))
    a["wk3"] = np.repeat(v["L3_xattn_Wk"].reshape(G3, C3, D), H3 // G3, 0).reshape(H3 * C3, D).T
    return {f"in_{k}": np.ascontiguousarray(b) for k, b in a.items()}


def kernel(**inputs):
    import concourse.bacc as bacc
    from concourse.bass_utils import run_bass_kernel_spmd

    nc = bacc.Bacc("TRN2", target_bir_lowering=False, num_devices=1)
    arrays = host_arrays({k: np.asarray(a) for k, a in inputs.items()})
    d = {k[3:]: nc.dram_tensor(k, a.shape, mybir.dt.from_np(a.dtype), kind="ExternalInput").ap()
         for k, a in arrays.items()}
    out = nc.dram_tensor("out", (B * L, D), F32, kind="ExternalOutput").ap()
    build(nc, d, out)
    r = run_bass_kernel_spmd(nc, [arrays], core_ids=[0])
    return r.results[0]["out"].reshape(B, L, D)
```
